# Optimizing a Trainium2 kernel written in Bass

```python
import numpy as np
import jax
import jax.numpy as jnp

def _softmax(x, axis=-1):
    return jax.nn.softmax(x, axis=axis)

def _gelu(x):
    return jax.nn.gelu(x, approximate=True)

def _silu(x):
    return jax.nn.silu(x)

def _sigmoid(x):
    return jax.nn.sigmoid(x)

def _layernorm(x, axis=-1, eps=1e-05):
    m = jnp.mean(x, axis=axis, keepdims=True)
    v = jnp.var(x, axis=axis, keepdims=True)
    return (x - m) / jnp.sqrt(v + eps)

def _scatter_add(tgt, idx, src, axis=0):
    return tgt.at[idx].add(src)

def _segment_sum(src, seg, n):
    return jax.ops.segment_sum(src, seg, n)
kernel_name = 'mk_hybrid_d2_jaxref_r8_2e1caf'

def setup_inputs(seed: int=0):
    np.random.seed(seed)
    _w = jnp.asarray

    def _L0_attn_a_setup():
        import jax, jax.numpy as jnp
        import numpy as np
        SLOPE = 25.0
        THR = 1.0
        BETA = 0.95
        SPIKE_STEPS = 4
        NUM_HEADS = 16

        @jax.custom_vjp
        def spike(u):
            return (u > 0).astype(u.dtype)

        def _spike_fwd(u):
            return (spike(u), u)

        def _spike_bwd(u, g):
            return (g / (SLOPE * jnp.abs(u) + 1.0) ** 2,)
        spike.defvjp(_spike_fwd, _spike_bwd)

        def lif_mean(cur):

            def step(mem, _):
                reset = jax.lax.stop_gradient(spike(mem - THR))
                mem = BETA * mem + cur - reset * THR
                return (mem, spike(mem - THR))
            _, spk = jax.lax.scan(step, jnp.zeros_like(cur), None, length=SPIKE_STEPS)
            return spk.mean(axis=0)
        B, S, D = (2, 256, 128)
        key = jax.random.key(seed)
        ks = jax.random.split(key, 9)
        std = 1.0 / np.sqrt(D)
        mkw = lambda k: jax.random.uniform(k, (D, D), jnp.float32, -std, std)
        mkb = lambda k: jax.random.uniform(k, (D,), jnp.float32, -std, std)
        return {'x': jax.random.normal(ks[0], (B, S, D), jnp.float32), 'q_w': mkw(ks[1]), 'q_b': mkb(ks[2]), 'k_w': mkw(ks[3]), 'k_b': mkb(ks[4]), 'v_w': mkw(ks[5]), 'v_b': mkb(ks[6]), 'o_w': mkw(ks[7]), 'o_b': mkb(ks[8])}
    _L0_attn_a_in = _L0_attn_a_setup()

    def _L0_attn_b_setup():
        import jax, jax.numpy as jnp
        import numpy as np
        DIM = 128
        HEADS = 16
        DIM_HEAD = 64
        INNER = HEADS * DIM_HEAD
        SCALE = DIM_HEAD ** (-0.5)

        def _layer_norm(x, gamma):
            mu = jnp.mean(x, axis=-1, keepdims=True)
            var = jnp.var(x, axis=-1, keepdims=True)
            return (x - mu) * jax.lax.rsqrt(var + 1e-05) * gamma
        key = jax.random.key(seed)
        ks = jax.random.split(key, 6)
        b, n = (4, 256)
        x = jax.random.normal(ks[0], (b, n, DIM), dtype=jnp.float32)
        gamma = jnp.ones((DIM,), dtype=jnp.float32)
        w_q = jax.random.normal(ks[1], (DIM, INNER), dtype=jnp.float32) * DIM ** (-0.5)
        w_kv = jax.random.normal(ks[2], (DIM, 2 * INNER), dtype=jnp.float32) * DIM ** (-0.5)
        w_out = jax.random.normal(ks[3], (INNER, DIM), dtype=jnp.float32) * INNER ** (-0.5)
        null_kv = jax.random.normal(ks[4], (2, HEADS, 1, DIM_HEAD), dtype=jnp.float32)
        return {'x': x, 'gamma': gamma, 'w_q': w_q, 'w_kv': w_kv, 'w_out': w_out, 'null_kv': null_kv}
    _L0_attn_b_in = _L0_attn_b_setup()

    def _L0_ffn_setup():
        import jax, jax.numpy as jnp
        import numpy as np
        TOP_K = 2
        key = jax.random.key(seed)
        k1, k2, k3, k4, k5 = jax.random.split(key, 5)
        B, S, D, F, E = (2, 128, 128, 256, 8)
        return {'x': jax.random.normal(k1, (B, S, D), dtype=jnp.float32), 'router_kernel_DE': jax.random.normal(k2, (D, E), dtype=jnp.float32) * 0.02, 'kernel_gating_EDF': jax.random.normal(k3, (E, D, F), dtype=jnp.float32) * 0.02, 'kernel_up_EDF': jax.random.normal(k4, (E, D, F), dtype=jnp.float32) * 0.02, 'kernel_down_EFD': jax.random.normal(k5, (E, F, D), dtype=jnp.float32) * 0.02}
    _L0_ffn_in = _L0_ffn_setup()

    def _L1_attn_a_setup():
        import jax, jax.numpy as jnp
        import numpy as np
        H = 16
        ROPE_BASE = 10000.0

        def _rotate_half(x):
            d = x.shape[-1]
            return jnp.concatenate((-x[..., d // 2:], x[..., :d // 2]), axis=-1)
        key = jax.random.key(seed)
        ks = jax.random.split(key, 9)
        B, S, E = (4, 256, 128)
        s = 0.02
        return {'x': jax.random.normal(ks[0], (B, S, E), dtype=jnp.float32), 'wq': jax.random.normal(ks[1], (E, E), dtype=jnp.float32) * s, 'bq': jax.random.normal(ks[2], (E,), dtype=jnp.float32) * s, 'wk': jax.random.normal(ks[3], (E, E), dtype=jnp.float32) * s, 'bk': jax.random.normal(ks[4], (E,), dtype=jnp.float32) * s, 'wv': jax.random.normal(ks[5], (E, E), dtype=jnp.float32) * s, 'bv': jax.random.normal(ks[6], (E,), dtype=jnp.float32) * s, 'wo': jax.random.normal(ks[7], (E, E), dtype=jnp.float32) * s, 'bo': jax.random.normal(ks[8], (E,), dtype=jnp.float32) * s}
    _L1_attn_a_in = _L1_attn_a_setup()

    def _L1_attn_b_setup():
        import jax, jax.numpy as jnp
        import numpy as np
        C = 128
        H = 16
        K = 2
        B, N = (4, 512)

        def _heads(t):
            shp = t.shape
            d = shp[-1] // H
            t = t.reshape(shp[:-1] + (H, d))
            return jnp.swapaxes(t, -2, -3)
        key = jax.random.key(seed)
        ks_ = jax.random.split(key, 12)
        s = 1.0 / np.sqrt(C)
        inp = {'x': jax.random.normal(ks_[0], (B, N, C), dtype=jnp.float32), 'Wq': jax.random.normal(ks_[1], (C, C), dtype=jnp.float32) * s, 'bq': jnp.zeros((C,), dtype=jnp.float32), 'Wk': jax.random.normal(ks_[2], (K, C, C), dtype=jnp.float32) * s, 'bk': jnp.zeros((K, C), dtype=jnp.float32), 'Wv': jax.random.normal(ks_[3], (K, C, C), dtype=jnp.float32) * s, 'bv': jnp.zeros((K, C), dtype=jnp.float32), 'Wo': jax.random.normal(ks_[4], (C, C), dtype=jnp.float32) * s, 'bo': jnp.zeros((C,), dtype=jnp.float32), 'ln_g': jnp.ones((C,), dtype=jnp.float32), 'ln_b': jnp.zeros((C,), dtype=jnp.float32)}
        return inp
    _L1_attn_b_in = _L1_attn_b_setup()

    def _L1_ffn_setup():
        import jax, jax.numpy as jnp
        import numpy as np
        from jax import lax
        DIM = 128
        INTER = 64
        N_EXPERTS = 16
        TOPK = 4
        ROUTE_SCALE = 2.5
        VOCAB = 4000

        def _silu_and_mul(gu):
            gate, up = jnp.split(gu, 2, axis=-1)
            return jax.nn.silu(gate) * up
        key = jax.random.key(seed)
        ks = jax.random.split(key, 8)
        x = jax.random.normal(ks[0], (2, 64, DIM), dtype=jnp.float32)
        input_ids = jax.random.randint(ks[1], (2, 64), 0, VOCAB)
        s = 0.02
        gate_w = jax.random.normal(ks[2], (N_EXPERTS, DIM), dtype=jnp.float32) * s
        gate_b = jax.random.normal(ks[3], (N_EXPERTS,), dtype=jnp.float32) * s
        w13 = jax.random.normal(ks[4], (N_EXPERTS, 2 * INTER, DIM), dtype=jnp.float32) * s
        w2 = jax.random.normal(ks[5], (N_EXPERTS, DIM, INTER), dtype=jnp.float32) * s
        w13_s = jax.random.normal(ks[6], (2 * INTER, DIM), dtype=jnp.float32) * s
        w2_s = jax.random.normal(ks[7], (DIM, INTER), dtype=jnp.float32) * s
        return {'x': x, 'input_ids': input_ids, 'gate_w': gate_w, 'gate_b': gate_b, 'w13': w13, 'w2': w2, 'w13_s': w13_s, 'w2_s': w2_s}
    _L1_ffn_in = _L1_ffn_setup()
    _d = {'L0_attn_a_x': _L0_attn_a_in['x'], 'L0_attn_a_q_w': _L0_attn_a_in['q_w'], 'L0_attn_a_q_b': _L0_attn_a_in['q_b'], 'L0_attn_a_k_w': _L0_attn_a_in['k_w'], 'L0_attn_a_k_b': _L0_attn_a_in['k_b'], 'L0_attn_a_v_w': _L0_attn_a_in['v_w'], 'L0_attn_a_v_b': _L0_attn_a_in['v_b'], 'L0_attn_a_o_w': _L0_attn_a_in['o_w'], 'L0_attn_a_o_b': _L0_attn_a_in['o_b'], 'L0_attn_b_gamma': _L0_attn_b_in['gamma'], 'L0_attn_b_w_q': _L0_attn_b_in['w_q'], 'L0_attn_b_w_kv': _L0_attn_b_in['w_kv'], 'L0_attn_b_w_out': _L0_attn_b_in['w_out'], 'L0_attn_b_null_kv': _L0_attn_b_in['null_kv'], 'L0_ffn_router_kernel_DE': _L0_ffn_in['router_kernel_DE'], 'L0_ffn_kernel_gating_EDF': _L0_ffn_in['kernel_gating_EDF'], 'L0_ffn_kernel_up_EDF': _L0_ffn_in['kernel_up_EDF'], 'L0_ffn_kernel_down_EFD': _L0_ffn_in['kernel_down_EFD'], 'L1_attn_a_wq': _L1_attn_a_in['wq'], 'L1_attn_a_bq': _L1_attn_a_in['bq'], 'L1_attn_a_wk': _L1_attn_a_in['wk'], 'L1_attn_a_bk': _L1_attn_a_in['bk'], 'L1_attn_a_wv': _L1_attn_a_in['wv'], 'L1_attn_a_bv': _L1_attn_a_in['bv'], 'L1_attn_a_wo': _L1_attn_a_in['wo'], 'L1_attn_a_bo': _L1_attn_a_in['bo'], 'L1_attn_b_Wq': _L1_attn_b_in['Wq'], 'L1_attn_b_bq': _L1_attn_b_in['bq'], 'L1_attn_b_Wk': _L1_attn_b_in['Wk'], 'L1_attn_b_bk': _L1_attn_b_in['bk'], 'L1_attn_b_Wv': _L1_attn_b_in['Wv'], 'L1_attn_b_bv': _L1_attn_b_in['bv'], 'L1_attn_b_Wo': _L1_attn_b_in['Wo'], 'L1_attn_b_bo': _L1_attn_b_in['bo'], 'L1_attn_b_ln_g': _L1_attn_b_in['ln_g'], 'L1_attn_b_ln_b': _L1_attn_b_in['ln_b'], 'L1_ffn_input_ids': _L1_ffn_in['input_ids'], 'L1_ffn_gate_w': _L1_ffn_in['gate_w'], 'L1_ffn_gate_b': _L1_ffn_in['gate_b'], 'L1_ffn_w13': _L1_ffn_in['w13'], 'L1_ffn_w2': _L1_ffn_in['w2'], 'L1_ffn_w13_s': _L1_ffn_in['w13_s'], 'L1_ffn_w2_s': _L1_ffn_in['w2_s']}
    _x0 = _d['L0_attn_a_x']
    _d['L0_attn_a_x'] = jax.random.normal(jax.random.fold_in(jax.random.key(seed), 1), (4, 1024, 128), dtype=_x0.dtype)
    del _x0
    return _d

def reference(L0_attn_a_x, L0_attn_a_q_w, L0_attn_a_q_b, L0_attn_a_k_w, L0_attn_a_k_b, L0_attn_a_v_w, L0_attn_a_v_b, L0_attn_a_o_w, L0_attn_a_o_b, L0_attn_b_gamma, L0_attn_b_w_q, L0_attn_b_w_kv, L0_attn_b_w_out, L0_attn_b_null_kv, L0_ffn_router_kernel_DE, L0_ffn_kernel_gating_EDF, L0_ffn_kernel_up_EDF, L0_ffn_kernel_down_EFD, L1_attn_a_wq, L1_attn_a_bq, L1_attn_a_wk, L1_attn_a_bk, L1_attn_a_wv, L1_attn_a_bv, L1_attn_a_wo, L1_attn_a_bo, L1_attn_b_Wq, L1_attn_b_bq, L1_attn_b_Wk, L1_attn_b_bk, L1_attn_b_Wv, L1_attn_b_bv, L1_attn_b_Wo, L1_attn_b_bo, L1_attn_b_ln_g, L1_attn_b_ln_b, L1_ffn_input_ids, L1_ffn_gate_w, L1_ffn_gate_b, L1_ffn_w13, L1_ffn_w2, L1_ffn_w13_s, L1_ffn_w2_s):

    def _L0_attn_a_ref(x, q_w, q_b, k_w, k_b, v_w, v_b, o_w, o_b):
        import jax, jax.numpy as jnp
        import numpy as np
        SLOPE = 25.0
        THR = 1.0
        BETA = 0.95
        SPIKE_STEPS = 4
        NUM_HEADS = 16

        @jax.custom_vjp
        def spike(u):
            return (u > 0).astype(u.dtype)

        def _spike_fwd(u):
            return (spike(u), u)

        def _spike_bwd(u, g):
            return (g / (SLOPE * jnp.abs(u) + 1.0) ** 2,)
        spike.defvjp(_spike_fwd, _spike_bwd)

        def lif_mean(cur):

            def step(mem, _):
                reset = jax.lax.stop_gradient(spike(mem - THR))
                mem = BETA * mem + cur - reset * THR
                return (mem, spike(mem - THR))
            _, spk = jax.lax.scan(step, jnp.zeros_like(cur), None, length=SPIKE_STEPS)
            return spk.mean(axis=0)
        B, S, D = x.shape
        H = NUM_HEADS
        Hd = D // H
        proj = lambda w, b: (x @ w + b).reshape(B, S, H, Hd).transpose(0, 2, 1, 3)
        q, k, v = (proj(q_w, q_b), proj(k_w, k_b), proj(v_w, v_b))
        q_agg, k_agg, v_agg = (lif_mean(q), lif_mean(k), lif_mean(v))
        scores = jnp.einsum('bhqd,bhkd->bhqk', q_agg, k_agg) / jnp.sqrt(jnp.float32(Hd))
        attn = jax.nn.softmax(scores, axis=-1)
        out = jnp.einsum('bhqk,bhkd->bhqd', attn, v_agg)
        out = out.transpose(0, 2, 1, 3).reshape(B, S, D)
        return out @ o_w + o_b

    def _L0_attn_b_ref(x, gamma, w_q, w_kv, w_out, null_kv):
        import jax, jax.numpy as jnp
        import numpy as np
        DIM = 128
        HEADS = 16
        DIM_HEAD = 64
        INNER = HEADS * DIM_HEAD
        SCALE = DIM_HEAD ** (-0.5)

        def _layer_norm(x, gamma):
            mu = jnp.mean(x, axis=-1, keepdims=True)
            var = jnp.var(x, axis=-1, keepdims=True)
            return (x - mu) * jax.lax.rsqrt(var + 1e-05) * gamma
        b, n, _ = x.shape
        xn = _layer_norm(x, gamma)
        q = xn @ w_q
        kv = xn @ w_kv
        k, v = jnp.split(kv, 2, axis=-1)
        q = q * SCALE

        def to_heads(t):
            return t.reshape(b, n, HEADS, DIM_HEAD).transpose(0, 2, 1, 3)
        q, k, v = map(to_heads, (q, k, v))
        nk = jnp.broadcast_to(null_kv[0][None], (b, HEADS, 1, DIM_HEAD))
        nv = jnp.broadcast_to(null_kv[1][None], (b, HEADS, 1, DIM_HEAD))
        k = jnp.concatenate([nk, k], axis=2)
        v = jnp.concatenate([nv, v], axis=2)
        sim = jnp.einsum('bhid,bhjd->bhij', q, k)
        attn = jax.nn.softmax(sim, axis=-1)
        out = jnp.einsum('bhij,bhjd->bhid', attn, v)
        out = out.transpose(0, 2, 1, 3).reshape(b, n, INNER)
        return out @ w_out

    def _L0_ffn_ref(x, router_kernel_DE, kernel_gating_EDF, kernel_up_EDF, kernel_down_EFD):
        import jax, jax.numpy as jnp
        import numpy as np
        TOP_K = 2
        E = router_kernel_DE.shape[-1]
        x = x.astype(jnp.float32)
        logits_BSE = jnp.einsum('BSD,DE->BSE', x, router_kernel_DE)
        probs_BSE = jax.nn.softmax(logits_BSE.astype(jnp.float32), axis=-1)
        weights_BSK, indices_BSK = jax.lax.top_k(probs_BSE, TOP_K)
        norm_weights_BSK = jax.nn.softmax(weights_BSK, axis=-1)
        one_hot_BSKE = jax.nn.one_hot(indices_BSK, num_classes=E, dtype=x.dtype)
        full_weights_BSE = jnp.sum(one_hot_BSKE * norm_weights_BSK[..., None], axis=2)
        gating_BSEF = jnp.einsum('BSD,EDF->BSEF', x, kernel_gating_EDF)
        act_BSEF = jax.nn.silu(gating_BSEF)
        up_BSEF = jnp.einsum('BSD,EDF->BSEF', x, kernel_up_EDF)
        fuse_BSEF = act_BSEF * up_BSEF
        down_BSED = jnp.einsum('BSEF,EFD->BSED', fuse_BSEF, kernel_down_EFD)
        out_BSD = jnp.einsum('BSED,BSE->BSD', down_BSED, full_weights_BSE)
        return out_BSD.astype(jnp.float32)

    def _L1_attn_a_ref(x, wq, bq, wk, bk, wv, bv, wo, bo):
        import jax, jax.numpy as jnp
        import numpy as np
        H = 16
        ROPE_BASE = 10000.0

        def _rotate_half(x):
            d = x.shape[-1]
            return jnp.concatenate((-x[..., d // 2:], x[..., :d // 2]), axis=-1)
        B, S, E = x.shape
        D = E // H

        def proj(w, b):
            return (x @ w.T + b).reshape(B, S, H, D).transpose(0, 2, 1, 3)
        q = proj(wq, bq)
        k = proj(wk, bk)
        v = proj(wv, bv)
        inv_freq = 1.0 / ROPE_BASE ** (jnp.arange(0, D, 2, dtype=jnp.float32) / D)
        freqs = jnp.arange(S, dtype=jnp.float32)[:, None] * inv_freq[None, :]
        cos = jnp.repeat(jnp.cos(freqs), 2, axis=-1)[None, None]
        sin = jnp.repeat(jnp.sin(freqs), 2, axis=-1)[None, None]
        q = q * cos + _rotate_half(q) * sin
        k = k * cos + _rotate_half(k) * sin
        scale = D ** (-0.5)
        scores = jnp.einsum('bhqd,bhkd->bhqk', q, k) * scale
        attn = jax.nn.softmax(scores, axis=-1)
        out = jnp.einsum('bhqk,bhkd->bhqd', attn, v)
        out = out.transpose(0, 2, 1, 3).reshape(B, S, E)
        return out @ wo.T + bo

    def _L1_attn_b_ref(x, Wq, bq, Wk, bk, Wv, bv, Wo, bo, ln_g, ln_b):
        import jax, jax.numpy as jnp
        import numpy as np
        C = 128
        H = 16
        K = 2
        B, N = (4, 512)

        def _heads(t):
            shp = t.shape
            d = shp[-1] // H
            t = t.reshape(shp[:-1] + (H, d))
            return jnp.swapaxes(t, -2, -3)
        dtype = x.dtype
        q = x + jnp.einsum('bnc,cd->bnd', x, Wq) + bq
        ks = x[None] + jnp.einsum('bnc,kcd->kbnd', x, Wk) + bk[:, None, None, :]
        vs = x[None] + jnp.einsum('bnc,kcd->kbnd', x, Wv) + bv[:, None, None, :]
        q = _heads(q)
        ks = _heads(ks)
        vs = _heads(vs)
        scale = 1.0 / jnp.sqrt(jnp.asarray(N, dtype=jnp.float32))
        ks = ks.astype(jnp.float32) * scale
        vs = vs.astype(jnp.float32) * scale
        states = jnp.einsum('kbhnd,kbhne->kbhde', ks, vs)
        state = jnp.prod(states, axis=0)
        out = jnp.einsum('bhnd,bhde->bhne', q.astype(jnp.float32), state)
        out = out.astype(dtype)
        out = jnp.swapaxes(out, 1, 2).reshape(x.shape[0], x.shape[1], C)
        mu = jnp.mean(out, axis=-1, keepdims=True)
        var = jnp.var(out, axis=-1, keepdims=True)
        out = (out - mu) / jnp.sqrt(var + 1e-05) * ln_g + ln_b
        out = jnp.einsum('bnc,cd->bnd', out, Wo) + bo
        return out

    def _L1_ffn_ref(x, input_ids, gate_w, gate_b, w13, w2, w13_s, w2_s):
        import jax, jax.numpy as jnp
        import numpy as np
        from jax import lax
        DIM = 128
        INTER = 64
        N_EXPERTS = 16
        TOPK = 4
        ROUTE_SCALE = 2.5
        VOCAB = 4000

        def _silu_and_mul(gu):
            gate, up = jnp.split(gu, 2, axis=-1)
            return jax.nn.silu(gate) * up
        B, S, D = x.shape
        xt = x.reshape(-1, D)
        T = xt.shape[0]
        scores = jax.nn.sigmoid(xt.astype(jnp.float32) @ gate_w.T)
        biased = scores + gate_b
        _, idx = lax.top_k(biased, TOPK)
        w = jnp.take_along_axis(scores, idx, axis=-1)
        w = w / jnp.sum(w, axis=-1, keepdims=True)
        w = w * ROUTE_SCALE
        comb = jnp.zeros((T, N_EXPERTS), jnp.float32)
        comb = comb.at[jnp.arange(T)[:, None], idx].add(w)
        comb = comb.astype(x.dtype)

        def expert_body(y, args):
            w13_e, w2_e, c_e = args
            h = _silu_and_mul(xt @ w13_e.T)
            return (y + c_e[:, None] * (h @ w2_e.T), None)
        y, _ = lax.scan(expert_body, jnp.zeros_like(xt), (w13, w2, comb.T))
        y = y + _silu_and_mul(xt @ w13_s.T) @ w2_s.T
        return y.astype(x.dtype).reshape(B, S, D)
    x = L0_attn_a_x
    x = x + _L0_attn_a_ref(_layernorm(x, axis=-1), L0_attn_a_q_w, L0_attn_a_q_b, L0_attn_a_k_w, L0_attn_a_k_b, L0_attn_a_v_w, L0_attn_a_v_b, L0_attn_a_o_w, L0_attn_a_o_b)
    x = x + _L0_ffn_ref(_layernorm(x, axis=-1), L0_ffn_router_kernel_DE, L0_ffn_kernel_gating_EDF, L0_ffn_kernel_up_EDF, L0_ffn_kernel_down_EFD)
    x = x + _L0_attn_b_ref(_layernorm(x, axis=-1), L0_attn_b_gamma, L0_attn_b_w_q, L0_attn_b_w_kv, L0_attn_b_w_out, L0_attn_b_null_kv)
    x = x + _L0_ffn_ref(_layernorm(x, axis=-1), L0_ffn_router_kernel_DE, L0_ffn_kernel_gating_EDF, L0_ffn_kernel_up_EDF, L0_ffn_kernel_down_EFD)
    x = x + _L1_attn_a_ref(_layernorm(x, axis=-1), L1_attn_a_wq, L1_attn_a_bq, L1_attn_a_wk, L1_attn_a_bk, L1_attn_a_wv, L1_attn_a_bv, L1_attn_a_wo, L1_attn_a_bo)
    x = x + _L1_ffn_ref(_layernorm(x, axis=-1), L1_ffn_input_ids, L1_ffn_gate_w, L1_ffn_gate_b, L1_ffn_w13, L1_ffn_w2, L1_ffn_w13_s, L1_ffn_w2_s)
    x = x + _L1_attn_b_ref(_layernorm(x, axis=-1), L1_attn_b_Wq, L1_attn_b_bq, L1_attn_b_Wk, L1_attn_b_bk, L1_attn_b_Wv, L1_attn_b_bv, L1_attn_b_Wo, L1_attn_b_bo, L1_attn_b_ln_g, L1_attn_b_ln_b)
    x = x + _L1_ffn_ref(_layernorm(x, axis=-1), L1_ffn_input_ids, L1_ffn_gate_w, L1_ffn_gate_b, L1_ffn_w13, L1_ffn_w2, L1_ffn_w13_s, L1_ffn_w2_s)
    return x

_drawn_inputs = setup_inputs


def setup_inputs(seed=0):
    import zlib

    import numpy as np

    out = dict(_drawn_inputs(seed))
    spreads = {'L0_attn_b_gamma': (1.0, 0.2),
     'L1_attn_b_bq': (0.0, 0.1),
     'L1_attn_b_bk': (0.0, 0.1),
     'L1_attn_b_bv': (0.0, 0.282),
     'L1_attn_b_bo': (0.0, 0.1),
     'L1_attn_b_ln_g': (1.0, 0.2),
     'L1_attn_b_ln_b': (0.0, 0.1)}
    factors = {'L0_attn_a_q_w': 8.0,
     'L0_attn_a_q_b': 8.0,
     'L0_attn_a_k_w': 8.0,
     'L0_attn_a_k_b': 8.0,
     'L0_attn_a_v_w': 4.788,
     'L0_attn_a_v_b': 2.684,
     'L0_attn_b_null_kv': 8.0,
     'L0_ffn_router_kernel_DE': 5.679,
     'L0_ffn_kernel_gating_EDF': 4.957,
     'L0_ffn_kernel_up_EDF': 4.934,
     'L0_ffn_kernel_down_EFD': 4.951,
     'L1_attn_a_wq': 8.0,
     'L1_attn_a_bq': 8.0,
     'L1_attn_a_wk': 8.0,
     'L1_attn_a_bk': 8.0,
     'L1_attn_a_wv': 5.505,
     'L1_attn_a_bv': 8.0,
     'L1_attn_a_wo': 4.581,
     'L1_ffn_gate_w': 8.0,
     'L1_ffn_gate_b': 8.0,
     'L1_ffn_w13': 8.0,
     'L1_ffn_w2': 8.0,
     'L1_ffn_w13_s': 8.0,
     'L1_ffn_w2_s': 8.0}
    for name, (base, spread) in spreads.items():
        noise = np.random.default_rng([zlib.crc32(name.encode()), seed]).standard_normal(out[name].shape)
        drawn = base * np.exp(spread * noise) if base else spread * noise
        out[name] = jnp.asarray(drawn.astype(out[name].dtype))
    for name, factor in factors.items():
        out[name] = (out[name] * factor).astype(out[name].dtype)
    return out
```

```python
from contextlib import ExitStack

import concourse.bass as bass
from concourse import mybir

F32 = mybir.dt.float32
BF16 = mybir.dt.bfloat16
ALU = mybir.AluOpType
ACT = mybir.ActivationFunctionType
AX = mybir.AxisListType

P = 128
B, S, D = 4, 1024, 128
TT = S // P
HALF = 512
NH = 16
DH = D // NH
WH = 64
GH = 4
GROUPS = NH // GH
E0, F0, K0 = 8, 256, 2
E1, F1, K1 = 16, 64, 4
ROUTE_SCALE = 2.5
BETA, THR, SPIKE_STEPS = 0.95, 1.0, 4
EPS = 1e-5
LIN_N = 512
LIN_K = 2


def hybrid_kernel(nc, A, out):
    ctx = ExitStack()
    with ctx:
        def sb(name, shape, dt=F32):
            return ctx.enter_context(nc.sbuf_tensor(name, shape, dt))

        sems = {}

        def sem(name):
            if name not in sems:
                sems[name] = ctx.enter_context(nc.semaphore(name))
            return sems[name]

        def end_stage(*names):
            nc.all_engine_barrier()
            for name in names:
                nc.sync.sem_clear(sem(name))
            nc.all_engine_barrier()

        ps = ctx.enter_context(nc.psum_tensor("ps", [P, 8, HALF], F32))

        ident = sb("ident", [P, P])
        head_mask = sb("head_mask", [P, NH])
        pair_mask = sb("pair_mask", [P, 2])
        block_mask = sb("block_mask", [P, P])
        tri = sb("tri", [P, E1, E1])
        half_neg = sb("half_neg", [P, TT])
        W = {}
        resident = ["a_qw", "a_kw", "a_vw", "a_ow", "a_qb", "a_kb", "a_vb", "a_ob",
                    "m_router", "m_gate", "m_up", "m_down", "b_gamma",
                    "c_qw", "c_kw", "c_qrw", "c_krw", "c_vw", "c_ow", "c_qb", "c_kb", "c_qrb", "c_krb", "c_vb", "c_ob",
                    "l_qw", "l_kw", "l_vw", "l_ow", "l_qb", "l_kb", "l_vb", "l_ob", "l_g", "l_b",
                    "n_router", "n_bias", "n_gate", "n_up", "n_down", "n_sgate", "n_sup", "n_sdown"]
        for n in resident:
            W[n] = sb("w_" + n, list(A[n].shape))

        x = sb("x", [P, TT, D])
        xn = sb("xn", [P, TT, D])
        xT = sb("xT", [P, S])
        stats = sb("stats", [P, TT, 6])
        meanvar = sb("meanvar", [P, TT, 2])
        rstd = sb("rstd", [P, TT])
        qT = sb("qT", [P, 2, S])
        kT = sb("kT", [P, 2, S])
        qc = sb("qc", [P, S], BF16)
        kc = sb("kc", [P, S], BF16)
        v_rows = sb("v_rows", [P, TT, 256])
        q_head = sb("q_head", [P, 2, S])
        q_head_bf = sb("q_head_bf", [P, 2, S], BF16)
        v_head = sb("v_head", [P, 2, TT, WH])
        probs = sb("probs", [P, 2, S + 8])
        probsT = sb("probsT", [P, 2, TT, S])
        null_probs = sb("null_probs", [P, GH, TT])
        neg_max = sb("neg_max", [P, GH, TT])
        row_sum = sb("row_sum", [P, GH, TT])
        row_rec = sb("row_rec", [P, GH, TT])
        outT = sb("outT", [P, GH, HALF])
        o_rows = sb("o_rows", [P, TT, 256])
        lifm, lift = q_head[:, 0, :], q_head[:, 1, :]
        o_tmp = q_head[:, :, :].rearrange("p a (t c) -> p (a t) c", c=256)
        r_s = sb("r_s", [P, TT])
        r_r = sb("r_r", [P, TT])
        big = probsT[:, :, :, :].rearrange("p a t s -> p (a t s)")
        r_cmp = big[:, 0:TT * E1 * E1]
        r_eq = big[:, TT * E1 * E1:2 * TT * E1 * E1]
        act_g = big[:, 4096:4096 + 2 * HALF].rearrange("p (a n) -> p a n", a=2)
        fuse = big[:, 5120:5120 + 4 * HALF].rearrange("p (a n) -> p a n", a=4)
        r_a, r_b, r_c, r_w = (big[:, 10240 + k * P:10240 + (k + 1) * P].rearrange("p (t e) -> p t e", e=E1) for k in range(4))
        cos_t, sin_t = probs[:, 0, 0:S], probs[:, 1, 0:S]

        x_in = A["x"].rearrange("b (t p) d -> b p t d", p=P)
        x_out = out.rearrange("b (t p) d -> b p t d", p=P)

        def tiles_of(bank, n=TT, w=P):
            per = HALF // w
            k = -(-n // per)
            return ps[:, bank:bank + k, :].rearrange("p k (t w) -> p (k t) w", w=w)[:, 0:n, :]

        def layer_norm(src, dst):
            st, mv, pw, nd, tp, ev = (sem(n) for n in ("ln_stats", "ln_meanvar", "ln_pow", "ln_rows", "ln_transposed", "ln_evacuated"))
            with nc.Block() as block:
                @block.vector
                def _(dve):
                    for t in range(TT):
                        dve.bn_stats(stats[:, t, :], src[:, t, :]).then_inc(st, 1)
                    dve.wait_ge(st, TT)
                    for t in range(TT):
                        dve.bn_aggr(meanvar[:, t, :], stats[:, t, :]).then_inc(mv, 1)
                    dve.wait_ge(mv, TT)
                    dve.tensor_scalar(rstd[:, :], meanvar[:, :, 1], EPS, None, ALU.add).then_inc(mv, 1)
                    dve.wait_ge(pw, 1)
                    for t in range(TT):
                        dve.tensor_scalar(dst[:, t, :], src[:, t, :], meanvar[:, t, 0:1], rstd[:, t:t + 1],
                                          ALU.subtract, ALU.mult).then_inc(nd, 1)

                @block.gpsimd
                def _(pool):
                    pool.wait_ge(mv, TT + 1)
                    pool.tensor_tensor(rstd[:, :], rstd[:, :], half_neg[:, :], ALU.pow).then_inc(pw, 1)

                @block.tensor
                def _(pe):
                    for t in range(TT):
                        pe.wait_ge(nd, t + 1)
                        pe.transpose(tiles_of(0)[:, t, :], dst[:, t, :], ident[:, :]).then_inc(tp, 1)

                @block.scalar
                def _(act):
                    for k in range(2):
                        act.wait_ge(tp, 4 * k + 4)
                        act.activation(xT[:, k * HALF:(k + 1) * HALF], ps[:, k, :], ACT.Copy).then_inc(ev, 1)
            end_stage("ln_stats", "ln_meanvar", "ln_pow", "ln_rows", "ln_transposed", "ln_evacuated")

        def rows_out(srcT, weights, bias_rows, first_bank=2):
            done, added = sem("ro_done"), sem("ro_added")
            with nc.Block() as block:
                @block.tensor
                def _(pe):
                    for t in range(TT):
                        for n, (s, w) in enumerate(zip(srcT, weights)):
                            mm = pe.matmul(tiles_of(first_bank)[:, t, :], s[:, t * P:(t + 1) * P], w,
                                           start=(n == 0), stop=(n == len(srcT) - 1))
                        mm.then_inc(done, 1)

                @block.vector
                def _(dve):
                    if bias_rows is not None:
                        dve.tensor_tensor(x[:, :, :], x[:, :, :],
                                          bias_rows[:, :].unsqueeze(1).broadcast_to([P, TT, D]), ALU.add).then_inc(added, 1)
                        dve.wait_ge(added, 1)
                    dve.wait_ge(done, TT)
                    dve.tensor_tensor(x[:, :, :], x[:, :, :], tiles_of(first_bank), ALU.add).then_inc(added, 1)
            end_stage("ro_done", "ro_added")

        def lif_projections():
            mm, cur, ch = sem("lp_products"), sem("lp_current"), sem("lp_chain")
            with nc.Block() as block:
                @block.tensor
                def _(pe):
                    for n, w in enumerate(("a_qw", "a_kw")):
                        for k in range(2):
                            pe.matmul(ps[:, 2 * n + k, :], W[w][:, :], xT[:, k * HALF:(k + 1) * HALF],
                                      start=True, stop=True).then_inc(mm, 1)
                    for t in range(TT):
                        pe.matmul(tiles_of(4)[:, t, :], xT[:, t * P:(t + 1) * P], W["a_vw"][:, :],
                                  start=True, stop=True).then_inc(mm, 1)

                @block.scalar
                def _(act):
                    for n, b in enumerate(("a_qb", "a_kb")):
                        act.wait_ge(mm, 2 * n + 2)
                        act.activation(qT[:, n, :].rearrange("p (k c) -> p k c", k=2), ps[:, 2 * n:2 * n + 2, :],
                                       ACT.Identity, bias=W[b][:, 0:1]).then_inc(cur, 1)

                @block.vector
                def _(dve):
                    n_chain = 0

                    def chained(ins):
                        nonlocal n_chain
                        n_chain += 1
                        ins.then_inc(ch, 1)
                        dve.wait_ge(ch, n_chain)

                    def neurons(c, counts):
                        mem, nxt = lifm, lift
                        chained(dve.tensor_scalar(mem, c, BETA, None, ALU.mult))
                        chained(dve.tensor_tensor(nxt, mem, c, ALU.add))
                        chained(dve.scalar_tensor_tensor(out=mem, in0=c, scalar=THR, in1=nxt, op0=ALU.is_gt,
                                                         op1=ALU.subtract, reverse1=True))
                        chained(dve.tensor_scalar(counts, c, THR, None, ALU.is_gt))
                        for step in range(2, SPIKE_STEPS + 1):
                            chained(dve.scalar_tensor_tensor(out=counts, in0=mem, scalar=THR, in1=counts,
                                                             op0=ALU.is_gt, op1=ALU.add))
                            if step < SPIKE_STEPS:
                                chained(dve.scalar_tensor_tensor(out=nxt, in0=mem, scalar=BETA, in1=c,
                                                                 op0=ALU.mult, op1=ALU.add))
                                chained(dve.scalar_tensor_tensor(out=mem, in0=mem, scalar=THR, in1=nxt,
                                                                 op0=ALU.is_gt, op1=ALU.subtract, reverse1=True))

                    dve.wait_ge(cur, 1)
                    neurons(qT[:, 0, :], qc[:, :])
                    dve.wait_ge(cur, 2)
                    neurons(qT[:, 1, :], kc[:, :])
                    dve.wait_ge(mm, 4 + TT)
                    chained(dve.tensor_tensor(kT[:, 0, :].rearrange("p (t d) -> p t d", d=D), tiles_of(4),
                                              W["a_vb"][:, :].unsqueeze(1).broadcast_to([P, TT, D]), ALU.add))
                    neurons(kT[:, 0, :], kT[:, 1, :])
                    chained(dve.tensor_copy(v_rows[:, :, 0:D], kT[:, 1, :].rearrange("p (t d) -> p t d", d=D)))
            end_stage("lp_products", "lp_current", "lp_chain")

        def narrow_value_head(eng, g, hh):
            return eng.tensor_copy(v_head[:, hh % 2, :, 0:DH], v_rows[:, :, bass.ds(g * (GH * DH) + hh * DH, DH)])

        def narrow_pv(pe, hh, kt):
            for c in range(4):
                mm = pe.matmul(ps[32 * c:32 * c + 32, 6, 0:256], v_head[:, hh % 2, kt, 0:32],
                               probsT[:, hh % 2, kt, 256 * c:256 * c + 256], start=(kt == 0), stop=(kt == TT - 1))
            return mm

        def narrow_post(g):
            tp, ch = sem("np_transposed"), sem("np_chain")
            with nc.Block() as block:
                @block.tensor
                def _(pe):
                    for hh in range(GH):
                        for j in range(2):
                            pe.transpose(tiles_of(0)[:, 2 * hh + j, :], outT[:, hh, j * P:(j + 1) * P],
                                         ident[:, :]).then_inc(tp, 1)

                @block.vector
                def _(dve):
                    for hh in range(GH):
                        dve.wait_ge(tp, 4 * (hh // 2) + 4)
                        part = tiles_of(0)[:, 2 * hh:2 * hh + 2, :].rearrange("p j (c w) -> p c j w", w=32)
                        rec = row_rec[:, hh, :].rearrange("p (c j) -> p c j", j=2)
                        dve.reciprocal(rec, part[:, :, :, DH]).then_inc(ch, 1)
                        dve.wait_ge(ch, 2 * hh + 1)
                        dst = o_rows[:, :, bass.ds(g * (GH * DH) + hh * DH, DH)].rearrange("p (c j) w -> p c j w", j=2)
                        dve.tensor_tensor(dst, part[:, :, :, 0:DH], rec.unsqueeze(3).broadcast_to([P, 4, 2, DH]),
                                          ALU.mult).then_inc(ch, 1)
            end_stage("np_transposed", "np_chain")

        def lif_heads(g):
            qh, vh, sc, ex, pv, oe = (sem(n) for n in ("lh_query", "lh_value", "lh_scores", "lh_exp", "lh_sums", "lh_out"))
            scale = 1.0 / (SPIKE_STEPS * SPIKE_STEPS) / float(DH) ** 0.5
            with nc.Block() as block:
                @block.vector
                def _(dve):
                    for hh in range(GH + 1):
                        if hh < GH:
                            if hh >= 2:
                                dve.wait_ge(sc, TT * (hh - 1))
                            dve.tensor_scalar(q_head_bf[:, hh % 2, :], qc[:, :], head_mask[:, bass.ds(g * GH + hh, 1)],
                                              None, ALU.mult).then_inc(qh, 1)
                        if hh >= 1:
                            dve.wait_ge(pv, hh)
                            dve.tensor_copy(outT[:, hh - 1, 0:256], ps[:, 6, 0:256]).then_inc(oe, 1)

                @block.gpsimd
                def _(pool):
                    for hh in range(GH):
                        if hh < 2:
                            pool.memset(v_head[:, hh, :, DH:32], 0.0).then_inc(vh, 1)
                            pool.wait_ge(vh, 3 * hh + 1)
                            pool.memset(v_head[:, hh, :, DH:DH + 1], float(SPIKE_STEPS)).then_inc(vh, 1)
                        else:
                            pool.wait_ge(pv, hh - 1)
                        narrow_value_head(pool, g, hh).then_inc(vh, 1)

                @block.tensor
                def _(pe):
                    def sums(hh, kt):
                        if kt == 0:
                            pe.wait_ge(vh, 3 * min(hh + 1, 2) + max(hh - 1, 0))
                            if hh >= 1:
                                pe.wait_ge(oe, hh)
                        pe.wait_ge(ex, TT * hh + kt + 1)
                        mm = narrow_pv(pe, hh, kt)
                        if kt == TT - 1:
                            mm.then_inc(pv, 1)

                    for hh in range(GH):
                        pe.wait_ge(qh, hh + 1)
                        for kt in range(TT):
                            u = TT * hh + kt
                            if u >= 2:
                                pe.wait_ge(ex, u - 1)
                            for k in range(2):
                                mm = pe.matmul(ps[:, 2 * (u % 2) + k, :], kc[:, kt * P:(kt + 1) * P],
                                               q_head_bf[:, hh % 2, k * HALF:(k + 1) * HALF], start=True, stop=True)
                            mm.then_inc(sc, 1)
                            if hh >= 1:
                                sums(hh - 1, kt)
                    for kt in range(TT):
                        sums(GH - 1, kt)

                @block.scalar
                def _(act):
                    for hh in range(GH):
                        if hh >= 2:
                            act.wait_ge(pv, hh - 1)
                        for kt in range(TT):
                            u = TT * hh + kt
                            act.wait_ge(sc, u + 1)
                            act.activation(probsT[:, hh % 2, kt, :].rearrange("p (k c) -> p k c", k=2),
                                           ps[:, 2 * (u % 2):2 * (u % 2) + 2, :], ACT.Exp, scale=scale).then_inc(ex, 1)
            end_stage("lh_query", "lh_value", "lh_scores", "lh_exp", "lh_sums", "lh_out")

        def softmax_heads(g, width, q_of, k_of, mask_of, null_of, value_head, value_sums, sums_bank, out_cols):
            names = ("sh_query", "sh_value", "sh_scores", "sh_max", "sh_exp", "sh_transposed", "sh_evac_act",
                     "sh_evac_dve", "sh_sums", "sh_out", "sh_null")
            qh, vh, sc, mx, ex, tp, ea, ed, pv, oe, nu = (sem(n) for n in names)
            wide = width > S
            banks = 3 if wide else 2
            units = GH * TT

            def scores_of(u):
                return ps[:, banks * (u % 2):banks * (u % 2) + banks, :].rearrange("p k c -> p (k c)")[:, 0:width]

            with nc.Block() as block:
                @block.tensor
                def _(pe):
                    def transposes(u):
                        pe.wait_ge(ex, u + 1)
                        for half in range(2):
                            if u > 0 or half:
                                pe.wait_ge(ed if half == 0 else ea, u if half == 0 else u + 1)
                            for j in range(4):
                                mm = pe.transpose(ps[:, 7, j * P:(j + 1) * P],
                                                  probs[:, u % 2, (4 * half + j) * P:(4 * half + j + 1) * P], ident[:, :])
                            mm.then_inc(tp, 1)
                            if half == 0:
                                between(u)

                    def between(u):
                        hh, qt = divmod(u, TT)
                        if hh >= 1:
                            sums(hh - 1, qt)

                    def sums(hh, kt):
                        if kt == 0:
                            pe.wait_ge(vh, hh + 1)
                            pe.wait_ge(ea, TT * (hh + 1))
                            pe.wait_ge(ed, TT * (hh + 1))
                            if hh >= 1:
                                pe.wait_ge(oe, hh)
                        mm = value_sums(pe, hh, kt)
                        if kt == TT - 1:
                            mm.then_inc(pv, 1)

                    for u in range(units + 1):
                        if u < units:
                            hh, qt = divmod(u, TT)
                            if qt == 0:
                                pe.wait_ge(qh, hh + 1)
                            if u >= 2:
                                pe.wait_ge(ex, u - 1)
                            for k in range(2):
                                mm = pe.matmul(scores_of(u)[:, k * HALF:(k + 1) * HALF],
                                               q_head[:, hh % 2, qt * P:(qt + 1) * P],
                                               k_of(hh)[:, k * HALF:(k + 1) * HALF], start=True, stop=True)
                            if wide:
                                mm = pe.matmul(scores_of(u)[:, S:S + 1], q_head[:, hh % 2, qt * P:(qt + 1) * P],
                                               null_of(hh), start=True, stop=True)
                            mm.then_inc(sc, 1)
                        if u >= 1:
                            transposes(u - 1)
                    for kt in range(TT):
                        sums(GH - 1, kt)

                @block.vector
                def _(dve):
                    def query_head(hh):
                        if hh >= 2:
                            dve.wait_ge(sc, TT * (hh - 1))
                        dve.tensor_scalar(q_head[:, hh % 2, :], q_of(hh), mask_of(hh), None, ALU.mult).then_inc(qh, 1)

                    query_head(0)
                    query_head(1)
                    for u in range(units + 1):
                        hh, qt = divmod(u, TT)
                        if u < units:
                            dve.wait_ge(sc, u + 1)
                            dve.tensor_reduce(neg_max[:, hh, qt:qt + 1], scores_of(u), AX.X, ALU.max,
                                              negate=True).then_inc(mx, 1)
                        if u >= 1:
                            ph, pq = divmod(u - 1, TT)
                            if pq == 0 and ph >= 2:
                                dve.wait_ge(pv, ph - 1)
                            dve.wait_ge(tp, 2 * u)
                            dve.tensor_copy(probsT[:, ph % 2, 4:8, pq * P:(pq + 1) * P],
                                            ps[:, 7, :].rearrange("p (j c) -> p j c", c=P)).then_inc(ed, 1)
                        if qt == 0 and 1 <= hh < GH - 1:
                            query_head(hh + 1)
                        if hh >= 2 and qt == 0:
                            dve.wait_ge(pv, hh - 1)
                            dve.tensor_copy(outT[:, hh - 2, 0:out_cols], ps[:, sums_bank, 0:out_cols]).then_inc(oe, 1)
                    for hh in range(GH - 1, GH):
                        dve.wait_ge(pv, hh + 1)
                        dve.tensor_copy(outT[:, hh, 0:out_cols], ps[:, sums_bank, 0:out_cols]).then_inc(oe, 1)

                @block.scalar
                def _(act):
                    for u in range(units + 1):
                        hh, qt = divmod(u, TT)
                        if u < units:
                            act.wait_ge(mx, u + 1)
                            if u >= 2:
                                act.wait_ge(tp, 2 * (u - 1))
                                if wide:
                                    act.wait_ge(nu, u - 1)
                            act.activation(probs[:, u % 2, 0:width], scores_of(u), ACT.Exp,
                                           bias=neg_max[:, hh, qt:qt + 1],
                                           accum_out=row_sum[:, hh, qt:qt + 1]).then_inc(ex, 1)
                        if u >= 1:
                            ph, pq = divmod(u - 1, TT)
                            if pq == 0 and ph >= 2:
                                act.wait_ge(pv, ph - 1)
                            act.wait_ge(tp, 2 * u - 1)
                            act.activation(probsT[:, ph % 2, 0:4, pq * P:(pq + 1) * P],
                                           ps[:, 7, :].rearrange("p (j c) -> p j c", c=P), ACT.Copy).then_inc(ea, 1)

                @block.gpsimd
                def _(pool):
                    for hh in range(GH):
                        if hh >= 2:
                            pool.wait_ge(pv, hh - 1)
                        value_head(pool, hh).then_inc(vh, 1)
                        if wide:
                            for qt in range(TT):
                                u = TT * hh + qt
                                pool.wait_ge(ex, u + 1)
                                pool.tensor_copy(null_probs[:, hh, qt:qt + 1], probs[:, u % 2, S:S + 1]).then_inc(nu, 1)
            end_stage(*names)

        def rope_projections():
            mm, ra, ro = sem("rp_products"), sem("rp_parts"), sem("rp_done")
            scale = float(DH) ** -0.5
            todo = (("c_qw", "c_qb", "c_qrw", "c_qrb", qT), ("c_kw", "c_kb", "c_krw", "c_krb", kT))
            with nc.Block() as block:
                @block.sync
                def _(sp):
                    sp.dma_start(cos_t, A["cos"]).then_inc(sem("rp_tables"), 16)
                    sp.dma_start(sin_t, A["sin"]).then_inc(sem("rp_tables"), 16)

                @block.tensor
                def _(pe):
                    for n, (w, _, wr, _, _) in enumerate(todo):
                        if n:
                            pe.wait_ge(ra, 2)
                        for m, ww in enumerate((w, wr)):
                            for k in range(2):
                                pe.matmul(ps[:, 2 * m + k, :], W[ww][:, :], xT[:, k * HALF:(k + 1) * HALF],
                                          start=True, stop=True).then_inc(mm, 1)
                    for t in range(TT):
                        pe.matmul(tiles_of(4)[:, t, :], xT[:, t * P:(t + 1) * P], W["c_vw"][:, :],
                                  start=True, stop=True).then_inc(mm, 1)

                @block.vector
                def _(dve):
                    dve.wait_ge(sem("rp_tables"), 32)
                    for n, (_, b, _, br, dst) in enumerate(todo):
                        for m, (bb, table) in enumerate(((b, cos_t), (br, sin_t))):
                            dve.wait_ge(mm, 4 * n + 2 * m + 2)
                            dve.scalar_tensor_tensor(out=dst[:, m, :].rearrange("p (k c) -> p k c", k=2),
                                                     in0=ps[:, 2 * m:2 * m + 2, :], scalar=W[bb][:, 0:1],
                                                     in1=table.rearrange("p (k c) -> p k c", k=2),
                                                     op0=ALU.add, op1=ALU.mult).then_inc(ra, 1)
                        dve.wait_ge(ra, 2 * n + 2)
                        dve.tensor_tensor(dst[:, 0, :], dst[:, 0, :], dst[:, 1, :], ALU.add).then_inc(ro, 1)
                    dve.wait_ge(ro, 1)
                    dve.tensor_scalar(qT[:, 0, :], qT[:, 0, :], scale, None, ALU.mult).then_inc(ro, 1)
                    dve.wait_ge(mm, 8 + TT)
                    dve.tensor_tensor(v_rows[:, :, 0:D], tiles_of(4),
                                      W["c_vb"][:, :].unsqueeze(1).broadcast_to([P, TT, D]), ALU.add).then_inc(ro, 1)

                @block.gpsimd
                def _(pool):
                    for hh in range(2):
                        pool.memset(v_head[:, hh, :, DH:32], 0.0).then_inc(ro, 1)
            end_stage("rp_products", "rp_parts", "rp_done", "rp_tables")

        def scaled_post(g):
            tp, ch = sem("np_transposed"), sem("np_chain")
            with nc.Block() as block:
                @block.tensor
                def _(pe):
                    for hh in range(GH):
                        for j in range(2):
                            pe.transpose(tiles_of(0)[:, 2 * hh + j, :], outT[:, hh, j * P:(j + 1) * P],
                                         ident[:, :]).then_inc(tp, 1)

                @block.vector
                def _(dve):
                    dve.reciprocal(row_rec[:, :, :], row_sum[:, :, :]).then_inc(ch, 1)
                    dve.wait_ge(ch, 1)
                    for hh in range(GH):
                        dve.wait_ge(tp, 4 * (hh // 2) + 4)
                        part = tiles_of(0)[:, 2 * hh:2 * hh + 2, :].rearrange("p j (c w) -> p c j w", w=32)
                        rec = row_rec[:, hh, :].rearrange("p (c j) -> p c j", j=2)
                        dst = o_rows[:, :, bass.ds(g * (GH * DH) + hh * DH, DH)].rearrange("p (c j) w -> p c j w", j=2)
                        dve.tensor_tensor(dst, part[:, :, :, 0:DH], rec.unsqueeze(3).broadcast_to([P, 4, 2, DH]),
                                          ALU.mult).then_inc(ch, 1)
            end_stage("np_transposed", "np_chain")

        def transposed_rows(n_blocks):
            tp, ev = sem("tr_transposed"), sem("tr_evacuated")
            with nc.Block() as block:
                @block.tensor
                def _(pe):
                    for c in range(n_blocks):
                        for t in range(TT):
                            pe.transpose(tiles_of(2 * c)[:, t, :], o_rows[:, t, c * P:(c + 1) * P],
                                         ident[:, :]).then_inc(tp, 1)

                @block.scalar
                def _(act):
                    for c in range(n_blocks):
                        for k in range(2):
                            act.wait_ge(tp, TT * c + 4 * k + 4)
                            act.activation(qT[:, c, k * HALF:(k + 1) * HALF], ps[:, 2 * c + k, :], ACT.Copy).then_inc(ev, 1)
            end_stage("tr_transposed", "tr_evacuated")

        bq_w = sb("bq_w", [P, 256])
        bk_w = sb("bk_w", [P, 256])
        bv_w = sb("bv_w", [P, 256])
        bo_w = sb("bo_w", [P, 2, D])
        bn_k = sb("bn_k", [P, 2])
        bn_v = sb("bn_v", [P, 256])

        def wide_projections(g):
            wl, mm, ev = sem("wp_weights"), sem("wp_products"), sem("wp_done")
            with nc.Block() as block:
                @block.sync
                def _(sp):
                    sp.dma_start(bq_w[:, :], A["b_qw"][:, bass.ds(g * 256, 256)]).then_inc(wl, 16)
                    sp.dma_start(bk_w[:, :], A["b_kvw"][:, bass.ds(g * 256, 256)]).then_inc(wl, 16)
                    sp.dma_start(bv_w[:, :], A["b_kvw"][:, bass.ds(g * 256 + 1024, 256)]).then_inc(wl, 16)
                    sp.dma_start(bo_w[:, :, :], A["b_ow"][:, bass.ds(g * 2, 2), :]).then_inc(wl, 16)
                    sp.dma_start(bn_k[:, :], A["b_nk"][:, bass.ds(g * 2, 2)]).then_inc(wl, 16)
                    sp.dma_start(bn_v[:, :], A["b_nv"][:, bass.ds(g * 256, 256)]).then_inc(wl, 16)

                @block.tensor
                def _(pe):
                    pe.wait_ge(wl, 96)
                    for c in range(2):
                        for n, w in enumerate((bq_w, bk_w)):
                            if c:
                                pe.wait_ge(ev, n + 1)
                            for k in range(2):
                                pe.matmul(ps[:, 2 * n + k, :], w[:, c * P:(c + 1) * P], xT[:, k * HALF:(k + 1) * HALF],
                                          start=True, stop=True).then_inc(mm, 1)
                    for t in range(TT):
                        pe.matmul(tiles_of(4, w=256)[:, t, :], xT[:, t * P:(t + 1) * P], bv_w[:, :],
                                  start=True, stop=True).then_inc(mm, 1)

                @block.scalar
                def _(act):
                    for c in range(2):
                        for n, (dst, s) in enumerate(((qT, float(WH) ** -0.5), (kT, 1.0))):
                            act.wait_ge(mm, 4 * c + 2 * n + 2)
                            act.activation(dst[:, c, :].rearrange("p (k c) -> p k c", k=2), ps[:, 2 * n:2 * n + 2, :],
                                           ACT.Copy, scale=s).then_inc(ev, 1)

                @block.vector
                def _(dve):
                    dve.wait_ge(mm, 8 + TT)
                    dve.tensor_copy(v_rows[:, :, :], tiles_of(4, w=256)).then_inc(ev, 1)

            end_stage("wp_weights", "wp_products", "wp_done")

        def wide_pv(pe, hh, kt):
            for c in range(2):
                mm = pe.matmul(ps[64 * c:64 * c + 64, 6, :], v_head[:, hh % 2, kt, :],
                               probsT[:, hh % 2, kt, HALF * c:HALF * c + HALF], start=(kt == 0), stop=(kt == TT - 1))
            return mm

        def wide_post(g):
            tp, ch, nn = sem("np_transposed"), sem("np_chain"), sem("wn_null")
            with nc.Block() as block:
                @block.tensor
                def _(pe):
                    for hh in range(GH):
                        for j in range(4):
                            pe.transpose(ps[:, hh, j * P:(j + 1) * P],
                                         outT[:, hh, j * P:(j + 1) * P], ident[:, :]).then_inc(tp, 1)

                @block.gpsimd
                def _(pool):
                    for hh in range(GH):
                        pool.tensor_tensor(o_tmp[:, :, hh * WH:(hh + 1) * WH],
                                           null_probs[:, hh, :].unsqueeze(2).broadcast_to([P, TT, WH]),
                                           bn_v[:, hh * WH:(hh + 1) * WH].unsqueeze(1).broadcast_to([P, TT, WH]),
                                           ALU.mult).then_inc(nn, 1)

                @block.vector
                def _(dve):
                    dve.reciprocal(row_rec[:, :, :], row_sum[:, :, :]).then_inc(ch, 1)
                    for hh in range(GH):
                        dve.wait_ge(tp, 4 * hh + 4)
                        dve.wait_ge(nn, hh + 1)
                        part = ps[:, hh, :].rearrange("p (j c w) -> p c j w", j=4, c=2)
                        tmp = o_tmp[:, :, hh * WH:(hh + 1) * WH]
                        t4 = tmp.rearrange("p (c j) w -> p c j w", c=2)
                        dve.tensor_tensor(t4, part, t4, ALU.add).then_inc(ch, 1)
                        dve.wait_ge(ch, 2 * hh + 2)
                        dve.tensor_tensor(o_rows[:, :, hh * WH:(hh + 1) * WH], tmp,
                                          row_rec[:, hh, :].unsqueeze(2).broadcast_to([P, TT, WH]),
                                          ALU.mult).then_inc(ch, 1)
            end_stage("np_transposed", "np_chain", "wn_null")

        def ranks(dve, ch, n0, vals, n_e, top):
            cmp4 = r_cmp[:, 0:TT * n_e * n_e].rearrange("p (t e f) -> p t e f", t=TT, e=n_e)
            eq4 = r_eq[:, 0:TT * n_e * n_e].rearrange("p (t e f) -> p t e f", t=TT, e=n_e)
            other = vals.unsqueeze(2).broadcast_to([P, TT, n_e, n_e])
            own = vals.unsqueeze(3).broadcast_to([P, TT, n_e, n_e])
            dve.tensor_tensor(cmp4, other, own, ALU.is_gt).then_inc(ch, 1)
            dve.tensor_tensor(eq4, other, own, ALU.is_equal).then_inc(ch, 1)
            dve.wait_ge(ch, n0 + 2)
            dve.tensor_tensor(eq4, eq4, tri[:, 0:n_e, 0:n_e].unsqueeze(1).broadcast_to([P, TT, n_e, n_e]),
                              ALU.mult).then_inc(ch, 1)
            dve.wait_ge(ch, n0 + 3)
            dve.tensor_tensor(cmp4, cmp4, eq4, ALU.add).then_inc(ch, 1)
            dve.wait_ge(ch, n0 + 4)
            dve.tensor_reduce(r_c[:, :, 0:n_e], cmp4, AX.X, ALU.add).then_inc(ch, 1)
            dve.wait_ge(ch, n0 + 5)
            dve.tensor_scalar(r_c[:, :, 0:n_e], r_c[:, :, 0:n_e], float(top) - 0.5, None, ALU.is_lt).then_inc(ch, 1)
            dve.wait_ge(ch, n0 + 6)
            return n0 + 6

        def router_first():
            mm, ch, ex = sem("rt_logits"), sem("rt_chain"), sem("rt_exp")
            lg = tiles_of(0, w=E0)
            with nc.Block() as block:
                @block.tensor
                def _(pe):
                    for t in range(TT):
                        last = pe.matmul(lg[:, t, :], xT[:, t * P:(t + 1) * P], W["m_router"][:, :], start=True, stop=True)
                    last.then_inc(mm, 1)

                @block.vector
                def _(dve):
                    a, b = r_a[:, :, 0:E0], r_b[:, :, 0:E0]
                    wide = lambda v: v[:, :].unsqueeze(2).broadcast_to([P, TT, E0])
                    dve.wait_ge(mm, 1)
                    dve.tensor_reduce(r_s[:, :], lg, AX.X, ALU.max).then_inc(ch, 1)
                    dve.wait_ge(ch, 1)
                    dve.tensor_tensor(a, lg, wide(r_s), ALU.subtract).then_inc(ch, 1)
                    dve.wait_ge(ex, 1)
                    dve.tensor_reduce(r_s[:, :], b, AX.X, ALU.add).then_inc(ch, 1)
                    dve.wait_ge(ch, 3)
                    dve.reciprocal(r_r[:, :], r_s[:, :]).then_inc(ch, 1)
                    dve.wait_ge(ch, 4)
                    dve.tensor_tensor(a, b, wide(r_r), ALU.mult).then_inc(ch, 1)
                    dve.wait_ge(ch, 5)
                    n = ranks(dve, ch, 5, a, E0, K0)
                    dve.wait_ge(ex, 2)
                    dve.tensor_tensor(b, b, r_c[:, :, 0:E0], ALU.mult).then_inc(ch, 1)
                    dve.wait_ge(ch, n + 1)
                    dve.tensor_reduce(r_s[:, :], b, AX.X, ALU.add).then_inc(ch, 1)
                    dve.wait_ge(ch, n + 2)
                    dve.reciprocal(r_r[:, :], r_s[:, :]).then_inc(ch, 1)
                    dve.wait_ge(ch, n + 3)
                    dve.tensor_tensor(r_w[:, :, 0:E0], b, wide(r_r), ALU.mult).then_inc(ch, 1)

                @block.scalar
                def _(act):
                    act.wait_ge(ch, 2)
                    act.activation(r_b[:, :, 0:E0], r_a[:, :, 0:E0], ACT.Exp).then_inc(ex, 1)
                    act.wait_ge(ch, 5)
                    act.activation(r_b[:, :, 0:E0], r_a[:, :, 0:E0], ACT.Exp).then_inc(ex, 1)
            end_stage("rt_logits", "rt_chain", "rt_exp")

        def experts_first():
            gt, up, si, fu, dn, ad = (sem(n) for n in ("ef_gate", "ef_up", "ef_silu", "ef_fused", "ef_down", "ef_added"))
            steps = 2 * E0 * (F0 // P)
            with nc.Block() as block:
                @block.tensor
                def _(pe):
                    def down(m):
                        pe.wait_ge(fu, 2 * m + 2)
                        if m >= 2:
                            pe.wait_ge(ad, 4 * (m - 1))
                        for s in range(4):
                            for f in range(2):
                                mm = pe.matmul(ps[:, 4 + m % 2, s * P:(s + 1) * P],
                                               fuse[:, (2 * m + f) % 4, s * P:(s + 1) * P],
                                               W["m_down"][:, 2 * (m % E0) + f, :], start=(f == 0), stop=(f == 1))
                        mm.then_inc(dn, 1)

                    for n in range(steps):
                        blk, e, f = n // (2 * E0), (n // 2) % E0, n % 2
                        if n >= 2:
                            pe.wait_ge(si, n - 1)
                            pe.wait_ge(fu, n - 1)
                        for m, w in enumerate(("m_gate", "m_up")):
                            pe.matmul(ps[:, 2 * m + n % 2, :], W[w][:, e * F0 + f * P:e * F0 + (f + 1) * P],
                                      xT[:, blk * HALF:(blk + 1) * HALF], start=True, stop=True).then_inc((gt, up)[m], 1)
                        if n % 2 == 0 and n >= 2:
                            down(n // 2 - 1)
                    down(steps // 2 - 1)

                @block.scalar
                def _(act):
                    for n in range(steps):
                        act.wait_ge(gt, n + 1)
                        if n >= 2:
                            act.wait_ge(fu, n - 1)
                        act.activation(act_g[:, n % 2, :], ps[:, n % 2, :], ACT.Silu).then_inc(si, 1)

                @block.vector
                def _(dve):
                    def add(m):
                        dve.wait_ge(dn, m + 1)
                        e = m % E0
                        for s in range(4):
                            t = 4 * (m // E0) + s
                            if m % E0:
                                dve.wait_ge(ad, 4 * (m - 1) + s + 1)
                            dve.scalar_tensor_tensor(out=x[:, t, :], in0=ps[:, 4 + m % 2, s * P:(s + 1) * P],
                                                     scalar=r_w[:, t, e:e + 1], in1=x[:, t, :],
                                                     op0=ALU.mult, op1=ALU.add).then_inc(ad, 1)

                    for n in range(steps):
                        dve.wait_ge(si, n + 1)
                        dve.wait_ge(up, n + 1)
                        if n >= 4:
                            dve.wait_ge(dn, (n - 4) // 2 + 1)
                        dve.tensor_tensor(fuse[:, n % 4, :], act_g[:, n % 2, :], ps[:, 2 + n % 2, :], ALU.mult).then_inc(fu, 1)
                        if n % 2 == 1 and n >= 3:
                            add(n // 2 - 1)
                    add(steps // 2 - 1)
            end_stage("ef_gate", "ef_up", "ef_silu", "ef_fused", "ef_down", "ef_added")

        def router_second():
            mm, ch, ex = sem("rt_logits"), sem("rt_chain"), sem("rt_exp")
            lg = tiles_of(0, w=E1)
            with nc.Block() as block:
                @block.tensor
                def _(pe):
                    for t in range(TT):
                        last = pe.matmul(lg[:, t, :], xT[:, t * P:(t + 1) * P], W["n_router"][:, :], start=True, stop=True)
                    last.then_inc(mm, 1)

                @block.scalar
                def _(act):
                    act.wait_ge(mm, 1)
                    act.activation(r_a[:, :, :], lg, ACT.Exp, scale=-1.0).then_inc(ex, 1)

                @block.vector
                def _(dve):
                    dve.wait_ge(ex, 1)
                    dve.tensor_scalar(r_b[:, :, :], r_a[:, :, :], 1.0, None, ALU.add).then_inc(ch, 1)
                    dve.wait_ge(ch, 1)
                    dve.reciprocal(r_a[:, :, :], r_b[:, :, :]).then_inc(ch, 1)
                    dve.wait_ge(ch, 2)
                    dve.tensor_tensor(r_b[:, :, :], r_a[:, :, :],
                                      W["n_bias"][:, :].unsqueeze(1).broadcast_to([P, TT, E1]), ALU.add).then_inc(ch, 1)
                    dve.wait_ge(ch, 3)
                    n = ranks(dve, ch, 3, r_b[:, :, :], E1, K1)
                    dve.tensor_tensor(r_b[:, :, :], r_a[:, :, :], r_c[:, :, :], ALU.mult).then_inc(ch, 1)
                    dve.wait_ge(ch, n + 1)
                    dve.tensor_reduce(r_s[:, :], r_b[:, :, :], AX.X, ALU.add).then_inc(ch, 1)
                    dve.wait_ge(ch, n + 2)
                    dve.reciprocal(r_r[:, :], r_s[:, :]).then_inc(ch, 1)
                    dve.wait_ge(ch, n + 3)
                    dve.scalar_tensor_tensor(out=r_w[:, :, :], in0=r_b[:, :, :], scalar=ROUTE_SCALE,
                                             in1=r_r[:, :].unsqueeze(2).broadcast_to([P, TT, E1]),
                                             op0=ALU.mult, op1=ALU.mult).then_inc(ch, 1)
            end_stage("rt_logits", "rt_chain", "rt_exp")

        def experts_second():
            gt, up, si, fu, dn, ad = (sem(n) for n in ("ef_gate", "ef_up", "ef_silu", "ef_fused", "ef_down", "ef_added"))
            pairs = E1 // 2 + 1
            steps = 2 * pairs
            with nc.Block() as block:
                @block.tensor
                def _(pe):
                    def down(n):
                        k = n % pairs
                        pe.wait_ge(fu, n + 1)
                        if n >= 2:
                            pe.wait_ge(ad, n - 1)
                        for j in range(2 if k < pairs - 1 else 1):
                            for s in range(4):
                                w = W["n_down"][64 * j:64 * j + 64, k, :] if k < pairs - 1 else W["n_sdown"][:, :]
                                mm = pe.matmul(ps[:, 4 + 2 * (n % 2) + j, s * P:(s + 1) * P],
                                               fuse[64 * j:64 * j + 64, n % 2, s * P:(s + 1) * P], w,
                                               start=True, stop=True)
                        mm.then_inc(dn, 1)

                    for n in range(steps):
                        blk, k = divmod(n, pairs)
                        rows = P if k < pairs - 1 else F1
                        if n >= 2:
                            pe.wait_ge(si, n - 1)
                            pe.wait_ge(fu, n - 1)
                        for m, (w, ws) in enumerate((("n_gate", "n_sgate"), ("n_up", "n_sup"))):
                            lhs = W[w][:, k * P:(k + 1) * P] if k < pairs - 1 else W[ws][:, :]
                            pe.matmul(ps[0:rows, 2 * m + n % 2, :], lhs, xT[:, blk * HALF:(blk + 1) * HALF],
                                      start=True, stop=True).then_inc((gt, up)[m], 1)
                        if n >= 1:
                            down(n - 1)
                    down(steps - 1)

                @block.scalar
                def _(act):
                    for n in range(steps):
                        rows = P if n % pairs < pairs - 1 else F1
                        act.wait_ge(gt, n + 1)
                        if n >= 2:
                            act.wait_ge(fu, n - 1)
                        act.activation(act_g[0:rows, n % 2, :], ps[0:rows, n % 2, :], ACT.Silu).then_inc(si, 1)

                @block.vector
                def _(dve):
                    added = 0

                    def add(n):
                        nonlocal added
                        blk, k = divmod(n, pairs)
                        dve.wait_ge(dn, n + 1)
                        for j in range(2 if k < pairs - 1 else 1):
                            for s in range(4):
                                t = 4 * blk + s
                                if k or j:
                                    dve.wait_ge(sem("es_chain"), added - 3)
                                scal = r_w[:, t, 2 * k + j:2 * k + j + 1] if k < pairs - 1 else 1.0
                                ins = dve.scalar_tensor_tensor(
                                    out=x[:, t, :], in0=ps[:, 4 + 2 * (n % 2) + j, s * P:(s + 1) * P], scalar=scal,
                                    in1=x[:, t, :], op0=ALU.mult, op1=ALU.add)
                                ins.then_inc(sem("es_chain"), 1)
                                added += 1
                        dve.wait_ge(sem("es_chain"), added)
                        dve.nop().then_inc(ad, 1)

                    for n in range(steps):
                        rows = P if n % pairs < pairs - 1 else F1
                        dve.wait_ge(si, n + 1)
                        dve.wait_ge(up, n + 1)
                        if n >= 2:
                            dve.wait_ge(dn, n - 1)
                        dve.tensor_tensor(fuse[0:rows, n % 2, :], act_g[0:rows, n % 2, :], ps[0:rows, 2 + n % 2, :],
                                          ALU.mult).then_inc(fu, 1)
                        if n >= 1:
                            add(n - 1)
                    add(steps - 1)
            end_stage("ef_gate", "ef_up", "ef_silu", "ef_fused", "ef_down", "ef_added", "es_chain")

        lin_k = big[:, 0:LIN_K * S].rearrange("p (k t d) -> p k t d", k=LIN_K, d=D)
        lin_v = big[:, 2048:2048 + LIN_K * S].rearrange("p (k t d) -> p k t d", k=LIN_K, d=D)
        lin_w = big[:, 4096:4096 + 5 * P].rearrange("p (k d) -> p k d", k=5)
        state = big[:, 4736:4736 + 2 * P].rearrange("p (k d) -> p k d", k=2)

        def linear_attention():
            wi, mm, ev, st, sv, om = (sem(n) for n in ("la_weights", "la_products", "la_evacuated", "la_states", "la_state", "la_out"))
            with nc.Block() as block:
                @block.gpsimd
                def _(pool):
                    ws = [W["l_qw"][:, :]] + [W[w][:, k * D:(k + 1) * D] for w in ("l_kw", "l_vw") for k in range(LIN_K)]
                    for n, w in enumerate(ws):
                        pool.tensor_tensor(lin_w[:, n, :], w, ident[:, :], ALU.add).then_inc(wi, 1)

                @block.tensor
                def _(pe):
                    pe.wait_ge(wi, 5)
                    for k in range(2):
                        pe.matmul(ps[:, k, :], lin_w[:, 0, :], xT[:, k * HALF:(k + 1) * HALF], start=True, stop=True).then_inc(mm, 1)
                    for n in range(2 * LIN_K):
                        if n >= 3:
                            pe.wait_ge(ev, 2)
                        for t in range(TT):
                            last = pe.matmul(tiles_of(2 + 2 * (n % 3))[:, t, :], xT[:, t * P:(t + 1) * P],
                                             lin_w[:, 1 + n, :], start=True, stop=True)
                        last.then_inc(mm, 1)
                    pe.wait_ge(ev, 1 + 2 * LIN_K)
                    for k in range(LIN_K):
                        for t in range(TT):
                            last = pe.matmul(ps[:, k, 0:P], lin_k[:, k, t, :], lin_v[:, k, t, :],
                                             start=(t == 0), stop=(t == TT - 1))
                        last.then_inc(st, 1)
                    pe.wait_ge(sv, 3)
                    for t in range(TT):
                        last = pe.matmul(tiles_of(2)[:, t, :], qT[:, 0, t * P:(t + 1) * P], state[:, 0, :], start=True, stop=True)
                    last.then_inc(mm, 1)

                @block.vector
                def _(dve):
                    dve.wait_ge(mm, 2)
                    dve.tensor_scalar(qT[:, 0, :].rearrange("p (k c) -> p k c", k=2), ps[:, 0:2, :], W["l_qb"][:, 0:1], None,
                                      ALU.add).then_inc(ev, 1)
                    for n in range(2 * LIN_K):
                        dst, b = ((lin_k, "l_kb"), (lin_v, "l_vb"))[n // LIN_K]
                        k = n % LIN_K
                        dve.wait_ge(mm, 3 + n)
                        dve.tensor_tensor(dst[:, k, :, :], tiles_of(2 + 2 * (n % 3)),
                                          W[b][:, k * D:(k + 1) * D].unsqueeze(1).broadcast_to([P, TT, D]), ALU.add).then_inc(ev, 1)
                    dve.wait_ge(st, 1)
                    dve.scalar_tensor_tensor(out=state[:, 0, :], in0=ps[:, 0, 0:P], scalar=1.0 / (LIN_N * LIN_N),
                                             in1=block_mask[:, :], op0=ALU.mult, op1=ALU.mult).then_inc(sv, 1)
                    dve.wait_ge(st, 2)
                    dve.tensor_copy(state[:, 1, :], ps[:, 1, 0:P]).then_inc(sv, 1)
                    dve.wait_ge(sv, 2)
                    dve.tensor_tensor(state[:, 0, :], state[:, 0, :], state[:, 1, :], ALU.mult).then_inc(sv, 1)
                    dve.wait_ge(mm, 3 + 2 * LIN_K)
                    dve.tensor_copy(o_rows[:, :, 0:D], tiles_of(2)).then_inc(om, 1)
            end_stage("la_weights", "la_products", "la_evacuated", "la_states", "la_state", "la_out")

        def affine_xT(gain, bias):
            with nc.Block() as block:
                @block.vector
                def _(dve):
                    if bias is None:
                        dve.tensor_scalar(xT[:, :], xT[:, :], gain, None, ALU.mult).then_inc(sem("af_done"), 1)
                    else:
                        dve.tensor_scalar(xT[:, :], xT[:, :], gain, bias, ALU.mult, ALU.add).then_inc(sem("af_done"), 1)
            end_stage("af_done")

        with nc.Block() as block:
            @block.sync
            def _(sp):
                const = {"ident": ident, "head_mask": head_mask, "pair_mask": pair_mask, "block_mask": block_mask,
                         "tri": tri}
                for n, t in const.items():
                    dims = (slice(None),) * len(t.shape)
                    sp.dma_start(t[dims], A[n]).then_inc(sem("weights_in"), 16)
                for n in resident:
                    dims = (slice(None),) * len(W[n].shape)
                    sp.dma_start(W[n][dims], A[n]).then_inc(sem("weights_in"), 16)
                sp.wait_ge(sem("weights_in"), 16 * (len(const) + len(resident)))

            @block.gpsimd
            def _(pool):
                pool.memset(half_neg[:, :], -0.5).then_inc(sem("half_set"), 1)
        end_stage("weights_in", "half_set")

        with nc.Fori(0, B) as b:
            with nc.Block() as block:
                @block.sync
                def _(sp):
                    sp.dma_start(x[:, :, :], x_in[b]).then_inc(sem("x_in"), 16)
                    sp.wait_ge(sem("x_in"), 16)
            end_stage("x_in")

            layer_norm(x, xn)
            lif_projections()
            with nc.Fori(0, GROUPS) as g:
                lif_heads(g)
                narrow_post(g)
            transposed_rows(1)
            rows_out([qT[:, 0, :]], [W["a_ow"][:, :]], W["a_ob"])
            layer_norm(x, xn)
            router_first()
            experts_first()
            layer_norm(x, xn)
            layer_norm(xn, xn)
            affine_xT(W["b_gamma"][:, 0:1], None)
            with nc.Fori(0, GROUPS) as g:
                wide_projections(g)
                softmax_heads(
                    g, S + 1, lambda hh: qT[:, hh // 2, :], lambda hh: kT[:, hh // 2, :],
                    lambda hh: pair_mask[:, hh % 2:hh % 2 + 1], lambda hh: bn_k[:, hh // 2:hh // 2 + 1],
                    lambda eng, hh: eng.tensor_copy(v_head[:, hh % 2, :, :], v_rows[:, :, hh * WH:(hh + 1) * WH]),
                    wide_pv, 6, HALF)
                wide_post(g)
                transposed_rows(2)
                rows_out([qT[:, 0, :], qT[:, 1, :]], [bo_w[:, 0, :], bo_w[:, 1, :]], None)
            layer_norm(x, xn)
            router_first()
            experts_first()
            layer_norm(x, xn)
            rope_projections()
            with nc.Fori(0, GROUPS) as g:
                softmax_heads(
                    g, S, lambda hh: qT[:, 0, :], lambda hh: kT[:, 0, :],
                    lambda hh: head_mask[:, bass.ds(g * GH + hh, 1)], None,
                    lambda eng, hh: narrow_value_head(eng, g, hh), narrow_pv, 6, 256)
                scaled_post(g)
            transposed_rows(1)
            rows_out([qT[:, 0, :]], [W["c_ow"][:, :]], W["c_ob"])
            layer_norm(x, xn)
            router_second()
            experts_second()
            layer_norm(x, xn)
            linear_attention()
            layer_norm(o_rows[:, :, 0:D], xn)
            affine_xT(W["l_g"][:, 0:1], W["l_b"][:, 0:1])
            rows_out([xT[:, :]], [W["l_ow"][:, :]], W["l_ob"])
            layer_norm(x, xn)
            router_second()
            experts_second()

            with nc.Block() as block:
                @block.sync
                def _(sp):
                    sp.dma_start(x_out[b], x[:, :, :]).then_inc(sem("x_out"), 16)
                    sp.wait_ge(sem("x_out"), 16)
            end_stage("x_out")




def _constants(np):
    inv_freq = (np.float32(1.0) / np.float32(10000.0) ** (np.arange(0, DH, 2, dtype=np.float32) / np.float32(DH))).astype(np.float32)
    freqs = np.arange(S, dtype=np.float32)[:, None] * inv_freq[None, :]
    cos = np.repeat(np.cos(freqs), 2, axis=-1).T.astype(np.float32)
    sin = np.repeat(np.sin(freqs), 2, axis=-1).T.astype(np.float32)
    sign = np.where(np.arange(DH) < DH // 2, -1.0, 1.0).astype(np.float32)[:, None]
    rows = np.arange(P)
    return {
        "ident": np.eye(P, dtype=np.float32),
        "head_mask": (rows[:, None] // DH == np.arange(NH)[None, :]).astype(np.float32),
        "pair_mask": (rows[:, None] // WH == np.arange(2)[None, :]).astype(np.float32),
        "block_mask": (rows[:, None] // DH == rows[None, :] // DH).astype(np.float32),
        "cos": np.tile(cos, (NH, 1)),
        "sin": np.tile(sin * sign, (NH, 1)),
        "tri": np.broadcast_to(np.tril(np.ones((E1, E1), np.float32), -1), (P, E1, E1)).copy(),
    }


def _layout(np, i):
    col = lambda v: v.reshape(P, 1)
    rows = lambda v: np.broadcast_to(v.reshape(1, -1), (P, v.size))
    d = np.arange(D)
    rot = (d // DH) * DH + (d % DH + DH // 2) % DH
    a = {"x": i["L0_attn_a_x"]}
    for k in "qkvo":
        a[f"a_{k}w"] = i[f"L0_attn_a_{k}_w"]
    a["a_qb"], a["a_kb"] = col(i["L0_attn_a_q_b"]), col(i["L0_attn_a_k_b"])
    a["a_vb"], a["a_ob"] = rows(i["L0_attn_a_v_b"]), rows(i["L0_attn_a_o_b"])
    a["m_router"] = i["L0_ffn_router_kernel_DE"]
    a["m_gate"] = i["L0_ffn_kernel_gating_EDF"].transpose(1, 0, 2).reshape(D, E0 * F0)
    a["m_up"] = i["L0_ffn_kernel_up_EDF"].transpose(1, 0, 2).reshape(D, E0 * F0)
    a["m_down"] = i["L0_ffn_kernel_down_EFD"].reshape(E0 * F0 // P, P, D).transpose(1, 0, 2)
    a["b_gamma"] = col(i["L0_attn_b_gamma"])
    a["b_qw"], a["b_kvw"] = i["L0_attn_b_w_q"], i["L0_attn_b_w_kv"]
    a["b_ow"] = i["L0_attn_b_w_out"].reshape(NH // 2, P, D).transpose(1, 0, 2)
    a["b_nk"] = i["L0_attn_b_null_kv"][0].reshape(NH // 2, P).T
    a["b_nv"] = rows(i["L0_attn_b_null_kv"][1].reshape(-1))
    for k in "qkvo":
        a[f"c_{k}w"] = i[f"L1_attn_a_w{k}"].T
    a["c_qrw"], a["c_krw"] = i["L1_attn_a_wq"].T[:, rot], i["L1_attn_a_wk"].T[:, rot]
    a["c_qb"], a["c_kb"] = col(i["L1_attn_a_bq"]), col(i["L1_attn_a_bk"])
    a["c_qrb"], a["c_krb"] = col(i["L1_attn_a_bq"][rot]), col(i["L1_attn_a_bk"][rot])
    a["c_vb"], a["c_ob"] = rows(i["L1_attn_a_bv"]), rows(i["L1_attn_a_bo"])
    a["l_qw"], a["l_ow"] = i["L1_attn_b_Wq"], i["L1_attn_b_Wo"]
    a["l_kw"] = i["L1_attn_b_Wk"].transpose(1, 0, 2).reshape(D, LIN_K * D)
    a["l_vw"] = i["L1_attn_b_Wv"].transpose(1, 0, 2).reshape(D, LIN_K * D)
    a["l_qb"] = col(i["L1_attn_b_bq"])
    a["l_kb"], a["l_vb"], a["l_ob"] = rows(i["L1_attn_b_bk"]), rows(i["L1_attn_b_bv"]), rows(i["L1_attn_b_bo"])
    a["l_g"], a["l_b"] = col(i["L1_attn_b_ln_g"]), col(i["L1_attn_b_ln_b"])
    a["n_router"], a["n_bias"] = i["L1_ffn_gate_w"].T, rows(i["L1_ffn_gate_b"])
    w13 = i["L1_ffn_w13"].transpose(2, 0, 1)
    a["n_gate"], a["n_up"] = w13[:, :, :F1].reshape(D, E1 * F1), w13[:, :, F1:].reshape(D, E1 * F1)
    a["n_down"] = i["L1_ffn_w2"].transpose(0, 2, 1).reshape(E1 // 2, P, D).transpose(1, 0, 2)
    a["n_sgate"], a["n_sup"] = i["L1_ffn_w13_s"].T[:, :F1], i["L1_ffn_w13_s"].T[:, F1:]
    a["n_sdown"] = i["L1_ffn_w2_s"].T
    return a


def kernel(**inputs):
    import numpy as np
    import concourse.bacc as bacc
    from concourse.bass_utils import run_bass_kernel_spmd

    nc = bacc.Bacc("TRN2", target_bir_lowering=False, num_devices=1)
    given = {n: np.asarray(v) for n, v in inputs.items()}
    laid = {**_layout(np, given), **_constants(np)}
    arrays = {f"in_{n}": np.ascontiguousarray(v) for n, v in laid.items()}
    aps = {n: nc.dram_tensor(f"in_{n}", arrays[f"in_{n}"].shape, mybir.dt.from_np(arrays[f"in_{n}"].dtype),
                             kind="ExternalInput").ap() for n in laid}
    out = nc.dram_tensor("out", (B, S, D), F32, kind="ExternalOutput").ap()
    hybrid_kernel(nc, aps, out)
    r = run_bass_kernel_spmd(nc, [arrays], core_ids=[0])
    return r.results[0]["out"]
```

```python
from contextlib import ExitStack

import concourse.bass as bass
from concourse import mybir

F32 = mybir.dt.float32
BF16 = mybir.dt.bfloat16
ALU = mybir.AluOpType
ACT = mybir.ActivationFunctionType
AX = mybir.AxisListType

P = 128
B, S, D = 4, 1024, 128
TT = S // P
HALF = 512
NH = 16
DH = D // NH
WH = 64
GH = 4
GROUPS = NH // GH
E0, F0, K0 = 8, 256, 2
E1, F1, K1 = 16, 64, 4
ROUTE_SCALE = 2.5
BETA, THR, SPIKE_STEPS = 0.95, 1.0, 4
EPS = 1e-5
LIN_N = 512
LIN_K = 2


def hybrid_kernel(nc, A, out):
    ctx = ExitStack()
    with ctx:
        def sb(name, shape, dt=F32):
            return ctx.enter_context(nc.sbuf_tensor(name, shape, dt))

        sems = {}

        def sem(name):
            if name not in sems:
                sems[name] = ctx.enter_context(nc.semaphore(name))
            return sems[name]

        def end_stage(*names):
            nc.all_engine_barrier()
            for name in names:
                nc.sync.sem_clear(sem(name))
            nc.all_engine_barrier()

        ps = ctx.enter_context(nc.psum_tensor("ps", [P, 8, HALF], F32))

        ident = sb("ident", [P, P])
        head_mask = sb("head_mask", [P, NH])
        pair_mask = sb("pair_mask", [P, 2])
        block_mask = sb("block_mask", [P, P])
        tri = sb("tri", [P, E1, E1])
        half_neg = sb("half_neg", [P, TT])
        W = {}
        resident = ["a_qw", "a_kw", "a_vw", "a_ow", "a_qb", "a_kb", "a_vb", "a_ob",
                    "m_router", "m_gate", "m_up", "m_down", "b_gamma",
                    "c_qw", "c_kw", "c_qrw", "c_krw", "c_vw", "c_ow", "c_qb", "c_kb", "c_qrb", "c_krb", "c_vb", "c_ob",
                    "l_qw", "l_kw", "l_vw", "l_ow", "l_qb", "l_kb", "l_vb", "l_ob", "l_g", "l_b",
                    "n_router", "n_bias", "n_gate", "n_up", "n_down", "n_sgate", "n_sup", "n_sdown"]
        for n in resident:
            W[n] = sb("w_" + n, list(A[n].shape))

        x = sb("x", [P, TT, D])
        xn = sb("xn", [P, TT, D])
        xT = sb("xT", [P, S])
        stats = sb("stats", [P, TT, 6])
        meanvar = sb("meanvar", [P, TT, 2])
        rstd = sb("rstd", [P, TT])
        qT = sb("qT", [P, 2, S])
        kT = sb("kT", [P, 2, S])
        v_rows = sb("v_rows", [P, TT, 256])
        q_head = sb("q_head", [P, 2, S])
        q_head_bf = sb("q_head_bf", [P, 2, S], BF16)
        v_head = sb("v_head", [P, 2, TT, 32])
        row_rec = sb("row_rec", [P, GH, TT])
        BIG = 24064
        big = sb("big", [P, BIG])
        probsT = big[:, 0:2 * TT * S].rearrange("p (a t s) -> p a t s", a=2, t=TT)
        outT = big[:, 2 * TT * S:2 * TT * S + GH * HALF].rearrange("p (h c) -> p h c", h=GH)
        o_rows = big[:, 20480:20480 + TT * 256].rearrange("p (t c) -> p t c", c=256)
        counts = big[:, 22528:22528 + S].bitcast(BF16).rearrange("p (n c) -> p n c", c=S)
        qc, kc = counts[:, 0, :], counts[:, 1, :]
        lifm, lift = q_head[:, 0, :], q_head[:, 1, :]
        o_tmp = q_head[:, :, :].rearrange("p a (t c) -> p (a t) c", c=256)
        r_s = sb("r_s", [P, TT])
        r_r = sb("r_r", [P, TT])
        r_cmp = big[:, 0:TT * E1 * E1]
        r_eq = big[:, TT * E1 * E1:2 * TT * E1 * E1]
        act_g = big[:, 4096:4096 + 2 * HALF].rearrange("p (a n) -> p a n", a=2)
        fuse = big[:, 5120:5120 + 4 * HALF].rearrange("p (a n) -> p a n", a=4)
        r_a, r_b, r_c, r_w = (big[:, 10240 + k * P:10240 + (k + 1) * P].rearrange("p (t e) -> p t e", e=E1) for k in range(4))
        cos_t, sin_t = q_head[:, 0, :], q_head[:, 1, :]

        x_in = A["x"].rearrange("b (t p) d -> b p t d", p=P)
        x_out = out.rearrange("b (t p) d -> b p t d", p=P)

        def tiles_of(bank, n=TT, w=P):
            per = HALF // w
            k = -(-n // per)
            return ps[:, bank:bank + k, :].rearrange("p k (t w) -> p (k t) w", w=w)[:, 0:n, :]

        def layer_norm(src, dst):
            st, mv, pw, nd, tp, ev = (sem(n) for n in ("ln_stats", "ln_meanvar", "ln_pow", "ln_rows", "ln_transposed", "ln_evacuated"))
            with nc.Block() as block:
                @block.vector
                def _(dve):
                    for t in range(TT):
                        dve.bn_stats(stats[:, t, :], src[:, t, :]).then_inc(st, 1)
                    dve.wait_ge(st, TT)
                    for t in range(TT):
                        dve.bn_aggr(meanvar[:, t, :], stats[:, t, :]).then_inc(mv, 1)
                    dve.wait_ge(mv, TT)
                    dve.tensor_scalar(rstd[:, :], meanvar[:, :, 1], EPS, None, ALU.add).then_inc(mv, 1)
                    dve.wait_ge(pw, 1)
                    for t in range(TT):
                        dve.tensor_scalar(dst[:, t, :], src[:, t, :], meanvar[:, t, 0:1], rstd[:, t:t + 1],
                                          ALU.subtract, ALU.mult).then_inc(nd, 1)

                @block.gpsimd
                def _(pool):
                    pool.wait_ge(mv, TT + 1)
                    pool.tensor_tensor(rstd[:, :], rstd[:, :], half_neg[:, :], ALU.pow).then_inc(pw, 1)

                @block.tensor
                def _(pe):
                    for t in range(TT):
                        pe.wait_ge(nd, t + 1)
                        pe.transpose(tiles_of(0)[:, t, :], dst[:, t, :], ident[:, :]).then_inc(tp, 1)

                @block.scalar
                def _(act):
                    for k in range(2):
                        act.wait_ge(tp, 4 * k + 4)
                        act.activation(xT[:, k * HALF:(k + 1) * HALF], ps[:, k, :], ACT.Copy).then_inc(ev, 1)
            end_stage("ln_stats", "ln_meanvar", "ln_pow", "ln_rows", "ln_transposed", "ln_evacuated")

        def rows_out(srcT, weights, bias_rows, first_bank=2):
            done, added = sem("ro_done"), sem("ro_added")
            with nc.Block() as block:
                @block.tensor
                def _(pe):
                    for t in range(TT):
                        for n, (s, w) in enumerate(zip(srcT, weights)):
                            mm = pe.matmul(tiles_of(first_bank)[:, t, :], s[:, t * P:(t + 1) * P], w,
                                           start=(n == 0), stop=(n == len(srcT) - 1))
                        mm.then_inc(done, 1)

                @block.vector
                def _(dve):
                    if bias_rows is not None:
                        dve.tensor_tensor(x[:, :, :], x[:, :, :],
                                          bias_rows[:, :].unsqueeze(1).broadcast_to([P, TT, D]), ALU.add).then_inc(added, 1)
                        dve.wait_ge(added, 1)
                    dve.wait_ge(done, TT)
                    dve.tensor_tensor(x[:, :, :], x[:, :, :], tiles_of(first_bank), ALU.add).then_inc(added, 1)
            end_stage("ro_done", "ro_added")

        def lif_projections():
            mm, cur, ch = sem("lp_products"), sem("lp_current"), sem("lp_chain")
            with nc.Block() as block:
                @block.tensor
                def _(pe):
                    for n, w in enumerate(("a_qw", "a_kw")):
                        for k in range(2):
                            pe.matmul(ps[:, 2 * n + k, :], W[w][:, :], xT[:, k * HALF:(k + 1) * HALF],
                                      start=True, stop=True).then_inc(mm, 1)
                    for t in range(TT):
                        pe.matmul(tiles_of(4)[:, t, :], xT[:, t * P:(t + 1) * P], W["a_vw"][:, :],
                                  start=True, stop=True).then_inc(mm, 1)

                @block.scalar
                def _(act):
                    for n, b in enumerate(("a_qb", "a_kb")):
                        act.wait_ge(mm, 2 * n + 2)
                        act.activation(qT[:, n, :].rearrange("p (k c) -> p k c", k=2), ps[:, 2 * n:2 * n + 2, :],
                                       ACT.Identity, bias=W[b][:, 0:1]).then_inc(cur, 1)

                @block.vector
                def _(dve):
                    n_chain = 0

                    def chained(ins):
                        nonlocal n_chain
                        n_chain += 1
                        ins.then_inc(ch, 1)
                        dve.wait_ge(ch, n_chain)

                    def neurons(c, counts):
                        mem, nxt = lifm, lift
                        chained(dve.tensor_scalar(mem, c, BETA, None, ALU.mult))
                        chained(dve.tensor_tensor(nxt, mem, c, ALU.add))
                        chained(dve.scalar_tensor_tensor(out=mem, in0=c, scalar=THR, in1=nxt, op0=ALU.is_gt,
                                                         op1=ALU.subtract, reverse1=True))
                        chained(dve.tensor_scalar(counts, c, THR, None, ALU.is_gt))
                        for step in range(2, SPIKE_STEPS + 1):
                            chained(dve.scalar_tensor_tensor(out=counts, in0=mem, scalar=THR, in1=counts,
                                                             op0=ALU.is_gt, op1=ALU.add))
                            if step < SPIKE_STEPS:
                                chained(dve.scalar_tensor_tensor(out=nxt, in0=mem, scalar=BETA, in1=c,
                                                                 op0=ALU.mult, op1=ALU.add))
                                chained(dve.scalar_tensor_tensor(out=mem, in0=mem, scalar=THR, in1=nxt,
                                                                 op0=ALU.is_gt, op1=ALU.subtract, reverse1=True))

                    dve.wait_ge(cur, 1)
                    neurons(qT[:, 0, :], qc)
                    dve.wait_ge(cur, 2)
                    neurons(qT[:, 1, :], kc)
                    dve.wait_ge(mm, 4 + TT)
                    chained(dve.tensor_tensor(kT[:, 0, :].rearrange("p (t d) -> p t d", d=D), tiles_of(4),
                                              W["a_vb"][:, :].unsqueeze(1).broadcast_to([P, TT, D]), ALU.add))
                    neurons(kT[:, 0, :], kT[:, 1, :])
                    chained(dve.tensor_copy(v_rows[:, :, 0:D], kT[:, 1, :].rearrange("p (t d) -> p t d", d=D)))
            end_stage("lp_products", "lp_current", "lp_chain")

        def narrow_value_head(eng, g, hh):
            return eng.tensor_copy(v_head[:, hh % 2, :, 0:DH], v_rows[:, :, bass.ds(g * (GH * DH) + hh * DH, DH)])

        def narrow_pv(pe, hh, kt):
            for c in range(4):
                mm = pe.matmul(ps[32 * c:32 * c + 32, 6, 0:256], v_head[:, hh % 2, kt, 0:32],
                               probsT[:, hh % 2, kt, 256 * c:256 * c + 256], start=(kt == 0), stop=(kt == TT - 1))
            return mm

        def narrow_post(g):
            tp, ch = sem("np_transposed"), sem("np_chain")
            with nc.Block() as block:
                @block.tensor
                def _(pe):
                    for hh in range(GH):
                        for j in range(2):
                            pe.transpose(tiles_of(0)[:, 2 * hh + j, :], outT[:, hh, j * P:(j + 1) * P],
                                         ident[:, :]).then_inc(tp, 1)

                @block.vector
                def _(dve):
                    for hh in range(GH):
                        dve.wait_ge(tp, 4 * (hh // 2) + 4)
                        part = tiles_of(0)[:, 2 * hh:2 * hh + 2, :].rearrange("p j (c w) -> p c j w", w=32)
                        rec = row_rec[:, hh, :].rearrange("p (c j) -> p c j", j=2)
                        dve.reciprocal(rec, part[:, :, :, DH]).then_inc(ch, 1)
                        dve.wait_ge(ch, 2 * hh + 1)
                        dst = o_rows[:, :, bass.ds(g * (GH * DH) + hh * DH, DH)].rearrange("p (c j) w -> p c j w", j=2)
                        dve.tensor_tensor(dst, part[:, :, :, 0:DH], rec.unsqueeze(3).broadcast_to([P, 4, 2, DH]),
                                          ALU.mult).then_inc(ch, 1)
            end_stage("np_transposed", "np_chain")

        def lif_heads(g):
            qh, vh, sc, ex, pv, oe = (sem(n) for n in ("lh_query", "lh_value", "lh_scores", "lh_exp", "lh_sums", "lh_out"))
            scale = 1.0 / (SPIKE_STEPS * SPIKE_STEPS) / float(DH) ** 0.5
            with nc.Block() as block:
                @block.vector
                def _(dve):
                    for hh in range(GH + 1):
                        if hh < GH:
                            if hh >= 2:
                                dve.wait_ge(sc, TT * (hh - 1))
                            dve.tensor_scalar(q_head_bf[:, hh % 2, :], qc, head_mask[:, bass.ds(g * GH + hh, 1)],
                                              None, ALU.mult).then_inc(qh, 1)
                        if hh >= 1:
                            dve.wait_ge(pv, hh)
                            dve.tensor_copy(outT[:, hh - 1, 0:256], ps[:, 6, 0:256]).then_inc(oe, 1)

                @block.gpsimd
                def _(pool):
                    for hh in range(GH):
                        if hh < 2:
                            pool.memset(v_head[:, hh, :, DH:32], 0.0).then_inc(vh, 1)
                            pool.wait_ge(vh, 3 * hh + 1)
                            pool.memset(v_head[:, hh, :, DH:DH + 1], float(SPIKE_STEPS)).then_inc(vh, 1)
                        else:
                            pool.wait_ge(pv, hh - 1)
                        narrow_value_head(pool, g, hh).then_inc(vh, 1)

                @block.tensor
                def _(pe):
                    def sums(hh, kt):
                        if kt == 0:
                            pe.wait_ge(vh, 3 * min(hh + 1, 2) + max(hh - 1, 0))
                            if hh >= 1:
                                pe.wait_ge(oe, hh)
                        pe.wait_ge(ex, TT * hh + kt + 1)
                        mm = narrow_pv(pe, hh, kt)
                        if kt == TT - 1:
                            mm.then_inc(pv, 1)

                    for hh in range(GH):
                        pe.wait_ge(qh, hh + 1)
                        for kt in range(TT):
                            u = TT * hh + kt
                            if u >= 2:
                                pe.wait_ge(ex, u - 1)
                            for k in range(2):
                                mm = pe.matmul(ps[:, 2 * (u % 2) + k, :], kc[:, kt * P:(kt + 1) * P],
                                               q_head_bf[:, hh % 2, k * HALF:(k + 1) * HALF], start=True, stop=True)
                            mm.then_inc(sc, 1)
                            if hh >= 1:
                                sums(hh - 1, kt)
                    for kt in range(TT):
                        sums(GH - 1, kt)

                @block.scalar
                def _(act):
                    for hh in range(GH):
                        if hh >= 2:
                            act.wait_ge(pv, hh - 1)
                        for kt in range(TT):
                            u = TT * hh + kt
                            act.wait_ge(sc, u + 1)
                            act.activation(probsT[:, hh % 2, kt, :].rearrange("p (k c) -> p k c", k=2),
                                           ps[:, 2 * (u % 2):2 * (u % 2) + 2, :], ACT.Exp, scale=scale).then_inc(ex, 1)
            end_stage("lh_query", "lh_value", "lh_scores", "lh_exp", "lh_sums", "lh_out")

        def rope_projections():
            mm, ra, ro = sem("rp_products"), sem("rp_parts"), sem("rp_done")
            scale = float(DH) ** -0.5
            todo = (("c_qw", "c_qb", "c_qrw", "c_qrb", qT), ("c_kw", "c_kb", "c_krw", "c_krb", kT))
            with nc.Block() as block:
                @block.sync
                def _(sp):
                    sp.dma_start(cos_t, A["cos"]).then_inc(sem("rp_tables"), 16)
                    sp.dma_start(sin_t, A["sin"]).then_inc(sem("rp_tables"), 16)

                @block.tensor
                def _(pe):
                    for n, (w, _, wr, _, _) in enumerate(todo):
                        if n:
                            pe.wait_ge(ra, 2)
                        for m, ww in enumerate((w, wr)):
                            for k in range(2):
                                pe.matmul(ps[:, 2 * m + k, :], W[ww][:, :], xT[:, k * HALF:(k + 1) * HALF],
                                          start=True, stop=True).then_inc(mm, 1)
                    for t in range(TT):
                        pe.matmul(tiles_of(4)[:, t, :], xT[:, t * P:(t + 1) * P], W["c_vw"][:, :],
                                  start=True, stop=True).then_inc(mm, 1)

                @block.vector
                def _(dve):
                    dve.wait_ge(sem("rp_tables"), 32)
                    for n, (_, b, _, br, dst) in enumerate(todo):
                        for m, (bb, table) in enumerate(((b, cos_t), (br, sin_t))):
                            dve.wait_ge(mm, 4 * n + 2 * m + 2)
                            dve.scalar_tensor_tensor(out=dst[:, m, :].rearrange("p (k c) -> p k c", k=2),
                                                     in0=ps[:, 2 * m:2 * m + 2, :], scalar=W[bb][:, 0:1],
                                                     in1=table.rearrange("p (k c) -> p k c", k=2),
                                                     op0=ALU.add, op1=ALU.mult).then_inc(ra, 1)
                        dve.wait_ge(ra, 2 * n + 2)
                        dve.tensor_tensor(dst[:, 0, :], dst[:, 0, :], dst[:, 1, :], ALU.add).then_inc(ro, 1)
                    dve.wait_ge(ro, 1)
                    dve.tensor_scalar(qT[:, 0, :], qT[:, 0, :], scale, None, ALU.mult).then_inc(ro, 1)
                    dve.wait_ge(mm, 8 + TT)
                    dve.tensor_tensor(v_rows[:, :, 0:D], tiles_of(4),
                                      W["c_vb"][:, :].unsqueeze(1).broadcast_to([P, TT, D]), ALU.add).then_inc(ro, 1)

                @block.gpsimd
                def _(pool):
                    for hh in range(2):
                        pool.memset(v_head[:, hh, :, DH:32], 0.0).then_inc(ro, 1)
            end_stage("rp_products", "rp_parts", "rp_done", "rp_tables")

        def transposed_rows(n_blocks):
            tp, ev = sem("tr_transposed"), sem("tr_evacuated")
            with nc.Block() as block:
                @block.tensor
                def _(pe):
                    for c in range(n_blocks):
                        for t in range(TT):
                            pe.transpose(tiles_of(2 * c)[:, t, :], o_rows[:, t, c * P:(c + 1) * P],
                                         ident[:, :]).then_inc(tp, 1)

                @block.scalar
                def _(act):
                    for c in range(n_blocks):
                        for k in range(2):
                            act.wait_ge(tp, TT * c + 4 * k + 4)
                            act.activation(qT[:, c, k * HALF:(k + 1) * HALF], ps[:, 2 * c + k, :], ACT.Copy).then_inc(ev, 1)
            end_stage("tr_transposed", "tr_evacuated")

        Q_PARTS = (0, 1, 0, 1, 2, 0)
        K_PARTS = (0, 0, 1, 1, 0, 2)
        PROD = len(Q_PARTS)
        SHIFT = 64
        HB = 4
        RING = 4
        AHEAD = TT + 3
        q_scratch = nc.dram_tensor("q_scratch", [NH, PROD, DH, S], BF16, kind="Internal").ap()
        k_scratch = nc.dram_tensor("k_scratch", [NH, PROD, DH, S], BF16, kind="Internal").ap()
        parts = big[:, 4096:4096 + 3072].bitcast(BF16).rearrange("p (n c) -> p n c", c=S)
        rest = big[:, 7168:7168 + 1024]
        q_ops = big[:, 8192:8192 + 2048].bitcast(BF16).rearrange("p (n c) -> p n c", c=S)
        k_ops = big[:, 10240:10240 + 2048].bitcast(BF16).rearrange("p (n c) -> p n c", c=S)
        ring = big[:, 12288:12288 + RING * S].rearrange("p (n c) -> p n c", c=S)
        w_ops = big[:, 16384:16384 + 7680].bitcast(BF16).rearrange("p (n c) -> p n c", c=S)
        wideT = big[:, 0:NH * HALF].rearrange("p (h c) -> p h c", c=HALF)
        w_parts = big[:, 8192:8192 + 3072].bitcast(BF16).rearrange("p (n c) -> p n c", c=S)
        rest2 = big[:, 11264:12288].rearrange("p (n c) -> p n c", c=HALF)
        v_pair = v_rows[:, :, :].rearrange("p t c -> p (t c)").rearrange("p (a t c) -> p a t c", a=2, c=P)
        key_acc, shift_rows = kT, q_head_bf
        half_max = sb("half_max", [P, 2, TT, 2])
        max_bf = sb("max_bf", [P, 2, TT], BF16)
        shift_z = sb("shift_z", [P, 2, TT, TT], BF16)
        eye8 = sb("eye8", [P, TT, TT])
        ident_bf = sb("ident_bf", [P, P], BF16)
        v_wide = big[:, 0:NH * TT * 32].rearrange("p (h t w) -> p h t w", h=NH, w=32)
        outT_all = big[:, 4096:4096 + NH * 256].rearrange("p (h c) -> p h c", c=256)

        def split_parts():
            ch, st, zo = sem("sp_chain"), sem("sp_stored"), sem("sp_set")
            with nc.Block() as block:
                @block.vector
                def _(dve):
                    for n, src in enumerate((qT, kT)):
                        a, c = src[:, 0, :], 6 * n
                        p1, p2, p3 = (parts[:, 3 * n + k, :] for k in range(3))
                        dve.tensor_copy(p1, a).then_inc(ch, 1)
                        dve.wait_ge(ch, c + 1)
                        dve.tensor_tensor(rest, a, p1, ALU.subtract).then_inc(ch, 1)
                        dve.wait_ge(ch, c + 2)
                        dve.tensor_copy(p2, rest).then_inc(ch, 1)
                        dve.wait_ge(ch, c + 3)
                        dve.tensor_tensor(p3, rest, p2, ALU.subtract).then_inc(ch, 1)
                        dve.wait_ge(ch, c + 4)
                        dve.nop().then_inc(ch, 2)
                    dve.tensor_copy(v_wide[:, :, :, 0:DH].rearrange("p h t d -> p t h d"),
                                    v_rows[:, :, 0:D].rearrange("p t (h d) -> p t h d", d=DH)).then_inc(zo, 1)

                @block.gpsimd
                def _(pool):
                    pool.memset(q_ops, 0.0).then_inc(zo, 1)
                    pool.memset(k_ops, 0.0).then_inc(zo, 1)
                    pool.memset(v_wide[:, :, :, DH:32], 0.0).then_inc(sem("sp_pool"), 1)
                    pool.wait_ge(sem("sp_pool"), 1)
                    pool.memset(v_wide[:, :, :, DH:DH + 1], 1.0).then_inc(zo, 1)
                    pool.wait_ge(zo, 4)
                    pool.memset(k_ops[SHIFT:SHIFT + TT, :, :], 1.0).then_inc(zo, 1)

                @block.sync
                def _(sp):
                    n = 0
                    for side, order, scratch in ((0, Q_PARTS, q_scratch), (1, K_PARTS, k_scratch)):
                        for r, part in enumerate(order):
                            sp.wait_ge(ch, 6 * side + (1, 3, 4)[part])
                            sp.dma_start(scratch[:, r, :, :].rearrange("h d c -> h d c"),
                                         parts[:, 3 * side + part, :]).then_inc(st, 16)
                            n += 1
                    sp.wait_ge(st, 16 * n)
            end_stage("sp_chain", "sp_stored", "sp_set", "sp_pool")

        def rotary_heads():
            names = ("ra_loaded_q", "ra_loaded_k", "ra_first", "ra_max", "ra_combined", "ra_shift", "ra_turned", "ra_shifted",
                     "ra_scores", "ra_exp", "ra_sums", "ra_out")
            lq, lk, fs, mx, cb, zs, tn, sh, sc, ex, pv, oe = (sem(n) for n in names)
            units = NH * TT
            turned = ps[SHIFT:SHIFT + TT, 7, :].bitcast(BF16)

            with nc.Block() as block:
                @block.sync
                def _(sp):
                    for h in range(NH):
                        if h >= HB:
                            sp.wait_ge(sc, TT * (h - HB + 1))
                        sp.dma_start(q_ops[0:PROD * DH, h % HB, :], q_scratch[h].rearrange("r d c -> (r d) c")).then_inc(lq, 16)
                        sp.dma_start(k_ops[0:PROD * DH, h % HB, :], k_scratch[h].rearrange("r d c -> (r d) c")).then_inc(lk, 16)
                        sp.wait_ge(lq, 16 * (h + 1))
                        sp.wait_ge(lk, 16 * (h + 1))
                        sp.nop().then_inc(sem("ra_loaded"), 1)

                @block.tensor
                def _(pe):
                    def first_scores(m, half):
                        h, qt = divmod(m, TT)
                        if qt == 0 and half == 0:
                            pe.wait_ge(sem("ra_loaded"), h + 1)
                            if h >= HB:
                                pe.wait_ge(sem("ra_cleared"), h - HB + 1)
                        if m >= 1:
                            pe.wait_ge(mx, 2 * (m - 1) + half + 1)
                        pe.matmul(ps[:, half, :], q_ops[:, h % HB, qt * P:(qt + 1) * P],
                                  k_ops[:, h % HB, half * HALF:(half + 1) * HALF], start=True, stop=True).then_inc(fs, 1)

                    def turn(h):
                        pe.wait_ge(zs, h + 1)
                        for t in range(TT):
                            mm = pe.transpose(turned[:, t * P:(t + 1) * P], shift_z[:, h % 2, t, :], ident_bf[:, :])
                        mm.then_inc(tn, 1)

                    def sums(n):
                        h, kt = divmod(n, TT)
                        if kt == 0 and h >= 1:
                            pe.wait_ge(oe, h)
                        pe.wait_ge(ex, n + 1)
                        for c in range(4):
                            mm = pe.matmul(ps[32 * c:32 * c + 32, 6, 0:256], v_wide[:, h, kt, :],
                                           ring[:, n % RING, 256 * c:256 * c + 256], start=(kt == 0), stop=(kt == TT - 1))
                        mm.then_inc(pv, 1)

                    for n in range(-AHEAD, units + 2):
                        m = n + AHEAD
                        if m < units:
                            first_scores(m, 0)
                        if 0 <= n < units:
                            h, kt = divmod(n, TT)
                            if kt == 0:
                                pe.wait_ge(sh, h + 1)
                            if n >= 2:
                                pe.wait_ge(ex, n - 1)
                            for k in range(2):
                                mm = pe.matmul(ps[:, 2 + 2 * (n % 2) + k, :], k_ops[:, h % HB, kt * P:(kt + 1) * P],
                                               q_ops[:, h % HB, k * HALF:(k + 1) * HALF], start=True, stop=True)
                            mm.then_inc(sc, 1)
                        if m < units:
                            first_scores(m, 1)
                        if m % TT == 0 and 1 <= m // TT <= NH:
                            turn(m // TT - 1)
                        if n >= 2:
                            sums(n - 2)

                @block.vector
                def _(dve):
                    for m in range(units):
                        h, qt = divmod(m, TT)
                        for half in range(2):
                            dve.wait_ge(fs, 2 * m + half + 1)
                            dve.tensor_reduce(half_max[:, h % 2, qt, half:half + 1], ps[:, half, :], AX.X, ALU.max).then_inc(mx, 1)
                        if qt == TT - 1:
                            dve.wait_ge(mx, 2 * m + 2)
                            dve.tensor_reduce(max_bf[:, h % 2, :], half_max[:, h % 2, :, :], AX.X, ALU.max).then_inc(cb, 1)
                            dve.wait_ge(cb, h + 1)
                            if h >= 2:
                                dve.wait_ge(tn, h - 1)
                            dve.scalar_tensor_tensor(out=shift_z[:, h % 2, :, :],
                                                     in0=max_bf[:, h % 2, :].unsqueeze(1).broadcast_to([P, TT, TT]), scalar=-1.0,
                                                     in1=eye8[:, :, :], op0=ALU.mult, op1=ALU.mult).then_inc(zs, 1)

                @block.scalar
                def _(act):
                    def shift_rows(h):
                        act.wait_ge(tn, h + 1)
                        if h >= HB:
                            act.wait_ge(sc, TT * (h - HB + 1))
                        act.activation(q_ops[SHIFT:SHIFT + TT, h % HB, :], turned, ACT.Copy).then_inc(sh, 1)

                    shift_rows(0)
                    for n in range(units + 2):
                        h, kt = divmod(n, TT)
                        if n < units:
                            act.wait_ge(sc, n + 1)
                            if n >= RING:
                                act.wait_ge(pv, n - RING + 1)
                            act.activation(ring[:, n % RING, :].rearrange("p (k c) -> p k c", k=2),
                                           ps[:, 2 + 2 * (n % 2):4 + 2 * (n % 2), :], ACT.Exp).then_inc(ex, 1)
                        if kt == TT + TT - AHEAD and h + 1 < NH:
                            shift_rows(h + 1)
                        if kt == 1 and h >= 1:
                            act.wait_ge(pv, TT * h)
                            act.activation(outT_all[:, h - 1, :], ps[:, 6, 0:256], ACT.Copy).then_inc(oe, 1)
                @block.gpsimd
                def _(pool):
                    for h in range(NH - HB):
                        pool.wait_ge(sc, TT * (h + 1))
                        pool.memset(q_ops[SHIFT:SHIFT + TT, h % HB, :], 0.0).then_inc(sem("ra_cleared"), 1)
            end_stage(*names, "ra_loaded", "ra_cleared")

        def rows_of_heads():
            tp, ch = sem("np_transposed"), sem("np_chain")
            rec = row_rec_all
            with nc.Block() as block:
                @block.tensor
                def _(pe):
                    for h in range(NH):
                        if h >= NH // 2 and h % 2 == 0:
                            pe.wait_ge(ch, 2 * (h - NH // 2) + 4)
                        for j in range(2):
                            pe.transpose(tiles_of(0, n=16)[:, 2 * (h % 8) + j, :], outT_all[:, h, j * P:(j + 1) * P],
                                         ident[:, :]).then_inc(tp, 1)

                @block.vector
                def _(dve):
                    for h in range(NH):
                        dve.wait_ge(tp, 4 * (h // 2) + 4)
                        part = tiles_of(0, n=16)[:, 2 * (h % 8):2 * (h % 8) + 2, :].rearrange("p j (c w) -> p c j w", w=32)
                        r = rec[:, h, :].rearrange("p (c j) -> p c j", j=2)
                        dve.reciprocal(r, part[:, :, :, DH]).then_inc(ch, 1)
                        dve.wait_ge(ch, 2 * h + 1)
                        dst = o_rows[:, :, h * DH:(h + 1) * DH].rearrange("p (c j) w -> p c j w", j=2)
                        dve.tensor_tensor(dst, part[:, :, :, 0:DH], r.unsqueeze(3).broadcast_to([P, 4, 2, DH]),
                                          ALU.mult).then_inc(ch, 1)
            end_stage("np_transposed", "np_chain")

        row_rec_all = sb("row_rec_all", [P, NH, TT])

        WB = 3
        q12 = w_ops[:, 0:WB, :]
        q13 = w_ops[:, WB:2 * WB, :]
        k11 = w_ops[:, 2 * WB:3 * WB, :]
        k22 = w_ops[:, 3 * WB:4 * WB, :]
        k31 = w_ops[:, 4 * WB:5 * WB, :]
        PLACES = ((q12, 0, 0), (q12, 1, 1), (q13, 0, 0), (q13, 1, 2),
                  (k11, 0, 3), (k11, 1, 3), (k22, 0, 4), (k22, 1, 4), (k31, 0, 5), (k31, 1, 3))
        pair_w = sb("pair_w", [P, 2, 3, P])
        null_v = sb("null_v", [P, 256])
        out_w = sb("out_w", [P, 2, D])
        null_map = sb("null_map", [P, NH])
        null_scores = sb("null_scores", [P, TT, NH])
        max_all = sb("max_all", [P, NH, TT], BF16)
        raw_max = sb("raw_max", [P, 2, TT])
        key_sums = sb("key_sums", [P, NH, TT])
        null_all = sb("null_all", [P, NH, TT])
        ones_f = sb("ones_f", [P, P])
        ones_bf = sb("ones_bf", [P, P], BF16)
        WIDE_SCALE = float(WH) ** -0.5

        def null_keys():
            ld, bl, mm = sem("nk_loaded"), sem("nk_blocks"), sem("nk_products")
            wqT = big[:, 0:NH // 2 * D].rearrange("p (a d) -> p a d", d=D)
            nk = big[:, 1024:1024 + NH // 2]
            blocks = big[:, 2048:2048 + NH].rearrange("p (a j) -> p a j", j=2)
            with nc.Block() as block:
                @block.sync
                def _(sp):
                    sp.dma_start(wqT, A["b_qwT"]).then_inc(ld, 16)
                    sp.dma_start(nk, A["b_nk"]).then_inc(ld, 16)

                @block.vector
                def _(dve):
                    dve.memset(ones_f[:, :], 1.0).then_inc(bl, 1)
                    dve.memset(ones_bf[:, :], 1.0).then_inc(bl, 1)
                    dve.wait_ge(ld, 32)
                    dve.tensor_tensor(blocks, nk.unsqueeze(2).broadcast_to([P, NH // 2, 2]),
                                      pair_mask[:, :].unsqueeze(1).broadcast_to([P, NH // 2, 2]), ALU.mult).then_inc(bl, 1)
                    dve.wait_ge(mm, 1)
                    dve.tensor_copy(null_map[:, :], ps[:, 0, 0:NH]).then_inc(bl, 1)

                @block.tensor
                def _(pe):
                    pe.wait_ge(bl, 3)
                    for a in range(NH // 2):
                        mm_ = pe.matmul(ps[:, 0, 2 * a:2 * a + 2], wqT[:, a, :], blocks[:, a, :], start=True, stop=True)
                    mm_.then_inc(mm, 1)
            end_stage("nk_loaded", "nk_blocks", "nk_products")

        def wide_heads():
            names = ("wa_chunk", "wa_part1", "wa_rest", "wa_part2", "wa_part3", "wa_values", "wa_kept",
                     "wa_loaded", "wa_null", "wa_first", "wa_max", "wa_combined", "wa_shift", "wa_turned", "wa_shifted",
                     "wa_scores", "wa_exp", "wa_sums", "wa_out", "wa_added", "wa_key_sums", "wa_zeroed", "wa_null_kept")
            wl = [sem("wa_weights_even"), sem("wa_weights_odd")]
            (ck, p1, rs, p2, p3, vv, kp, ld, nl, fs, mx, cb, zs, tn, sh, sc, ex, pv, oe, ad, ks, zr, nk) = (sem(n) for n in names)
            units = NH * TT
            pairs = NH // 2
            turned = ps[0:TT, 7, :].bitcast(BF16)
            AT = {-22: 0, -21: 1, -20: 2, -18: 3, -12: 4, -10: 5}
            START = -22

            def chunks_at(n):
                return [(i, c) for o, c in AT.items() for i in range(pairs) if 2 * TT * i + o == n]

            slots = range(START, units + 3)

            with nc.Block() as block:
                @block.sync
                def _(sp):
                    def weights(i):
                        if i >= 2:
                            sp.wait_ge(ck, 6 * (i - 1))
                        sp.dma_start(pair_w[:, i % 2, :, :], A["b_pw"][:, i, :, :]).then_inc(wl[i % 2], 16)

                    weights(0)
                    weights(1)
                    for h in range(NH):
                        i, j = divmod(h, 2)
                        if h >= WB:
                            sp.wait_ge(sc, TT * (h - WB + 1))
                        for n, (dst, half, part) in enumerate(PLACES):
                            done = 4 * i + (2 if part < 3 else 4)
                            sp.wait_ge((p1, p2, p3)[part % 3], done)
                            sp.dma_start(dst[WH * half:WH * half + WH, h % WB, :], w_parts[WH * j:WH * j + WH, part, :]).then_inc(ld, 16)
                        sp.wait_ge(ld, 16 * len(PLACES) * (h + 1))
                        sp.nop().then_inc(sem("wa_operands"), 1)
                        if j == 1 and i + 2 < pairs:
                            weights(i + 2)

                @block.tensor
                def _(pe):
                    readers_of_7 = []

                    def bank7(*readers):
                        for signal, count in readers_of_7:
                            pe.wait_ge(signal, count)
                        readers_of_7[:] = readers

                    def chunk(i, c):
                        if c == 0:
                            pe.wait_ge(wl[i % 2], 16 * (i // 2 + 1))
                        if c < 4:
                            bank7((p1, 4 * i + c + 1), (rs, 4 * i + c + 1))
                        else:
                            bank7((vv, 2 * i + c - 3))
                        if c < 4:
                            pe.matmul(ps[:, 7, :], pair_w[:, i % 2, c // 2, :], xT[:, (c % 2) * HALF:(c % 2 + 1) * HALF],
                                      start=True, stop=True).then_inc(ck, 1)
                        else:
                            for t in range(4):
                                k = 4 * (c - 4) + t
                                mm = pe.matmul(ps[:, 7, t * P:(t + 1) * P], xT[:, k * P:(k + 1) * P], pair_w[:, i % 2, 2, :],
                                               start=True, stop=True)
                            mm.then_inc(ck, 1)

                    def first_scores(m, half):
                        h, qt = divmod(m, TT)
                        if qt == 0 and half == 0:
                            pe.wait_ge(sem("wa_operands"), h + 1)
                        if m >= 1:
                            pe.wait_ge(mx, 2 * (m - 1) + half + 1)
                        pe.matmul(ps[:, half, :], q12[:, h % WB, qt * P:(qt + 1) * P],
                                  k11[:, h % WB, half * HALF:(half + 1) * HALF], start=True, stop=True).then_inc(fs, 1)

                    def turn(h):
                        pe.wait_ge(zs, h + 1)
                        bank7((sh, h + 1))
                        for t in range(TT):
                            mm = pe.transpose(turned[:, t * P:(t + 1) * P], shift_z[:, h % 2, t, :], ident_bf[:, :])
                        mm.then_inc(tn, 1)

                    def sums(n):
                        h, kt = divmod(n, TT)
                        if kt == 0:
                            pe.wait_ge(vv, 2 * (h // 2) + 2)
                            if h >= 1:
                                pe.wait_ge(oe, h)
                        pe.wait_ge(ex, n + 1)
                        for c in range(2):
                            mm = pe.matmul(ps[WH * c:WH * c + WH, 6, :], v_pair[:, (h // 2) % 2, kt, WH * (h % 2):WH * (h % 2) + WH],
                                           ring[:, n % RING, HALF * c:HALF * c + HALF], start=(kt == 0), stop=(kt == TT - 1))
                        mm.then_inc(pv, 1)

                    def across(h):
                        pe.wait_ge(ad, (TT - 1) * (h + 1))
                        bank7((kp, h + 1))
                        for t in range(TT):
                            mm = pe.matmul(ps[:, 7, t:t + P], key_acc[:, h % 2, t * P:(t + 1) * P], ones_f[:, :], start=True, stop=True)
                        mm.then_inc(ks, 1)

                    bank7((nk, 1))
                    for t in range(TT):
                        mm = pe.matmul(tiles_of(7, w=NH)[:, t, :], xT[:, t * P:(t + 1) * P], null_map[:, :], start=True, stop=True)
                    mm.then_inc(nl, 1)
                    for n in slots:
                        m = n + AHEAD
                        for i, c in chunks_at(n):
                            chunk(i, c)
                        if 0 <= m < units:
                            first_scores(m, 0)
                        if 0 <= n < units:
                            h, kt = divmod(n, TT)
                            if kt == 0:
                                pe.wait_ge(sh, h + 1)
                            if n >= 2:
                                pe.wait_ge(ex, n - 1)
                            keys = [o[:, h % WB, kt * P:(kt + 1) * P] for o in (k11, k22, k31)] + [ones_bf[:, :]]
                            queries = [o[:, h % WB, :] for o in (q12, q12, q13)] + [shift_rows[:, h % 2, :]]
                            for k in range(2):
                                for s, (kk, qq) in enumerate(zip(keys, queries)):
                                    mm = pe.matmul(ps[:, 2 + 2 * (n % 2) + k, :], kk, qq[:, k * HALF:(k + 1) * HALF],
                                                   start=(s == 0), stop=(s == 3))
                            mm.then_inc(sc, 1)
                        if 0 <= m < units:
                            first_scores(m, 1)
                        if m >= TT and m % TT == 0 and m // TT <= NH:
                            turn(m // TT - 1)
                        if 2 <= n < units + 2:
                            sums(n - 2)
                        if n >= TT + 1 and n % TT == 1:
                            across(n // TT - 1)

                @block.vector
                def _(dve):
                    def chunk(i, c):
                        if c < 4:
                            g = 4 * i + c
                            dve.wait_ge(ck, 6 * i + c + 1)
                            dve.wait_ge(p1, g + 1)
                            if g >= 2:
                                dve.wait_ge(p3, g - 1)
                            dve.tensor_tensor(rest2[:, g % 2, :], ps[:, 7, :], w_parts[:, 3 * (c // 2), (c % 2) * HALF:(c % 2 + 1) * HALF],
                                              ALU.subtract).then_inc(rs, 1)

                    dve.memset(shift_rows[:, :, :], 0.0).then_inc(zr, 1)
                    dve.wait_ge(nl, 1)
                    dve.tensor_copy(null_scores[:, :, :], tiles_of(7, w=NH)).then_inc(nk, 1)
                    for n in slots:
                        m = n + AHEAD
                        for i, c in chunks_at(n):
                            chunk(i, c)
                        if 0 <= m < units:
                            h, qt = divmod(m, TT)
                            for half in range(2):
                                dve.wait_ge(fs, 2 * m + half + 1)
                                dve.tensor_reduce(half_max[:, h % 2, qt, half:half + 1], ps[:, half, :], AX.X, ALU.max).then_inc(mx, 1)
                            if qt == TT - 1:
                                dve.wait_ge(mx, 2 * m + 2)
                                dve.tensor_reduce(raw_max[:, h % 2, :], half_max[:, h % 2, :, :], AX.X, ALU.max).then_inc(cb, 1)
                                dve.wait_ge(cb, 2 * h + 1)
                                if h == 0:
                                    dve.wait_ge(nk, 1)
                                dve.tensor_tensor(max_all[:, h, :], raw_max[:, h % 2, :], null_scores[:, :, h], ALU.max).then_inc(cb, 1)
                                dve.wait_ge(cb, 2 * h + 2)
                                if h >= 2:
                                    dve.wait_ge(tn, h - 1)
                                dve.scalar_tensor_tensor(out=shift_z[:, h % 2, :, :],
                                                         in0=max_all[:, h, :].unsqueeze(1).broadcast_to([P, TT, TT]), scalar=-1.0,
                                                         in1=eye8[:, :, :], op0=ALU.mult, op1=ALU.mult).then_inc(zs, 1)
                        if 1 <= n <= units:
                            h, kt = divmod(n - 1, TT)
                            if kt >= 1:
                                if kt == 1 and h >= 2:
                                    dve.wait_ge(ks, h - 1)
                                dve.wait_ge(ex, n)
                                if kt >= 2:
                                    dve.wait_ge(ad, (TT - 1) * h + kt - 1)
                                first = ring[:, (n - 2) % RING, :] if kt == 1 else key_acc[:, h % 2, :]
                                dve.tensor_tensor(key_acc[:, h % 2, :], first, ring[:, (n - 1) % RING, :], ALU.add).then_inc(ad, 1)
                        if n >= TT + 1 and n % TT == 1:
                            h = n // TT - 1
                            dve.wait_ge(ks, h + 1)
                            dve.tensor_copy(key_sums[:, h, :], ps[:, 7, 0:TT]).then_inc(kp, 1)

                @block.scalar
                def _(act):
                    def shift_row(h):
                        act.wait_ge(tn, h + 1)
                        if h == 0:
                            act.wait_ge(zr, 1)
                        if h >= 2:
                            act.wait_ge(sc, TT * (h - 1))
                        act.activation(shift_rows[0:TT, h % 2, :], turned, ACT.Copy).then_inc(sh, 1)

                    for n in slots:
                        m = n + AHEAD
                        for i, c in chunks_at(n):
                            act.wait_ge(ck, 6 * i + c + 1)
                            if c < 4:
                                if c in (0, 2) and i >= 1:
                                    act.wait_ge(sem("wa_operands"), 2 * i)
                                act.activation(w_parts[:, 3 * (c // 2), (c % 2) * HALF:(c % 2 + 1) * HALF], ps[:, 7, :],
                                               ACT.Copy).then_inc(p1, 1)
                            else:
                                if c == 4 and i >= 2:
                                    act.wait_ge(pv, 2 * TT * (i - 1))
                                act.activation(v_pair[:, i % 2, 4 * (c - 4):4 * (c - 4) + 4, :],
                                               ps[:, 7, :].rearrange("p (t c) -> p t c", c=P), ACT.Copy).then_inc(vv, 1)
                        if 0 <= n < units:
                            h, kt = divmod(n, TT)
                            act.wait_ge(sc, n + 1)
                            if n >= RING:
                                hr, kr = divmod(n - RING, TT)
                                act.wait_ge(pv, n - RING + 1)
                                act.wait_ge(ad, (TT - 1) * hr + max(kr, 1))
                            act.activation(ring[:, n % RING, :].rearrange("p (k c) -> p k c", k=2),
                                           ps[:, 2 + 2 * (n % 2):4 + 2 * (n % 2), :], ACT.Exp, scale=WIDE_SCALE).then_inc(ex, 1)
                        if m >= TT and m % TT == 0 and m // TT <= NH:
                            shift_row(m // TT - 1)
                        if n % TT == 1 and n >= TT + 1:
                            h = n // TT - 1
                            act.wait_ge(pv, TT * (h + 1))
                            act.activation(wideT[:, h, :], ps[:, 6, :], ACT.Copy).then_inc(oe, 1)

                @block.gpsimd
                def _(pool):
                    for g in range(4 * pairs):
                        i, c = divmod(g, 4)
                        cols = slice((c % 2) * HALF, (c % 2 + 1) * HALF)
                        if c in (0, 2) and i >= 1:
                            pool.wait_ge(sem("wa_operands"), 2 * i)
                        pool.wait_ge(rs, g + 1)
                        pool.tensor_copy(w_parts[:, 3 * (c // 2) + 1, cols], rest2[:, g % 2, :]).then_inc(p2, 1)
                        pool.wait_ge(p2, g + 1)
                        pool.tensor_tensor(w_parts[:, 3 * (c // 2) + 2, cols], rest2[:, g % 2, :],
                                           w_parts[:, 3 * (c // 2) + 1, cols], ALU.subtract).then_inc(p3, 1)
            end_stage(*names, "wa_operands", "wa_weights_even", "wa_weights_odd")

        def null_share():
            ch, ex = sem("ns_chain"), sem("ns_exp")
            with nc.Block() as block:
                @block.vector
                def _(dve):
                    dve.tensor_tensor(null_all[:, :, :], null_scores[:, :, :].rearrange("p t h -> p h t"), max_all[:, :, :],
                                      ALU.subtract).then_inc(ch, 1)
                    dve.wait_ge(ex, 1)
                    dve.tensor_tensor(key_sums[:, :, :], key_sums[:, :, :], null_all[:, :, :], ALU.add).then_inc(ch, 1)
                    dve.wait_ge(ch, 2)
                    dve.reciprocal(row_rec_all[:, :, :], key_sums[:, :, :]).then_inc(ch, 1)

                @block.scalar
                def _(act):
                    act.wait_ge(ch, 1)
                    act.activation(null_all[:, :, :], null_all[:, :, :], ACT.Exp, scale=WIDE_SCALE).then_inc(ex, 1)
            end_stage("ns_chain", "ns_exp")
        def wide_post(g):
            tp, ch, nn, wl = sem("np_transposed"), sem("np_chain"), sem("wn_null"), sem("wn_loaded")
            with nc.Block() as block:
                @block.sync
                def _(sp):
                    sp.dma_start(null_v[:, :], A["b_nv"][:, g * 256:(g + 1) * 256]).then_inc(wl, 16)
                    sp.dma_start(out_w[:, :, :], A["b_ow"][:, 2 * g:2 * g + 2, :]).then_inc(wl, 16)
                    sp.wait_ge(wl, 32)

                @block.tensor
                def _(pe):
                    for hh in range(GH):
                        for j in range(4):
                            pe.transpose(ps[:, hh, j * P:(j + 1) * P],
                                         wideT[:, GH * g + hh, j * P:(j + 1) * P], ident[:, :]).then_inc(tp, 1)

                @block.gpsimd
                def _(pool):
                    pool.wait_ge(wl, 32)
                    for hh in range(GH):
                        pool.tensor_tensor(o_tmp[:, :, hh * WH:(hh + 1) * WH],
                                           null_all[:, GH * g + hh, :].unsqueeze(2).broadcast_to([P, TT, WH]),
                                           null_v[:, hh * WH:(hh + 1) * WH].unsqueeze(1).broadcast_to([P, TT, WH]),
                                           ALU.mult).then_inc(nn, 1)

                @block.vector
                def _(dve):
                    for hh in range(GH):
                        dve.wait_ge(tp, 4 * hh + 4)
                        dve.wait_ge(nn, hh + 1)
                        part = ps[:, hh, :].rearrange("p (j c w) -> p c j w", j=4, c=2)
                        tmp = o_tmp[:, :, hh * WH:(hh + 1) * WH]
                        t4 = tmp.rearrange("p (c j) w -> p c j w", c=2)
                        dve.tensor_tensor(t4, part, t4, ALU.add).then_inc(ch, 1)
                        dve.wait_ge(ch, 2 * hh + 1)
                        dve.tensor_tensor(o_rows[:, :, hh * WH:(hh + 1) * WH], tmp,
                                          row_rec_all[:, GH * g + hh, :].unsqueeze(2).broadcast_to([P, TT, WH]),
                                          ALU.mult).then_inc(ch, 1)
            end_stage("np_transposed", "np_chain", "wn_null", "wn_loaded")

        def ranks(dve, ch, n0, vals, n_e, top):
            cmp4 = r_cmp[:, 0:TT * n_e * n_e].rearrange("p (t e f) -> p t e f", t=TT, e=n_e)
            eq4 = r_eq[:, 0:TT * n_e * n_e].rearrange("p (t e f) -> p t e f", t=TT, e=n_e)
            other = vals.unsqueeze(2).broadcast_to([P, TT, n_e, n_e])
            own = vals.unsqueeze(3).broadcast_to([P, TT, n_e, n_e])
            dve.tensor_tensor(cmp4, other, own, ALU.is_gt).then_inc(ch, 1)
            dve.tensor_tensor(eq4, other, own, ALU.is_equal).then_inc(ch, 1)
            dve.wait_ge(ch, n0 + 2)
            dve.tensor_tensor(eq4, eq4, tri[:, 0:n_e, 0:n_e].unsqueeze(1).broadcast_to([P, TT, n_e, n_e]),
                              ALU.mult).then_inc(ch, 1)
            dve.wait_ge(ch, n0 + 3)
            dve.tensor_tensor(cmp4, cmp4, eq4, ALU.add).then_inc(ch, 1)
            dve.wait_ge(ch, n0 + 4)
            dve.tensor_reduce(r_c[:, :, 0:n_e], cmp4, AX.X, ALU.add).then_inc(ch, 1)
            dve.wait_ge(ch, n0 + 5)
            dve.tensor_scalar(r_c[:, :, 0:n_e], r_c[:, :, 0:n_e], float(top) - 0.5, None, ALU.is_lt).then_inc(ch, 1)
            dve.wait_ge(ch, n0 + 6)
            return n0 + 6

        def router_first():
            mm, ch, ex = sem("rt_logits"), sem("rt_chain"), sem("rt_exp")
            lg = tiles_of(0, w=E0)
            with nc.Block() as block:
                @block.tensor
                def _(pe):
                    for t in range(TT):
                        last = pe.matmul(lg[:, t, :], xT[:, t * P:(t + 1) * P], W["m_router"][:, :], start=True, stop=True)
                    last.then_inc(mm, 1)

                @block.vector
                def _(dve):
                    a, b = r_a[:, :, 0:E0], r_b[:, :, 0:E0]
                    wide = lambda v: v[:, :].unsqueeze(2).broadcast_to([P, TT, E0])
                    dve.wait_ge(mm, 1)
                    dve.tensor_reduce(r_s[:, :], lg, AX.X, ALU.max).then_inc(ch, 1)
                    dve.wait_ge(ch, 1)
                    dve.tensor_tensor(a, lg, wide(r_s), ALU.subtract).then_inc(ch, 1)
                    dve.wait_ge(ex, 1)
                    dve.tensor_reduce(r_s[:, :], b, AX.X, ALU.add).then_inc(ch, 1)
                    dve.wait_ge(ch, 3)
                    dve.reciprocal(r_r[:, :], r_s[:, :]).then_inc(ch, 1)
                    dve.wait_ge(ch, 4)
                    dve.tensor_tensor(a, b, wide(r_r), ALU.mult).then_inc(ch, 1)
                    dve.wait_ge(ch, 5)
                    n = ranks(dve, ch, 5, a, E0, K0)
                    dve.wait_ge(ex, 2)
                    dve.tensor_tensor(b, b, r_c[:, :, 0:E0], ALU.mult).then_inc(ch, 1)
                    dve.wait_ge(ch, n + 1)
                    dve.tensor_reduce(r_s[:, :], b, AX.X, ALU.add).then_inc(ch, 1)
                    dve.wait_ge(ch, n + 2)
                    dve.reciprocal(r_r[:, :], r_s[:, :]).then_inc(ch, 1)
                    dve.wait_ge(ch, n + 3)
                    dve.tensor_tensor(r_w[:, :, 0:E0], b, wide(r_r), ALU.mult).then_inc(ch, 1)

                @block.scalar
                def _(act):
                    act.wait_ge(ch, 2)
                    act.activation(r_b[:, :, 0:E0], r_a[:, :, 0:E0], ACT.Exp).then_inc(ex, 1)
                    act.wait_ge(ch, 5)
                    act.activation(r_b[:, :, 0:E0], r_a[:, :, 0:E0], ACT.Exp).then_inc(ex, 1)
            end_stage("rt_logits", "rt_chain", "rt_exp")

        def experts_first():
            gt, up, si, fu, dn, ad = (sem(n) for n in ("ef_gate", "ef_up", "ef_silu", "ef_fused", "ef_down", "ef_added"))
            steps = 2 * E0 * (F0 // P)
            with nc.Block() as block:
                @block.tensor
                def _(pe):
                    def down(m):
                        pe.wait_ge(fu, 2 * m + 2)
                        if m >= 2:
                            pe.wait_ge(ad, 4 * (m - 1))
                        for s in range(4):
                            for f in range(2):
                                mm = pe.matmul(ps[:, 4 + m % 2, s * P:(s + 1) * P],
                                               fuse[:, (2 * m + f) % 4, s * P:(s + 1) * P],
                                               W["m_down"][:, 2 * (m % E0) + f, :], start=(f == 0), stop=(f == 1))
                        mm.then_inc(dn, 1)

                    for n in range(steps):
                        blk, e, f = n // (2 * E0), (n // 2) % E0, n % 2
                        if n >= 2:
                            pe.wait_ge(si, n - 1)
                            pe.wait_ge(fu, n - 1)
                        for m, w in enumerate(("m_gate", "m_up")):
                            pe.matmul(ps[:, 2 * m + n % 2, :], W[w][:, e * F0 + f * P:e * F0 + (f + 1) * P],
                                      xT[:, blk * HALF:(blk + 1) * HALF], start=True, stop=True).then_inc((gt, up)[m], 1)
                        if n % 2 == 0 and n >= 2:
                            down(n // 2 - 1)
                    down(steps // 2 - 1)

                @block.scalar
                def _(act):
                    for n in range(steps):
                        act.wait_ge(gt, n + 1)
                        if n >= 2:
                            act.wait_ge(fu, n - 1)
                        act.activation(act_g[:, n % 2, :], ps[:, n % 2, :], ACT.Silu).then_inc(si, 1)

                @block.vector
                def _(dve):
                    def add(m):
                        dve.wait_ge(dn, m + 1)
                        e = m % E0
                        for s in range(4):
                            t = 4 * (m // E0) + s
                            if m % E0:
                                dve.wait_ge(ad, 4 * (m - 1) + s + 1)
                            dve.scalar_tensor_tensor(out=x[:, t, :], in0=ps[:, 4 + m % 2, s * P:(s + 1) * P],
                                                     scalar=r_w[:, t, e:e + 1], in1=x[:, t, :],
                                                     op0=ALU.mult, op1=ALU.add).then_inc(ad, 1)

                    for n in range(steps):
                        dve.wait_ge(si, n + 1)
                        dve.wait_ge(up, n + 1)
                        if n >= 4:
                            dve.wait_ge(dn, (n - 4) // 2 + 1)
                        dve.tensor_tensor(fuse[:, n % 4, :], act_g[:, n % 2, :], ps[:, 2 + n % 2, :], ALU.mult).then_inc(fu, 1)
                        if n % 2 == 1 and n >= 3:
                            add(n // 2 - 1)
                    add(steps // 2 - 1)
            end_stage("ef_gate", "ef_up", "ef_silu", "ef_fused", "ef_down", "ef_added")

        def router_second():
            mm, ch, ex = sem("rt_logits"), sem("rt_chain"), sem("rt_exp")
            lg = tiles_of(0, w=E1)
            with nc.Block() as block:
                @block.tensor
                def _(pe):
                    for t in range(TT):
                        last = pe.matmul(lg[:, t, :], xT[:, t * P:(t + 1) * P], W["n_router"][:, :], start=True, stop=True)
                    last.then_inc(mm, 1)

                @block.scalar
                def _(act):
                    act.wait_ge(mm, 1)
                    act.activation(r_a[:, :, :], lg, ACT.Exp, scale=-1.0).then_inc(ex, 1)

                @block.vector
                def _(dve):
                    dve.wait_ge(ex, 1)
                    dve.tensor_scalar(r_b[:, :, :], r_a[:, :, :], 1.0, None, ALU.add).then_inc(ch, 1)
                    dve.wait_ge(ch, 1)
                    dve.reciprocal(r_a[:, :, :], r_b[:, :, :]).then_inc(ch, 1)
                    dve.wait_ge(ch, 2)
                    dve.tensor_tensor(r_b[:, :, :], r_a[:, :, :],
                                      W["n_bias"][:, :].unsqueeze(1).broadcast_to([P, TT, E1]), ALU.add).then_inc(ch, 1)
                    dve.wait_ge(ch, 3)
                    n = ranks(dve, ch, 3, r_b[:, :, :], E1, K1)
                    dve.tensor_tensor(r_b[:, :, :], r_a[:, :, :], r_c[:, :, :], ALU.mult).then_inc(ch, 1)
                    dve.wait_ge(ch, n + 1)
                    dve.tensor_reduce(r_s[:, :], r_b[:, :, :], AX.X, ALU.add).then_inc(ch, 1)
                    dve.wait_ge(ch, n + 2)
                    dve.reciprocal(r_r[:, :], r_s[:, :]).then_inc(ch, 1)
                    dve.wait_ge(ch, n + 3)
                    dve.scalar_tensor_tensor(out=r_w[:, :, :], in0=r_b[:, :, :], scalar=ROUTE_SCALE,
                                             in1=r_r[:, :].unsqueeze(2).broadcast_to([P, TT, E1]),
                                             op0=ALU.mult, op1=ALU.mult).then_inc(ch, 1)
            end_stage("rt_logits", "rt_chain", "rt_exp")

        def experts_second():
            gt, up, si, fu, dn, ad = (sem(n) for n in ("ef_gate", "ef_up", "ef_silu", "ef_fused", "ef_down", "ef_added"))
            pairs = E1 // 2 + 1
            steps = 2 * pairs
            with nc.Block() as block:
                @block.tensor
                def _(pe):
                    def down(n):
                        k = n % pairs
                        pe.wait_ge(fu, n + 1)
                        if n >= 2:
                            pe.wait_ge(ad, n - 1)
                        for j in range(2 if k < pairs - 1 else 1):
                            for s in range(4):
                                w = W["n_down"][64 * j:64 * j + 64, k, :] if k < pairs - 1 else W["n_sdown"][:, :]
                                mm = pe.matmul(ps[:, 4 + 2 * (n % 2) + j, s * P:(s + 1) * P],
                                               fuse[64 * j:64 * j + 64, n % 2, s * P:(s + 1) * P], w,
                                               start=True, stop=True)
                        mm.then_inc(dn, 1)

                    for n in range(steps):
                        blk, k = divmod(n, pairs)
                        rows = P if k < pairs - 1 else F1
                        if n >= 2:
                            pe.wait_ge(si, n - 1)
                            pe.wait_ge(fu, n - 1)
                        for m, (w, ws) in enumerate((("n_gate", "n_sgate"), ("n_up", "n_sup"))):
                            lhs = W[w][:, k * P:(k + 1) * P] if k < pairs - 1 else W[ws][:, :]
                            pe.matmul(ps[0:rows, 2 * m + n % 2, :], lhs, xT[:, blk * HALF:(blk + 1) * HALF],
                                      start=True, stop=True).then_inc((gt, up)[m], 1)
                        if n >= 1:
                            down(n - 1)
                    down(steps - 1)

                @block.scalar
                def _(act):
                    for n in range(steps):
                        rows = P if n % pairs < pairs - 1 else F1
                        act.wait_ge(gt, n + 1)
                        if n >= 2:
                            act.wait_ge(fu, n - 1)
                        act.activation(act_g[0:rows, n % 2, :], ps[0:rows, n % 2, :], ACT.Silu).then_inc(si, 1)

                @block.vector
                def _(dve):
                    added = 0

                    def add(n):
                        nonlocal added
                        blk, k = divmod(n, pairs)
                        dve.wait_ge(dn, n + 1)
                        for j in range(2 if k < pairs - 1 else 1):
                            for s in range(4):
                                t = 4 * blk + s
                                if k or j:
                                    dve.wait_ge(sem("es_chain"), added - 3)
                                scal = r_w[:, t, 2 * k + j:2 * k + j + 1] if k < pairs - 1 else 1.0
                                ins = dve.scalar_tensor_tensor(
                                    out=x[:, t, :], in0=ps[:, 4 + 2 * (n % 2) + j, s * P:(s + 1) * P], scalar=scal,
                                    in1=x[:, t, :], op0=ALU.mult, op1=ALU.add)
                                ins.then_inc(sem("es_chain"), 1)
                                added += 1
                        dve.wait_ge(sem("es_chain"), added)
                        dve.nop().then_inc(ad, 1)

                    for n in range(steps):
                        rows = P if n % pairs < pairs - 1 else F1
                        dve.wait_ge(si, n + 1)
                        dve.wait_ge(up, n + 1)
                        if n >= 2:
                            dve.wait_ge(dn, n - 1)
                        dve.tensor_tensor(fuse[0:rows, n % 2, :], act_g[0:rows, n % 2, :], ps[0:rows, 2 + n % 2, :],
                                          ALU.mult).then_inc(fu, 1)
                        if n >= 1:
                            add(n - 1)
                    add(steps - 1)
            end_stage("ef_gate", "ef_up", "ef_silu", "ef_fused", "ef_down", "ef_added", "es_chain")

        lin_k = big[:, 0:LIN_K * S].rearrange("p (k t d) -> p k t d", k=LIN_K, d=D)
        lin_v = big[:, 2048:2048 + LIN_K * S].rearrange("p (k t d) -> p k t d", k=LIN_K, d=D)
        lin_w = big[:, 4096:4096 + 5 * P].rearrange("p (k d) -> p k d", k=5)
        state = big[:, 4736:4736 + 2 * P].rearrange("p (k d) -> p k d", k=2)

        def linear_attention():
            wi, mm, ev, st, sv, om = (sem(n) for n in ("la_weights", "la_products", "la_evacuated", "la_states", "la_state", "la_out"))
            with nc.Block() as block:
                @block.gpsimd
                def _(pool):
                    ws = [W["l_qw"][:, :]] + [W[w][:, k * D:(k + 1) * D] for w in ("l_kw", "l_vw") for k in range(LIN_K)]
                    for n, w in enumerate(ws):
                        pool.tensor_tensor(lin_w[:, n, :], w, ident[:, :], ALU.add).then_inc(wi, 1)

                @block.tensor
                def _(pe):
                    pe.wait_ge(wi, 5)
                    for k in range(2):
                        pe.matmul(ps[:, k, :], lin_w[:, 0, :], xT[:, k * HALF:(k + 1) * HALF], start=True, stop=True).then_inc(mm, 1)
                    for n in range(2 * LIN_K):
                        if n >= 3:
                            pe.wait_ge(ev, 2)
                        for t in range(TT):
                            last = pe.matmul(tiles_of(2 + 2 * (n % 3))[:, t, :], xT[:, t * P:(t + 1) * P],
                                             lin_w[:, 1 + n, :], start=True, stop=True)
                        last.then_inc(mm, 1)
                    pe.wait_ge(ev, 1 + 2 * LIN_K)
                    for k in range(LIN_K):
                        for t in range(TT):
                            last = pe.matmul(ps[:, k, 0:P], lin_k[:, k, t, :], lin_v[:, k, t, :],
                                             start=(t == 0), stop=(t == TT - 1))
                        last.then_inc(st, 1)
                    pe.wait_ge(sv, 3)
                    for t in range(TT):
                        last = pe.matmul(tiles_of(2)[:, t, :], qT[:, 0, t * P:(t + 1) * P], state[:, 0, :], start=True, stop=True)
                    last.then_inc(mm, 1)

                @block.vector
                def _(dve):
                    dve.wait_ge(mm, 2)
                    dve.tensor_scalar(qT[:, 0, :].rearrange("p (k c) -> p k c", k=2), ps[:, 0:2, :], W["l_qb"][:, 0:1], None,
                                      ALU.add).then_inc(ev, 1)
                    for n in range(2 * LIN_K):
                        dst, b = ((lin_k, "l_kb"), (lin_v, "l_vb"))[n // LIN_K]
                        k = n % LIN_K
                        dve.wait_ge(mm, 3 + n)
                        dve.tensor_tensor(dst[:, k, :, :], tiles_of(2 + 2 * (n % 3)),
                                          W[b][:, k * D:(k + 1) * D].unsqueeze(1).broadcast_to([P, TT, D]), ALU.add).then_inc(ev, 1)
                    dve.wait_ge(st, 1)
                    dve.scalar_tensor_tensor(out=state[:, 0, :], in0=ps[:, 0, 0:P], scalar=1.0 / (LIN_N * LIN_N),
                                             in1=block_mask[:, :], op0=ALU.mult, op1=ALU.mult).then_inc(sv, 1)
                    dve.wait_ge(st, 2)
                    dve.tensor_copy(state[:, 1, :], ps[:, 1, 0:P]).then_inc(sv, 1)
                    dve.wait_ge(sv, 2)
                    dve.tensor_tensor(state[:, 0, :], state[:, 0, :], state[:, 1, :], ALU.mult).then_inc(sv, 1)
                    dve.wait_ge(mm, 3 + 2 * LIN_K)
                    dve.tensor_copy(o_rows[:, :, 0:D], tiles_of(2)).then_inc(om, 1)
            end_stage("la_weights", "la_products", "la_evacuated", "la_states", "la_state", "la_out")

        def affine_xT(gain, bias):
            with nc.Block() as block:
                @block.vector
                def _(dve):
                    if bias is None:
                        dve.tensor_scalar(xT[:, :], xT[:, :], gain, None, ALU.mult).then_inc(sem("af_done"), 1)
                    else:
                        dve.tensor_scalar(xT[:, :], xT[:, :], gain, bias, ALU.mult, ALU.add).then_inc(sem("af_done"), 1)
            end_stage("af_done")

        N_CONST = 6
        with nc.Block() as block:
            @block.sync
            def _(sp):
                const = {"ident": ident, "head_mask": head_mask, "pair_mask": pair_mask, "block_mask": block_mask,
                         "tri": tri, "eye8": eye8}
                for n, t in const.items():
                    dims = (slice(None),) * len(t.shape)
                    sp.dma_start(t[dims], A[n]).then_inc(sem("weights_in"), 16)
                for n in resident:
                    dims = (slice(None),) * len(W[n].shape)
                    sp.dma_start(W[n][dims], A[n]).then_inc(sem("weights_in"), 16)
                sp.wait_ge(sem("weights_in"), 16 * (len(const) + len(resident)))

            @block.gpsimd
            def _(pool):
                pool.memset(half_neg[:, :], -0.5).then_inc(sem("half_set"), 1)

            @block.vector
            def _(dve):
                dve.wait_ge(sem("weights_in"), 16 * (N_CONST + len(resident)))
                dve.tensor_copy(ident_bf[:, :], ident[:, :]).then_inc(sem("half_set"), 1)
        end_stage("weights_in", "half_set")

        null_keys()

        with nc.Fori(0, B) as b:
            with nc.Block() as block:
                @block.sync
                def _(sp):
                    sp.dma_start(x[:, :, :], x_in[b]).then_inc(sem("x_in"), 16)
                    sp.wait_ge(sem("x_in"), 16)
            end_stage("x_in")

            layer_norm(x, xn)
            lif_projections()
            with nc.Fori(0, GROUPS) as g:
                lif_heads(g)
                narrow_post(g)
            transposed_rows(1)
            rows_out([qT[:, 0, :]], [W["a_ow"][:, :]], W["a_ob"])
            layer_norm(x, xn)
            router_first()
            experts_first()
            layer_norm(x, xn)
            layer_norm(xn, xn)
            affine_xT(W["b_gamma"][:, 0:1], None)
            wide_heads()
            null_share()
            for g in range(GROUPS):
                wide_post(g)
                transposed_rows(2)
                rows_out([qT[:, 0, :], qT[:, 1, :]], [out_w[:, 0, :], out_w[:, 1, :]], None)
            layer_norm(x, xn)
            router_first()
            experts_first()
            layer_norm(x, xn)
            rope_projections()
            split_parts()
            rotary_heads()
            rows_of_heads()
            transposed_rows(1)
            rows_out([qT[:, 0, :]], [W["c_ow"][:, :]], W["c_ob"])
            layer_norm(x, xn)
            router_second()
            experts_second()
            layer_norm(x, xn)
            linear_attention()
            layer_norm(o_rows[:, :, 0:D], xn)
            affine_xT(W["l_g"][:, 0:1], W["l_b"][:, 0:1])
            rows_out([xT[:, :]], [W["l_ow"][:, :]], W["l_ob"])
            layer_norm(x, xn)
            router_second()
            experts_second()

            with nc.Block() as block:
                @block.sync
                def _(sp):
                    sp.dma_start(x_out[b], x[:, :, :]).then_inc(sem("x_out"), 16)
                    sp.wait_ge(sem("x_out"), 16)
            end_stage("x_out")




def _constants(np):
    inv_freq = (np.float32(1.0) / np.float32(10000.0) ** (np.arange(0, DH, 2, dtype=np.float32) / np.float32(DH))).astype(np.float32)
    freqs = np.arange(S, dtype=np.float32)[:, None] * inv_freq[None, :]
    cos = np.repeat(np.cos(freqs), 2, axis=-1).T.astype(np.float32)
    sin = np.repeat(np.sin(freqs), 2, axis=-1).T.astype(np.float32)
    sign = np.where(np.arange(DH) < DH // 2, -1.0, 1.0).astype(np.float32)[:, None]
    rows = np.arange(P)
    return {
        "ident": np.eye(P, dtype=np.float32),
        "eye8": np.broadcast_to(np.eye(TT, dtype=np.float32), (P, TT, TT)).copy(),
        "head_mask": (rows[:, None] // DH == np.arange(NH)[None, :]).astype(np.float32),
        "pair_mask": (rows[:, None] // WH == np.arange(2)[None, :]).astype(np.float32),
        "block_mask": (rows[:, None] // DH == rows[None, :] // DH).astype(np.float32),
        "cos": np.tile(cos, (NH, 1)),
        "sin": np.tile(sin * sign, (NH, 1)),
        "tri": np.broadcast_to(np.tril(np.ones((E1, E1), np.float32), -1), (P, E1, E1)).copy(),
    }


def _layout(np, i):
    col = lambda v: v.reshape(P, 1)
    rows = lambda v: np.broadcast_to(v.reshape(1, -1), (P, v.size))
    d = np.arange(D)
    rot = (d // DH) * DH + (d % DH + DH // 2) % DH
    a = {"x": i["L0_attn_a_x"]}
    for k in "qkvo":
        a[f"a_{k}w"] = i[f"L0_attn_a_{k}_w"]
    a["a_qb"], a["a_kb"] = col(i["L0_attn_a_q_b"]), col(i["L0_attn_a_k_b"])
    a["a_vb"], a["a_ob"] = rows(i["L0_attn_a_v_b"]), rows(i["L0_attn_a_o_b"])
    a["m_router"] = i["L0_ffn_router_kernel_DE"]
    a["m_gate"] = i["L0_ffn_kernel_gating_EDF"].transpose(1, 0, 2).reshape(D, E0 * F0)
    a["m_up"] = i["L0_ffn_kernel_up_EDF"].transpose(1, 0, 2).reshape(D, E0 * F0)
    a["m_down"] = i["L0_ffn_kernel_down_EFD"].reshape(E0 * F0 // P, P, D).transpose(1, 0, 2)
    a["b_gamma"] = col(i["L0_attn_b_gamma"])
    a["b_qwT"] = i["L0_attn_b_w_q"].T.reshape(NH // 2, P, D).transpose(1, 0, 2)
    wkv = i["L0_attn_b_w_kv"]
    a["b_pw"] = np.stack([w.reshape(D, NH // 2, P) for w in (i["L0_attn_b_w_q"], wkv[:, :NH * WH], wkv[:, NH * WH:])], 2)
    a["b_ow"] = i["L0_attn_b_w_out"].reshape(NH // 2, P, D).transpose(1, 0, 2)
    a["b_nk"] = i["L0_attn_b_null_kv"][0].reshape(NH // 2, P).T
    a["b_nv"] = rows(i["L0_attn_b_null_kv"][1].reshape(-1))
    for k in "qkvo":
        a[f"c_{k}w"] = i[f"L1_attn_a_w{k}"].T
    a["c_qrw"], a["c_krw"] = i["L1_attn_a_wq"].T[:, rot], i["L1_attn_a_wk"].T[:, rot]
    a["c_qb"], a["c_kb"] = col(i["L1_attn_a_bq"]), col(i["L1_attn_a_bk"])
    a["c_qrb"], a["c_krb"] = col(i["L1_attn_a_bq"][rot]), col(i["L1_attn_a_bk"][rot])
    a["c_vb"], a["c_ob"] = rows(i["L1_attn_a_bv"]), rows(i["L1_attn_a_bo"])
    a["l_qw"], a["l_ow"] = i["L1_attn_b_Wq"], i["L1_attn_b_Wo"]
    a["l_kw"] = i["L1_attn_b_Wk"].transpose(1, 0, 2).reshape(D, LIN_K * D)
    a["l_vw"] = i["L1_attn_b_Wv"].transpose(1, 0, 2).reshape(D, LIN_K * D)
    a["l_qb"] = col(i["L1_attn_b_bq"])
    a["l_kb"], a["l_vb"], a["l_ob"] = rows(i["L1_attn_b_bk"]), rows(i["L1_attn_b_bv"]), rows(i["L1_attn_b_bo"])
    a["l_g"], a["l_b"] = col(i["L1_attn_b_ln_g"]), col(i["L1_attn_b_ln_b"])
    a["n_router"], a["n_bias"] = i["L1_ffn_gate_w"].T, rows(i["L1_ffn_gate_b"])
    w13 = i["L1_ffn_w13"].transpose(2, 0, 1)
    a["n_gate"], a["n_up"] = w13[:, :, :F1].reshape(D, E1 * F1), w13[:, :, F1:].reshape(D, E1 * F1)
    a["n_down"] = i["L1_ffn_w2"].transpose(0, 2, 1).reshape(E1 // 2, P, D).transpose(1, 0, 2)
    a["n_sgate"], a["n_sup"] = i["L1_ffn_w13_s"].T[:, :F1], i["L1_ffn_w13_s"].T[:, F1:]
    a["n_sdown"] = i["L1_ffn_w2_s"].T
    return a


def kernel(**inputs):
    import numpy as np
    import concourse.bacc as bacc
    from concourse.bass_utils import run_bass_kernel_spmd

    nc = bacc.Bacc("TRN2", target_bir_lowering=False, num_devices=1)
    given = {n: np.asarray(v) for n, v in inputs.items()}
    laid = {**_layout(np, given), **_constants(np)}
    arrays = {f"in_{n}": np.ascontiguousarray(v) for n, v in laid.items()}
    aps = {n: nc.dram_tensor(f"in_{n}", arrays[f"in_{n}"].shape, mybir.dt.from_np(arrays[f"in_{n}"].dtype),
                             kind="ExternalInput").ap() for n in laid}
    out = nc.dram_tensor("out", (B, S, D), F32, kind="ExternalOutput").ap()
    hybrid_kernel(nc, aps, out)
    r = run_bass_kernel_spmd(nc, [arrays], core_ids=[0])
    return r.results[0]["out"]
```

```python
from contextlib import ExitStack

import numpy as np

import concourse.bass as bass
from concourse import mybir

F32 = mybir.dt.float32
BF16 = mybir.dt.bfloat16
ALU = mybir.AluOpType
ACT = mybir.ActivationFunctionType
AX = mybir.AxisListType

P = 128
B, S, D = 4, 1024, 128
TT = S // P
HALF = 512
NH = 16
DH = D // NH
WH = 64
E0, F0, K0 = 8, 256, 2
E1, F1, K1 = 16, 64, 4
ROUTE_SCALE = 2.5
BETA, THR, SPIKE_STEPS = 0.95, 1.0, 4
EPS = 1e-5
LIN_N = 512
LIN_K = 2


def firing_thresholds():
    f = np.float32

    def fires(c):
        mem, n = f(0), 0
        for _ in range(SPIKE_STEPS):
            reset = f(mem - f(THR) > 0)
            mem = f(f(f(f(BETA) * mem) + c) - f(reset * f(THR)))
            n += int(f(mem - f(THR)) > 0)
        return n

    found = []
    for k in range(1, SPIKE_STEPS + 1):
        low, high = f(0), f(4)
        while np.nextafter(low, high, dtype=np.float32) < high:
            mid = f((float(low) + float(high)) / 2)
            low, high = (low, mid) if fires(mid) >= k else (mid, high)
        found.append(float(low))
    return found


def hybrid_kernel(nc, A, out):
    ctx = ExitStack()
    with ctx:
        def sb(name, shape, dt=F32):
            return ctx.enter_context(nc.sbuf_tensor(name, shape, dt))

        sems = {}
        turn_of = [0]

        def sem(name):
            key = (name, turn_of[0])
            if key not in sems:
                sems[key] = ctx.enter_context(nc.semaphore(f"{name}_{turn_of[0]}"))
            return sems[key]

        def end_stage(*names):
            for name in names:
                nc.sync.sem_clear(sem(name))
            turn_of[0] ^= 1

        ps = ctx.enter_context(nc.psum_tensor("ps", [P, 8, HALF], F32))

        ident = sb("ident", [P, P])
        head_mask = sb("head_mask", [P, NH])
        pair_mask = sb("pair_mask", [P, 2])
        block_mask = sb("block_mask", [P, P])
        tri = sb("tri", [P, E1, E1])
        expert_rows = sb("expert_rows", [P, E1])
        expert_of_row = sb("expert_of_row", [P, E1 * F1], BF16)
        half_neg = sb("half_neg", [P, TT])
        W = {}
        resident = ["a_qw", "a_kw", "a_vw", "a_ow", "a_qb", "a_kb", "a_vb", "a_ob",
                    "m_router", "m_gate", "m_up", "m_down", "b_gamma",
                    "c_qw", "c_kw", "c_qrw", "c_krw", "c_vw", "c_ow", "c_qb", "c_kb", "c_qrb", "c_krb", "c_vb", "c_ob",
                    "l_qw", "l_kw", "l_vw", "l_ow", "l_qb", "l_kb", "l_vb", "l_ob", "l_g", "l_b",
                    "n_router", "n_bias", "n_gate", "n_up", "n_down", "n_sgate", "n_sup", "n_sdown"]
        for n in resident:
            W[n] = sb("w_" + n, list(A[n].shape))

        x = sb("x", [P, TT, D])
        xn = sb("xn", [P, TT, D])
        xT = sb("xT", [P, S])
        stats = sb("stats", [P, TT, 6])
        meanvar = sb("meanvar", [P, TT, 2])
        rstd = sb("rstd", [P, TT])
        qT = sb("qT", [P, 2, S])
        kT = sb("kT", [P, 2, S])
        v_rows = sb("v_rows", [P, TT, 256])
        rotary_tables = sb("rotary_tables", [P, 2, S])
        q_head_bf = sb("q_head_bf", [P, 2, S], BF16)
        row_rec_all = sb("row_rec_all", [P, NH, TT])
        BIG = 24064
        big = sb("big", [P, BIG])
        RING = 4
        v_wide = big[:, 0:NH * TT * 32].rearrange("p (h t w) -> p h t w", h=NH, w=32)
        outT_all = big[:, 4096:4096 + NH * 256].rearrange("p (h c) -> p h c", c=256)
        ring = big[:, 12288:12288 + RING * S].rearrange("p (n c) -> p n c", c=S)
        o_rows = big[:, 20480:20480 + TT * 256].rearrange("p (t c) -> p t c", c=256)
        counts = big[:, 22528:22528 + S].bitcast(BF16).rearrange("p (n c) -> p n c", c=S)
        qc, kc = counts[:, 0, :], counts[:, 1, :]
        r_s = sb("r_s", [P, TT])
        r_r = sb("r_r", [P, TT])
        r_cmp = big[:, 0:TT * E1 * E1]
        r_eq = big[:, TT * E1 * E1:2 * TT * E1 * E1]
        act_g = big[:, 4096:4096 + 2 * HALF].rearrange("p (a n) -> p a n", a=2)
        fuse = big[:, 5120:5120 + 8 * HALF].rearrange("p (a n) -> p a n", a=8)
        r_a, r_b, r_c, r_w = (big[:, 10240 + k * P:10240 + (k + 1) * P].rearrange("p (t e) -> p t e", e=E1) for k in range(4))
        cos_t, sin_t = rotary_tables[:, 0, :], rotary_tables[:, 1, :]

        x_in = A["x"].rearrange("b (t p) d -> b p t d", p=P)
        x_out = out.rearrange("b (t p) d -> b p t d", p=P)

        def tiles_of(bank, n=TT, w=P):
            per = HALF // w
            k = -(-n // per)
            return ps[:, bank:bank + k, :].rearrange("p k (t w) -> p (k t) w", w=w)[:, 0:n, :]

        LN_SIGNALS = ("ln_stats", "ln_meanvar", "ln_pow", "ln_rows", "ln_transposed", "ln_evacuated")
        LN_BANK = 6

        H = TT // 2

        def norm_statistics(dve, src, k, turn):
            st, mv = sem("ln_stats"), sem("ln_meanvar")
            for t in range(H * k, H * k + H):
                dve.bn_stats(stats[:, t, :], src[:, t, :]).then_inc(st, 1)
            dve.wait_ge(st, H * (turn + 1))
            for t in range(H * k, H * k + H):
                dve.bn_aggr(meanvar[:, t, :], stats[:, t, :]).then_inc(mv, 1)
            dve.wait_ge(mv, H * (turn + 1) + turn)
            dve.tensor_scalar(rstd[:, H * k:H * k + H], meanvar[:, H * k:H * k + H, 1], EPS, None, ALU.add).then_inc(mv, 1)

        def norm_scale(dve, src, dst, k, turn):
            dve.wait_ge(sem("ln_pow"), turn + 1)
            for t in range(H * k, H * k + H):
                dve.tensor_scalar(dst[:, t, :], src[:, t, :], meanvar[:, t, 0:1], rstd[:, t:t + 1],
                                  ALU.subtract, ALU.mult).then_inc(sem("ln_rows"), 1)

        def norm_rows(dve, src, dst, halves=(0, 1)):
            for turn, k in enumerate(halves):
                norm_statistics(dve, src, k, turn)
            for turn, k in enumerate(halves):
                norm_scale(dve, src, dst, k, turn)

        def norm_power(pool, halves=(0, 1)):
            for turn, k in enumerate(halves):
                pool.wait_ge(sem("ln_meanvar"), (H + 1) * (turn + 1))
                pool.tensor_tensor(rstd[:, H * k:H * k + H], rstd[:, H * k:H * k + H], half_neg[:, 0:H],
                                   ALU.pow).then_inc(sem("ln_pow"), 1)

        def norm_transpose(pe, dst, before=0):
            for t in range(TT):
                if t + before >= 0:
                    pe.wait_ge(sem("ln_rows"), t + before + 1)
                pe.transpose(tiles_of(LN_BANK)[:, t, :], dst[:, t, :], ident[:, :]).then_inc(sem("ln_transposed"), 1)

        def norm_evacuate(act, gain=None, bias=None):
            tp, ev = sem("ln_transposed"), sem("ln_evacuated")
            for k in range(2):
                act.wait_ge(tp, H * k + H)
                out_ = xT[:, k * HALF:(k + 1) * HALF]
                if gain is None:
                    act.activation(out_, ps[:, LN_BANK + k, :], ACT.Copy).then_inc(ev, 1)
                elif bias is None:
                    act.activation(out_, ps[:, LN_BANK + k, :], ACT.Identity, scale=gain).then_inc(ev, 1)
                else:
                    act.activation(out_, ps[:, LN_BANK + k, :], ACT.Identity, scale=gain, bias=bias).then_inc(ev, 1)

        def normed_rows_out(src, gain, shift, weight, bias_rows):
            done, added = sem("ro_done"), sem("ro_added")
            with nc.Block() as block:
                @block.gpsimd
                def _(pool):
                    norm_power(pool)

                @block.scalar
                def _(act):
                    norm_evacuate(act, gain, shift)

                @block.tensor
                def _(pe):
                    norm_transpose(pe, xn)
                    for t in range(TT):
                        pe.wait_ge(sem("ln_evacuated"), t // 4 + 1)
                        pe.matmul(tiles_of(2)[:, t, :], xT[:, t * P:(t + 1) * P], weight, start=True, stop=True).then_inc(done, 1)

                @block.vector
                def _(dve):
                    norm_rows(dve, src, xn)
                    dve.tensor_tensor(x[:, :, :], x[:, :, :],
                                      bias_rows[:, :].unsqueeze(1).broadcast_to([P, TT, D]), ALU.add).then_inc(added, 1)
                    dve.wait_ge(added, 1)
                    for k in range(2):
                        dve.wait_ge(done, 4 * k + 4)
                        dve.tensor_tensor(x[:, 4 * k:4 * k + 4, :], x[:, 4 * k:4 * k + 4, :], tiles_of(2 + k, n=4),
                                          ALU.add).then_inc(added, 1)
            end_stage(*LN_SIGNALS, "ro_done", "ro_added")

        def lif_projections(rows):
            mm, cur, ch, vz = sem("lp_products"), sem("lp_current"), sem("lp_chain"), sem("lp_values_set")
            thresholds = firing_thresholds()
            loaded = [sem("x_first"), sem("x_second")]
            with nc.Block() as block:
                @block.sync
                def _(sp):
                    for k in range(2):
                        sp.dma_start(x[:, 4 * k:4 * k + 4, :], rows[:, 4 * k:4 * k + 4, :]).then_inc(loaded[k], 16)
                    sp.wait_ge(loaded[0], 16)
                    sp.wait_ge(loaded[1], 16)

                @block.tensor
                def _(pe):
                    norm_transpose(pe, xn)
                    for n, w in enumerate(("a_qw", "a_kw")):
                        for k in range(2):
                            if n == 0:
                                pe.wait_ge(sem("ln_evacuated"), k + 1)
                            pe.matmul(ps[:, 2 * n + k, :], W[w][:, :], xT[:, k * HALF:(k + 1) * HALF],
                                      start=True, stop=True).then_inc(mm, 1)
                    for t in range(TT):
                        pe.matmul(tiles_of(4)[:, t, :], xT[:, t * P:(t + 1) * P], W["a_vw"][:, :],
                                  start=True, stop=True).then_inc(mm, 1)

                @block.scalar
                def _(act):
                    norm_evacuate(act)
                    for n, b in enumerate(("a_qb", "a_kb")):
                        act.wait_ge(mm, 2 * n + 2)
                        act.activation(qT[:, n, :].rearrange("p (k c) -> p k c", k=2), ps[:, 2 * n:2 * n + 2, :],
                                       ACT.Identity, bias=W[b][:, 0:1]).then_inc(cur, 1)

                @block.vector
                def _(dve):
                    n_chain = 0

                    def chained(ins):
                        nonlocal n_chain
                        n_chain += 1
                        ins.then_inc(ch, 1)
                        dve.wait_ge(ch, n_chain)

                    def neurons(c, counts):
                        chained(dve.tensor_scalar(counts, c, thresholds[0], None, ALU.is_gt))
                        for th in thresholds[1:]:
                            chained(dve.scalar_tensor_tensor(out=counts, in0=c, scalar=th, in1=counts,
                                                             op0=ALU.is_gt, op1=ALU.add))

                    for k in range(2):
                        dve.wait_ge(loaded[k], 16)
                        norm_statistics(dve, x, k, k)
                    for k in range(2):
                        norm_scale(dve, x, xn, k, k)
                    dve.wait_ge(cur, 1)
                    neurons(qT[:, 0, :], qc)
                    dve.wait_ge(cur, 2)
                    neurons(qT[:, 1, :], kc)
                    dve.wait_ge(mm, 4 + TT)
                    chained(dve.tensor_tensor(kT[:, 0, :].rearrange("p (t d) -> p t d", d=D), tiles_of(4),
                                              W["a_vb"][:, :].unsqueeze(1).broadcast_to([P, TT, D]), ALU.add))

                @block.gpsimd
                def _(pool):
                    norm_power(pool)
                    pool.memset(v_wide[:, :, :, DH:32], 0.0).then_inc(vz, 1)
                    pool.wait_ge(vz, 1)
                    pool.memset(v_wide[:, :, :, DH:DH + 1], float(SPIKE_STEPS)).then_inc(vz, 2)
            end_stage(*LN_SIGNALS, "lp_products", "lp_current", "lp_chain", "lp_values_set", "x_first", "x_second")

        def lif_heads():
            names = ("lh_query", "lh_scores", "lh_exp", "lh_sums", "lh_out", "lh_values", "lh_counted")
            qh, sc, ex, pv, oe, vl, ct = (sem(n) for n in names)
            thresholds = firing_thresholds()
            scale = 1.0 / (SPIKE_STEPS * SPIKE_STEPS) / float(DH) ** 0.5
            units = NH * TT
            with nc.Block() as block:
                @block.vector
                def _(dve):
                    for h in range(NH):
                        if h >= 2:
                            dve.wait_ge(sc, TT * (h - 1))
                        dve.tensor_scalar(q_head_bf[:, h % 2, :], qc, head_mask[:, h:h + 1], None, ALU.mult).then_inc(qh, 1)
                        if h == 1:
                            for g in range(TT // 2):
                                c, n = kT[:, 0, 256 * g:256 * g + 256], kT[:, 1, 256 * g:256 * g + 256]
                                for k, th in enumerate(thresholds):
                                    if k == 0:
                                        dve.tensor_scalar(n, c, th, None, ALU.is_gt).then_inc(ct, 1)
                                    else:
                                        dve.wait_ge(ct, SPIKE_STEPS * g + k)
                                        dve.scalar_tensor_tensor(out=n, in0=c, scalar=th, in1=n,
                                                                 op0=ALU.is_gt, op1=ALU.add).then_inc(ct, 1)
                                dve.wait_ge(ct, SPIKE_STEPS * (g + 1))
                                dve.tensor_copy(v_wide[:, :, 2 * g:2 * g + 2, 0:DH].rearrange("p h t d -> p t h d"),
                                                n.rearrange("p (t h d) -> p t h d", h=NH, d=DH)).then_inc(vl, 1)
                        if h >= 2:
                            dve.wait_ge(pv, TT * (h - 1))
                            dve.tensor_copy(outT_all[:, h - 2, :], ps[:, 6 + h % 2, 0:256]).then_inc(oe, 1)
                    for h in range(NH - 2, NH):
                        dve.wait_ge(pv, TT * (h + 1))
                        dve.tensor_copy(outT_all[:, h, :], ps[:, 6 + h % 2, 0:256]).then_inc(oe, 1)

                @block.tensor
                def _(pe):
                    for n in range(units + 2):
                        if n < units:
                            h, kt = divmod(n, TT)
                            if kt == 0:
                                pe.wait_ge(qh, h + 1)
                            if n >= 3:
                                pe.wait_ge(ex, n - 2)
                            for k in range(2):
                                mm = pe.matmul(ps[:, 2 * (n % 3) + k, :], kc[:, kt * P:(kt + 1) * P],
                                               q_head_bf[:, h % 2, k * HALF:(k + 1) * HALF], start=True, stop=True)
                            mm.then_inc(sc, 1)
                        if n >= 2:
                            h, kt = divmod(n - 2, TT)
                            if kt == 0 and h >= 2:
                                pe.wait_ge(oe, h - 1)
                            if h == 0:
                                pe.wait_ge(vl, kt // 2 + 1)
                            pe.wait_ge(ex, n - 1)
                            for c in range(4):
                                mm = pe.matmul(ps[32 * c:32 * c + 32, 6 + h % 2, 0:256], v_wide[:, h, kt, :],
                                               ring[:, (n - 2) % RING, 256 * c:256 * c + 256],
                                               start=(kt == 0), stop=(kt == TT - 1))
                            mm.then_inc(pv, 1)

                @block.scalar
                def _(act):
                    for n in range(units):
                        act.wait_ge(sc, n + 1)
                        if n >= RING:
                            act.wait_ge(pv, n - RING + 1)
                        act.activation(ring[:, n % RING, :].rearrange("p (k c) -> p k c", k=2),
                                       ps[:, 2 * (n % 3):2 * (n % 3) + 2, :], ACT.Exp, scale=scale).then_inc(ex, 1)
            end_stage(*names)

        Q_PARTS = (0, 1, 0, 1, 2, 0)
        K_PARTS = (0, 0, 1, 1, 0, 2)
        PROD = len(Q_PARTS)
        SHIFT = 64
        HB = 4
        AHEAD = TT + 3
        q_scratch = nc.dram_tensor("q_scratch", [NH, PROD, DH, S], BF16, kind="Internal").ap()
        k_scratch = nc.dram_tensor("k_scratch", [NH, PROD, DH, S], BF16, kind="Internal").ap()
        parts = big[:, 4096:4096 + 3072].bitcast(BF16).rearrange("p (n c) -> p n c", c=S)
        q_ops = big[:, 8192:8192 + 2048].bitcast(BF16).rearrange("p (n c) -> p n c", c=S)
        k_ops = big[:, 10240:10240 + 2048].bitcast(BF16).rearrange("p (n c) -> p n c", c=S)
        wideT = big[:, 0:NH * HALF].rearrange("p (h c) -> p h c", c=HALF)
        WB = 4
        k_wide = big[:, 8192:8192 + WB * S].rearrange("p (n c) -> p n c", c=S)
        q_wide = big[:, 16384:16384 + WB * S].rearrange("p (n c) -> p n c", c=S)
        q_wide_bf = big[:, 20480:20480 + S].bitcast(BF16).rearrange("p (n c) -> p n c", c=S)
        k_wide_bf = big[:, 21504:21504 + WB * HALF].bitcast(BF16).rearrange("p (n c) -> p n c", c=S)
        v_pair = v_rows[:, :, :].rearrange("p t c -> p (t c)").rearrange("p (a t c) -> p a t c", a=2, c=P)
        key_acc = kT
        half_max = sb("half_max", [P, 2, TT, 2])
        max_bf = sb("max_bf", [P, 2, TT], BF16)
        shift_z = sb("shift_z", [P, 2, TT, TT], BF16)
        eye8 = sb("eye8", [P, TT, TT])
        ident_bf = sb("ident_bf", [P, P], BF16)

        def rope_projections():
            mm, ra, ro, cp, df, st, zo = (sem(n) for n in ("rp_products", "rp_parts", "rp_rotated", "rp_copied",
                                                           "rp_differences", "rp_stored", "rp_set"))
            todo = (("c_qw", "c_qb", "c_qrw", "c_qrb", qT, 0), ("c_kw", "c_kb", "c_krw", "c_krb", kT, 6))
            part_ready = lambda side, part: (cp, 2 * part + side + 1) if part < 2 else (df, side + 3)

            with nc.Block() as block:
                @block.sync
                def _(sp):
                    for part in range(3):
                        for side, order, scratch in ((0, Q_PARTS, q_scratch), (1, K_PARTS, k_scratch)):
                            sp.wait_ge(*part_ready(side, part))
                            for r in range(PROD):
                                if order[r] == part:
                                    sp.dma_start(scratch[:, r, :, :].rearrange("h d c -> h d c"),
                                                 parts[:, 3 * side + part, :]).then_inc(st, 16)
                    sp.wait_ge(st, 2 * 16 * PROD)

                @block.tensor
                def _(pe):
                    norm_transpose(pe, xn, -H)
                    for n, (w, _, wr, _, _, bank) in enumerate(todo):
                        for m, ww in enumerate((w, wr)):
                            for k in range(2):
                                if n == 0 and m == 0:
                                    pe.wait_ge(sem("ln_evacuated"), k + 1)
                                if n and m:
                                    pe.wait_ge(ra, 1)
                                pe.matmul(ps[:, (bank + 2 * m) % 8 + k, :], W[ww][:, :], xT[:, k * HALF:(k + 1) * HALF],
                                          start=True, stop=True).then_inc(mm, 1)
                    for t in range(TT):
                        pe.matmul(tiles_of(4)[:, t, :], xT[:, t * P:(t + 1) * P], W["c_vw"][:, :],
                                  start=True, stop=True).then_inc(mm, 1)

                @block.vector
                def _(dve):
                    norm_rows(dve, x, xn, (1,))
                    for n, (_, b, _, br, dst, bank) in enumerate(todo):
                        for m, (bb, table) in enumerate(((b, cos_t), (br, sin_t))):
                            at = (bank + 2 * m) % 8
                            dve.wait_ge(mm, 4 * n + 2 * m + 2)
                            dve.scalar_tensor_tensor(out=dst[:, m, :].rearrange("p (k c) -> p k c", k=2),
                                                     in0=ps[:, at:at + 2, :], scalar=W[bb][:, 0:1],
                                                     in1=table.rearrange("p (k c) -> p k c", k=2),
                                                     op0=ALU.add, op1=ALU.mult).then_inc(ra, 1)
                        dve.wait_ge(ra, 2 * n + 2)
                        dve.tensor_tensor(dst[:, 0, :], dst[:, 0, :], dst[:, 1, :], ALU.add).then_inc(ro, 1)
                    for n, whole in enumerate((qT, kT)):
                        dve.wait_ge(cp, n + 1)
                        dve.tensor_tensor(whole[:, 1, :], whole[:, 0, :], parts[:, 3 * n, :], ALU.subtract).then_inc(df, 1)
                    for n, whole in enumerate((qT, kT)):
                        dve.wait_ge(cp, n + 3)
                        dve.tensor_tensor(parts[:, 3 * n + 2, :], whole[:, 1, :], parts[:, 3 * n + 1, :], ALU.subtract).then_inc(df, 1)
                    dve.wait_ge(mm, 8 + TT)
                    dve.tensor_tensor(v_rows[:, :, 0:D], tiles_of(4),
                                      W["c_vb"][:, :].unsqueeze(1).broadcast_to([P, TT, D]), ALU.add).then_inc(ro, 1)
                    dve.wait_ge(ro, 3)
                    dve.wait_ge(zo, 3)
                    dve.tensor_copy(v_wide[:, :, :, 0:DH].rearrange("p h t d -> p t h d"),
                                    v_rows[:, :, 0:D].rearrange("p t (h d) -> p t h d", d=DH)).then_inc(zo, 1)

                @block.gpsimd
                def _(pool):
                    norm_power(pool, (1,))
                    pool.memset(v_wide[:, :, :, DH:32], 0.0).then_inc(zo, 1)
                    pool.wait_ge(zo, 1)
                    pool.memset(v_wide[:, :, :, DH:DH + 1], 1.0).then_inc(zo, 2)
                    pool.memset(k_ops, 0.0).then_inc(sem("rp_cleared"), 1)
                    pool.memset(q_ops, 0.0).then_inc(sem("rp_cleared"), 1)
                    pool.wait_ge(sem("rp_cleared"), 2)
                    pool.memset(k_ops[SHIFT:SHIFT + TT, :, :], 1.0).then_inc(sem("rp_cleared"), 1)

                @block.scalar
                def _(act):
                    norm_evacuate(act)
                    for n, whole in enumerate((qT, kT)):
                        act.wait_ge(ro, n + 1)
                        act.activation(parts[:, 3 * n, :], whole[:, 0, :], ACT.Copy).then_inc(cp, 1)
                    for n, whole in enumerate((qT, kT)):
                        act.wait_ge(df, n + 1)
                        act.activation(parts[:, 3 * n + 1, :], whole[:, 1, :], ACT.Copy).then_inc(cp, 1)
            end_stage(*LN_SIGNALS, "rp_products", "rp_parts", "rp_rotated", "rp_copied", "rp_differences", "rp_stored", "rp_set",
                      "rp_cleared")

        def rotary_heads():
            names = ("ra_loaded_q", "ra_loaded_k", "ra_first", "ra_max", "ra_combined", "ra_shift", "ra_turned", "ra_shifted",
                     "ra_scores", "ra_exp", "ra_sums", "ra_out")
            lq, lk, fs, mx, cb, zs, tn, sh, sc, ex, pv, oe = (sem(n) for n in names)
            units = NH * TT
            turned = ps[SHIFT:SHIFT + TT, 7, :].bitcast(BF16)

            with nc.Block() as block:
                @block.sync
                def _(sp):
                    for h in range(NH):
                        if h >= HB:
                            sp.wait_ge(sc, TT * (h - HB + 1))
                        sp.dma_start(q_ops[0:PROD * DH, h % HB, :], q_scratch[h].rearrange("r d c -> (r d) c")).then_inc(lq, 16)
                        sp.dma_start(k_ops[0:PROD * DH, h % HB, :], k_scratch[h].rearrange("r d c -> (r d) c")).then_inc(lk, 16)
                        sp.wait_ge(lq, 16 * (h + 1))
                        sp.wait_ge(lk, 16 * (h + 1))
                        sp.nop().then_inc(sem("ra_loaded"), 1)

                @block.tensor
                def _(pe):
                    def first_scores(m, half):
                        h, qt = divmod(m, TT)
                        if qt == 0 and half == 0:
                            pe.wait_ge(sem("ra_loaded"), h + 1)
                            if h >= HB:
                                pe.wait_ge(sem("ra_cleared"), h - HB + 1)
                        if m >= 1:
                            pe.wait_ge(mx, 2 * (m - 1) + half + 1)
                        pe.matmul(ps[:, half, :], q_ops[:, h % HB, qt * P:(qt + 1) * P],
                                  k_ops[:, h % HB, half * HALF:(half + 1) * HALF], start=True, stop=True).then_inc(fs, 1)

                    def turn(h):
                        pe.wait_ge(zs, h + 1)
                        for t in range(TT):
                            mm = pe.transpose(turned[:, t * P:(t + 1) * P], shift_z[:, h % 2, t, :], ident_bf[:, :])
                        mm.then_inc(tn, 1)

                    def sums(n):
                        h, kt = divmod(n, TT)
                        if kt == 0 and h >= 1:
                            pe.wait_ge(oe, h)
                        pe.wait_ge(ex, n + 1)
                        for c in range(4):
                            mm = pe.matmul(ps[32 * c:32 * c + 32, 6, 0:256], v_wide[:, h, kt, :],
                                           ring[:, n % RING, 256 * c:256 * c + 256], start=(kt == 0), stop=(kt == TT - 1))
                        mm.then_inc(pv, 1)

                    for n in range(-AHEAD, units + 2):
                        m = n + AHEAD
                        if m < units:
                            first_scores(m, 0)
                        if 0 <= n < units:
                            h, kt = divmod(n, TT)
                            if kt == 0:
                                pe.wait_ge(sh, h + 1)
                            if n >= 2:
                                pe.wait_ge(ex, n - 1)
                            for k in range(2):
                                mm = pe.matmul(ps[:, 2 + 2 * (n % 2) + k, :], k_ops[:, h % HB, kt * P:(kt + 1) * P],
                                               q_ops[:, h % HB, k * HALF:(k + 1) * HALF], start=True, stop=True)
                            mm.then_inc(sc, 1)
                        if m < units:
                            first_scores(m, 1)
                        if m % TT == 0 and 1 <= m // TT <= NH:
                            turn(m // TT - 1)
                        if n >= 2:
                            sums(n - 2)

                @block.vector
                def _(dve):
                    for m in range(units):
                        h, qt = divmod(m, TT)
                        for half in range(2):
                            dve.wait_ge(fs, 2 * m + half + 1)
                            dve.tensor_reduce(half_max[:, h % 2, qt, half:half + 1], ps[:, half, :], AX.X, ALU.max).then_inc(mx, 1)
                        if qt == TT - 1:
                            dve.wait_ge(mx, 2 * m + 2)
                            dve.tensor_reduce(max_bf[:, h % 2, :], half_max[:, h % 2, :, :], AX.X, ALU.max).then_inc(cb, 1)
                            dve.wait_ge(cb, h + 1)
                            if h >= 2:
                                dve.wait_ge(tn, h - 1)
                            dve.scalar_tensor_tensor(out=shift_z[:, h % 2, :, :],
                                                     in0=max_bf[:, h % 2, :].unsqueeze(1).broadcast_to([P, TT, TT]), scalar=-1.0,
                                                     in1=eye8[:, :, :], op0=ALU.mult, op1=ALU.mult).then_inc(zs, 1)

                @block.scalar
                def _(act):
                    def shift_rows(h):
                        act.wait_ge(tn, h + 1)
                        if h >= HB:
                            act.wait_ge(sc, TT * (h - HB + 1))
                        act.activation(q_ops[SHIFT:SHIFT + TT, h % HB, :], turned, ACT.Copy).then_inc(sh, 1)

                    shift_rows(0)
                    for n in range(units + 2):
                        h, kt = divmod(n, TT)
                        if n < units:
                            act.wait_ge(sc, n + 1)
                            if n >= RING:
                                act.wait_ge(pv, n - RING + 1)
                            act.activation(ring[:, n % RING, :].rearrange("p (k c) -> p k c", k=2),
                                           ps[:, 2 + 2 * (n % 2):4 + 2 * (n % 2), :], ACT.Exp, scale=float(DH) ** -0.5).then_inc(ex, 1)
                        if kt == TT + TT - AHEAD and h + 1 < NH:
                            shift_rows(h + 1)
                        if kt == 1 and h >= 1:
                            act.wait_ge(pv, TT * h)
                            act.activation(outT_all[:, h - 1, :], ps[:, 6, 0:256], ACT.Copy).then_inc(oe, 1)
                @block.gpsimd
                def _(pool):
                    for h in range(NH - HB):
                        pool.wait_ge(sc, TT * (h + 1))
                        pool.memset(q_ops[SHIFT:SHIFT + TT, h % HB, :], 0.0).then_inc(sem("ra_cleared"), 1)
            end_stage(*names, "ra_loaded", "ra_cleared")

        def heads_out(weight, bias_rows):
            names = ("ho_transposed", "ho_divided", "ho_turned", "ho_kept", "ho_products", "ho_added")
            tp, ch, tn, kp, mm, ad = (sem(n) for n in names)
            G, per = 4, NH // 4
            heads = tiles_of(0, n=2 * NH)
            with nc.Block() as block:
                @block.tensor
                def _(pe):
                    for h in range(NH):
                        for j in range(2):
                            last = pe.transpose(heads[:, 2 * h + j, :], outT_all[:, h, j * P:(j + 1) * P], ident[:, :])
                        last.then_inc(tp, 1)
                    pe.wait_ge(ch, 3 * G)
                    for t in range(TT):
                        pe.transpose(tiles_of(0)[:, t, :], o_rows[:, t, 0:D], ident[:, :]).then_inc(tn, 1)
                    for t in range(TT):
                        pe.wait_ge(kp, t // 4 + 1)
                        pe.matmul(tiles_of(2)[:, t, :], qT[:, 0, t * P:(t + 1) * P], weight, start=True, stop=True).then_inc(mm, 1)

                @block.vector
                def _(dve):
                    dve.tensor_tensor(x[:, :, :], x[:, :, :], bias_rows[:, :].unsqueeze(1).broadcast_to([P, TT, D]),
                                      ALU.add).then_inc(ad, 1)
                    for g in range(G):
                        dve.wait_ge(tp, per * (g + 1))
                        mine = slice(per * g, per * (g + 1))
                        part = heads[:, 2 * per * g:2 * per * (g + 1), :].rearrange("p (h j) (c w) -> p h j c w", j=2, w=32)
                        rec = row_rec_all[:, mine, :].rearrange("p h (c j) -> p h j c", j=2)
                        dve.reciprocal(rec, part[:, :, :, :, DH]).then_inc(ch, 1)
                        dve.wait_ge(ch, 3 * g + 1)
                        for j in range(2):
                            dst = o_rows[:, :, 0:D].rearrange("p (c j) (h w) -> p h j c w", j=2, w=DH)[:, mine, j, :, :]
                            dve.tensor_tensor(dst, part[:, :, j, :, 0:DH],
                                              rec[:, :, j, :].unsqueeze(3).broadcast_to([P, per, 4, DH]), ALU.mult).then_inc(ch, 1)
                    dve.wait_ge(ad, 1)
                    for k in range(2):
                        dve.wait_ge(mm, 4 * k + 4)
                        dve.tensor_tensor(x[:, 4 * k:4 * k + 4, :], x[:, 4 * k:4 * k + 4, :], tiles_of(2 + k, n=4),
                                          ALU.add).then_inc(ad, 1)

                @block.scalar
                def _(act):
                    for k in range(2):
                        act.wait_ge(tn, 4 * k + 4)
                        act.activation(qT[:, 0, k * HALF:(k + 1) * HALF], ps[:, k, :], ACT.Copy).then_inc(kp, 1)
            end_stage(*names)

        pair_w = sb("pair_w", [P, 2, 3, P])
        null_map = sb("null_map", [P, NH])
        null_scores = sb("null_scores", [P, TT, NH])
        max_all = sb("max_all", [P, NH, TT], BF16)
        raw_max = sb("raw_max", [P, 2, TT])
        key_sums = sb("key_sums", [P, NH, TT])
        null_all = sb("null_all", [P, NH, TT])
        sums_T = sb("sums_T", [P, 256])
        pick = sb("pick", [P, 63])
        WIDE_SCALE = float(WH) ** -0.5

        def null_keys():
            ld, bl, mm = sem("nk_loaded"), sem("nk_blocks"), sem("nk_products")
            wqT = big[:, 0:NH // 2 * D].rearrange("p (a d) -> p a d", d=D)
            nk = big[:, 1024:1024 + NH // 2]
            blocks = big[:, 2048:2048 + NH].rearrange("p (a j) -> p a j", j=2)
            with nc.Block() as block:
                @block.sync
                def _(sp):
                    sp.dma_start(wqT, A["b_qwT"]).then_inc(ld, 16)
                    sp.dma_start(nk, A["b_nk"]).then_inc(ld, 16)

                @block.vector
                def _(dve):
                    dve.memset(pick[:, :], 0.0).then_inc(bl, 1)
                    dve.wait_ge(bl, 1)
                    dve.memset(pick[:, 31:32], 1.0).then_inc(bl, 1)
                    dve.wait_ge(ld, 32)
                    dve.tensor_tensor(blocks, nk.unsqueeze(2).broadcast_to([P, NH // 2, 2]),
                                      pair_mask[:, :].unsqueeze(1).broadcast_to([P, NH // 2, 2]), ALU.mult).then_inc(bl, 1)
                    dve.wait_ge(mm, 1)
                    dve.tensor_copy(null_map[:, :], ps[:, 0, 0:NH]).then_inc(bl, 1)

                @block.tensor
                def _(pe):
                    pe.wait_ge(bl, 3)
                    for a in range(NH // 2):
                        mm_ = pe.matmul(ps[:, 0, 2 * a:2 * a + 2], wqT[:, a, :], blocks[:, a, :], start=True, stop=True)
                    mm_.then_inc(mm, 1)
            end_stage("nk_loaded", "nk_blocks", "nk_products")

        def wide_heads():
            names = ("wa_projected", "wa_placed", "wa_keys_bf", "wa_values", "wa_kept",
                     "wa_set", "wa_null", "wa_first", "wa_max", "wa_combined", "wa_shift", "wa_turned", "wa_shifted",
                     "wa_scores", "wa_exp", "wa_sums", "wa_out", "wa_added", "wa_key_sums", "wa_null_kept")
            wl = [sem("wa_weights_even"), sem("wa_weights_odd")]
            (ck, pl, kb, vv, kp, zr, nl, fs, mx, cb, zs, tn, sh, sc, ex, pv, oe, ad, ks, nk) = (sem(n) for n in names)
            units = NH * TT
            pairs = NH // 2
            AT = {-16: 0, -15: 1, -14: 2, -13: 3, -10: 4, -9: 5}
            START = -16

            def chunks_at(n):
                return [(i, c) for o, c in AT.items() for i in range(pairs) if 2 * TT * i + o == n]

            def chunk_bank(i, c):
                return 2 + c if i == 0 and c < 4 else 7

            def rows_of(j):
                return slice(WH * j, WH * j + WH)

            def turned(h):
                base = WH * (1 - h % 2)
                return ps[base:base + TT, 7, :].bitcast(BF16), q_wide[base:base + TT, h % WB, :]

            slots = range(START, units + 3)

            with nc.Block() as block:
                @block.sync
                def _(sp):
                    for i in range(pairs):
                        if i >= 2:
                            sp.wait_ge(ck, 6 * (i - 1))
                        sp.dma_start(pair_w[:, i % 2, :, :], A["b_pw"][:, i, :, :]).then_inc(wl[i % 2], 16)
                    for odd in range(2):
                        sp.wait_ge(wl[odd], 16 * (pairs // 2))

                @block.gpsimd
                def _(pool):
                    norm_power(pool, (1, 0, 1))
                    pool.wait_ge(sem("ln_pow"), 3)
                    for b in range(WB):
                        pool.memset(k_wide_bf[rows_of(1 - b % 2), b, :], 0.0).then_inc(zr, 1)
                    for b in range(WB):
                        pool.memset(k_wide[rows_of(1 - b % 2), b, :], 1.0).then_inc(zr, 1)
                        pool.memset(q_wide[rows_of(1 - b % 2), b, :], 0.0).then_inc(zr, 1)

                @block.tensor
                def _(pe):
                    readers_of_7 = []

                    def bank7(*readers):
                        for signal, count in readers_of_7:
                            pe.wait_ge(signal, count)
                        readers_of_7[:] = readers

                    def chunk(i, c):
                        if c == 0:
                            pe.wait_ge(wl[i % 2], 16 * (i // 2 + 1))
                        if i == 0 and c < 2:
                            pe.wait_ge(sem("ln_evacuated"), c + 1)
                        if c >= 4:
                            bank7((vv, 2 * i + c - 3))
                        elif i:
                            bank7((pl, 10 * i + (2, 4, 7, 10)[c]))
                        if c < 4:
                            pe.matmul(ps[:, chunk_bank(i, c), :], pair_w[:, i % 2, 1 - c // 2, :],
                                      xT[:, (c % 2) * HALF:(c % 2 + 1) * HALF], start=True, stop=True).then_inc(ck, 1)
                        else:
                            for t in range(4):
                                k = 4 * (c - 4) + t
                                mm = pe.matmul(ps[:, 7, t * P:(t + 1) * P], xT[:, k * P:(k + 1) * P], pair_w[:, i % 2, 2, :],
                                               start=True, stop=True)
                            mm.then_inc(ck, 1)

                    def first_scores(m, half):
                        h, qt = divmod(m, TT)
                        if m == 0 and half == 0:
                            pe.wait_ge(zr, WB)
                        if h % 2 == 0 and qt == 0 and half == 0:
                            pe.wait_ge(pl, 10 * (h // 2 + 1))
                            pe.wait_ge(kb, 4 * (h // 2 + 1))
                        if m >= 1:
                            pe.wait_ge(mx, 2 * (m - 1) + half + 1)
                        pe.matmul(ps[:, half, :], q_wide_bf[:, (h // 2) % 2, qt * P:(qt + 1) * P],
                                  k_wide_bf[:, h % WB, half * HALF:(half + 1) * HALF], start=True, stop=True).then_inc(fs, 1)

                    def turn(h):
                        pe.wait_ge(zs, h + 1)
                        bank7((sh, h + 1))
                        for t in range(TT):
                            mm = pe.transpose(turned(h)[0][:, t * P:(t + 1) * P], shift_z[:, h % 2, t, :], ident_bf[:, :])
                        mm.then_inc(tn, 1)

                    def sums(n):
                        h, kt = divmod(n, TT)
                        if kt == 0:
                            pe.wait_ge(vv, 2 * (h // 2) + 2)
                            if h >= 1:
                                pe.wait_ge(oe, h)
                        pe.wait_ge(ex, n + 1)
                        for c in range(2):
                            mm = pe.matmul(ps[rows_of(c), 6, :], v_pair[:, (h // 2) % 2, kt, rows_of(h % 2)],
                                           ring[:, n % RING, HALF * c:HALF * c + HALF], start=(kt == 0), stop=(kt == TT - 1))
                        mm.then_inc(pv, 1)

                    def across(h):
                        pe.wait_ge(ad, (TT - 1) * (h + 1))
                        bank7((kp, h + 1))
                        for c in range(4):
                            mm = pe.matmul(ps[32 * c:32 * c + 32, 7, 0:256], pick[:, 31 - h:63 - h],
                                           key_acc[:, h % 2, 256 * c:256 * c + 256], start=True, stop=True)
                        mm.then_inc(ks, 1)

                    norm_transpose(pe, xn, H)
                    for n in slots:
                        m = n + AHEAD
                        for i, c in chunks_at(n):
                            chunk(i, c)
                        if n == START + 4:
                            bank7((nk, 1))
                            for t in range(TT):
                                mm = pe.matmul(tiles_of(7, w=NH)[:, t, :], xT[:, t * P:(t + 1) * P], null_map[:, :],
                                               start=True, stop=True)
                            mm.then_inc(nl, 1)
                        if 0 <= m < units:
                            first_scores(m, 0)
                        if 0 <= n < units:
                            h, kt = divmod(n, TT)
                            if n == 0:
                                pe.wait_ge(zr, 3 * WB)
                            if kt == 0:
                                pe.wait_ge(sh, h + 1)
                            if n >= 2:
                                pe.wait_ge(ex, n - 1)
                            for k in range(2):
                                mm = pe.matmul(ps[:, 2 + 2 * (n % 2) + k, :], k_wide[:, h % WB, kt * P:(kt + 1) * P],
                                               q_wide[:, h % WB, k * HALF:(k + 1) * HALF], start=True, stop=True)
                            mm.then_inc(sc, 1)
                        if 0 <= m < units:
                            first_scores(m, 1)
                        if m >= TT and m % TT == 0 and m // TT <= NH:
                            turn(m // TT - 1)
                        if 2 <= n < units + 2:
                            sums(n - 2)
                        if n >= TT + 1 and n % TT == 1:
                            across(n // TT - 1)

                @block.vector
                def _(dve):
                    norm_statistics(dve, x, 1, 0)
                    norm_statistics(dve, xn, 0, 1)
                    norm_scale(dve, x, xn, 1, 0)
                    norm_scale(dve, xn, xn, 0, 1)
                    dve.wait_ge(sem("ln_rows"), H)
                    norm_statistics(dve, xn, 1, 2)
                    norm_scale(dve, xn, xn, 1, 2)
                    for n in slots:
                        m = n + AHEAD
                        for i, c in chunks_at(n):
                            if c < 2:
                                if i >= 2:
                                    dve.wait_ge(fs, 4 * TT * (i - 1))
                                half = slice(c * HALF, (c + 1) * HALF)
                                for j in range(2):
                                    dve.wait_ge(pl, 10 * i + 2 * c + j + 1)
                                    dve.tensor_copy(k_wide_bf[rows_of(j), (2 * i + j) % WB, half],
                                                    k_wide[rows_of(j), (2 * i + j) % WB, half]).then_inc(kb, 1)
                        if n == START + 4:
                            dve.wait_ge(nl, 1)
                            dve.tensor_copy(null_scores[:, :, :], tiles_of(7, w=NH)).then_inc(nk, 1)
                        if 0 <= m < units:
                            h, qt = divmod(m, TT)
                            for half in range(2):
                                dve.wait_ge(fs, 2 * m + half + 1)
                                dve.tensor_reduce(half_max[:, h % 2, qt, half:half + 1], ps[:, half, :], AX.X, ALU.max).then_inc(mx, 1)
                            if qt == TT - 1:
                                dve.wait_ge(mx, 2 * m + 2)
                                dve.tensor_reduce(raw_max[:, h % 2, :], half_max[:, h % 2, :, :], AX.X, ALU.max).then_inc(cb, 1)
                                dve.wait_ge(cb, 2 * h + 1)
                                if h == 0:
                                    dve.wait_ge(nk, 1)
                                dve.tensor_tensor(max_all[:, h, :], raw_max[:, h % 2, :], null_scores[:, :, h], ALU.max).then_inc(cb, 1)
                                dve.wait_ge(cb, 2 * h + 2)
                                if h >= 2:
                                    dve.wait_ge(tn, h - 1)
                                dve.scalar_tensor_tensor(out=shift_z[:, h % 2, :, :],
                                                         in0=max_all[:, h, :].unsqueeze(1).broadcast_to([P, TT, TT]), scalar=-1.0,
                                                         in1=eye8[:, :, :], op0=ALU.mult, op1=ALU.mult).then_inc(zs, 1)
                        if 1 <= n <= units:
                            h, kt = divmod(n - 1, TT)
                            if kt >= 1:
                                if kt == 1 and h >= 2:
                                    dve.wait_ge(ks, h - 1)
                                dve.wait_ge(ex, n)
                                if kt >= 2:
                                    dve.wait_ge(ad, (TT - 1) * h + kt - 1)
                                first = ring[:, (n - 2) % RING, :] if kt == 1 else key_acc[:, h % 2, :]
                                dve.tensor_tensor(key_acc[:, h % 2, :], first, ring[:, (n - 1) % RING, :], ALU.add).then_inc(ad, 1)
                        if n >= TT + 1 and n % TT == 1:
                            h = n // TT - 1
                            dve.wait_ge(ks, h + 1)
                            if h == 0:
                                dve.tensor_copy(sums_T[:, :], ps[:, 7, 0:256]).then_inc(kp, 1)
                            else:
                                dve.wait_ge(kp, h)
                                dve.tensor_tensor(sums_T[:, :], sums_T[:, :], ps[:, 7, 0:256], ALU.add).then_inc(kp, 1)

                @block.scalar
                def _(act):
                    norm_evacuate(act, W["b_gamma"][:, 0:1])
                    for n in slots:
                        m = n + AHEAD
                        for i, c in chunks_at(n):
                            act.wait_ge(ck, 6 * i + c + 1)
                            if c < 4:
                                half = slice((c % 2) * HALF, (c % 2 + 1) * HALF)
                                if i >= 2:
                                    act.wait_ge(sc, 2 * TT * (i - 1))
                                if c >= 2:
                                    if i >= 2:
                                        act.wait_ge(fs, 4 * TT * (i - 1))
                                    act.activation(q_wide_bf[:, i % 2, half], ps[:, chunk_bank(i, c), :], ACT.Copy).then_inc(pl, 1)
                                for j in range(2):
                                    act.activation((k_wide, q_wide)[c // 2][rows_of(j), (2 * i + j) % WB, half],
                                                   ps[rows_of(j), chunk_bank(i, c), :], ACT.Copy).then_inc(pl, 1)
                            else:
                                if c == 4 and i >= 2:
                                    act.wait_ge(pv, 2 * TT * (i - 1))
                                act.activation(v_pair[:, i % 2, 4 * (c - 4):4 * (c - 4) + 4, :],
                                               ps[:, 7, :].rearrange("p (t c) -> p t c", c=P), ACT.Copy).then_inc(vv, 1)
                        if 0 <= n < units:
                            h, kt = divmod(n, TT)
                            act.wait_ge(sc, n + 1)
                            if n >= RING:
                                hr, kr = divmod(n - RING, TT)
                                act.wait_ge(pv, n - RING + 1)
                                act.wait_ge(ad, (TT - 1) * hr + max(kr, 1))
                            act.activation(ring[:, n % RING, :].rearrange("p (k c) -> p k c", k=2),
                                           ps[:, 2 + 2 * (n % 2):4 + 2 * (n % 2), :], ACT.Exp, scale=WIDE_SCALE).then_inc(ex, 1)
                        if m >= TT and m % TT == 0 and m // TT <= NH:
                            h = m // TT - 1
                            act.wait_ge(tn, h + 1)
                            if h == 0:
                                act.wait_ge(zr, 3 * WB)
                            if h >= WB:
                                act.wait_ge(sc, TT * (h - WB + 1))
                            act.activation(turned(h)[1], turned(h)[0], ACT.Copy).then_inc(sh, 1)
                        if n % TT == 1 and n >= TT + 1:
                            h = n // TT - 1
                            act.wait_ge(pv, TT * (h + 1))
                            act.activation(wideT[:, h, :], ps[:, 6, :], ACT.Copy).then_inc(oe, 1)
            end_stage(*LN_SIGNALS, *names, "wa_weights_even", "wa_weights_odd")

        def wide_out():
            names = ("wo_null_ready", "wo_null_exp", "wo_loaded", "wo_share", "wo_rows", "wo_added", "wo_scaled",
                     "wo_turned", "wo_kept", "wo_out", "wo_sums")
            ch, ex, wl, nn, tp, ad, ro, tn, kp, ot, sm = (sem(n) for n in names)
            null_v = big[:, 16384:16384 + NH * WH]
            out_w = big[:, 17408:17408 + S].rearrange("p (a d) -> p a d", d=D)
            share = big[:, 18432:18432 + 4 * HALF].rearrange("p (n t w) -> p n t w", n=4, w=WH)
            pair_rows = o_rows[:, :, :].rearrange("p t c -> p (t c)").rearrange("p (a t c) -> p a t c", a=2, c=P)
            pairs = NH // 2
            with nc.Block() as block:
                @block.sync
                def _(sp):
                    sp.dma_start(null_v, A["b_nv"]).then_inc(wl, 16)
                    sp.dma_start(out_w, A["b_ow"]).then_inc(wl, 16)
                    sp.wait_ge(wl, 32)

                @block.tensor
                def _(pe):
                    def to_rows(h):
                        if h >= 2:
                            pe.wait_ge(ad, h - 1)
                        for j in range(4):
                            mm = pe.transpose(ps[:, h % 2, j * P:(j + 1) * P], wideT[:, h, j * P:(j + 1) * P], ident[:, :])
                        mm.then_inc(tp, 1)

                    def to_columns(a):
                        pe.wait_ge(ro, 2 * a + 2)
                        if a >= 1:
                            pe.wait_ge(kp, 2 * a)
                        for k in range(2):
                            for t in range(4):
                                mm = pe.transpose(ps[:, 2 + k, t * P:(t + 1) * P], pair_rows[:, a % 2, 4 * k + t, :], ident[:, :])
                            mm.then_inc(tn, 1)

                    def multiply(a):
                        pe.wait_ge(kp, 2 * a + 2)
                        if a == 0:
                            pe.wait_ge(wl, 32)
                        for t in range(TT):
                            mm = pe.matmul(tiles_of(4)[:, t, :], qT[:, a % 2, t * P:(t + 1) * P], out_w[:, a, :],
                                           start=(a == 0 and t % 4 == 0), stop=(a == pairs - 1), skip_group_check=True)
                        mm.then_inc(ot, 1)

                    for j in range(2):
                        mm_ = pe.transpose(ps[:, 6, j * P:(j + 1) * P], sums_T[:, j * P:(j + 1) * P], ident[:, :])
                    mm_.then_inc(sm, 1)
                    to_rows(0)
                    to_rows(1)
                    for a in range(pairs + 1):
                        for h in (2 * a + 2, 2 * a + 3):
                            if h < NH:
                                to_rows(h)
                        if a < pairs:
                            to_columns(a)
                        if a >= 1:
                            multiply(a - 1)

                @block.gpsimd
                def _(pool):
                    pool.wait_ge(wl, 32)
                    pool.wait_ge(ex, 1)
                    for h in range(NH):
                        if h >= 4:
                            pool.wait_ge(ro, h - 3)
                        pool.tensor_tensor(share[:, h % 4, :, :], null_all[:, h, :].unsqueeze(2).broadcast_to([P, TT, WH]),
                                           null_v[:, h * WH:(h + 1) * WH].unsqueeze(1).broadcast_to([P, TT, WH]),
                                           ALU.mult).then_inc(nn, 1)

                @block.vector
                def _(dve):
                    dve.tensor_tensor(null_all[:, :, :], null_scores[:, :, :].rearrange("p t h -> p h t"), max_all[:, :, :],
                                      ALU.subtract).then_inc(ch, 1)
                    dve.wait_ge(ex, 1)
                    dve.wait_ge(sm, 1)
                    for j in range(2):
                        by_head = lambda v: v[:, :, :].rearrange("p h (c j) -> p h c j", j=2)[:, :, :, j]
                        dve.tensor_tensor(by_head(key_sums), ps[:, 6, j * P:(j + 1) * P].rearrange("p (c h) -> p h c", h=32)[:, 0:NH, :],
                                          by_head(null_all), ALU.add).then_inc(ch, 1)
                    dve.wait_ge(ch, 3)
                    dve.reciprocal(row_rec_all[:, :, :], key_sums[:, :, :]).then_inc(ch, 1)
                    dve.wait_ge(ch, 4)
                    for h in range(NH):
                        a, j = divmod(h, 2)
                        dve.wait_ge(tp, h + 1)
                        dve.wait_ge(nn, h + 1)
                        part = ps[:, h % 2, :].rearrange("p (j c w) -> p c j w", j=4, c=2)
                        mine = share[:, h % 4, :, :]
                        m4 = mine.rearrange("p (c j) w -> p c j w", c=2)
                        dve.tensor_tensor(m4, part, m4, ALU.add).then_inc(ad, 1)
                        dve.wait_ge(ad, h + 1)
                        if j == 0 and a >= 2:
                            dve.wait_ge(tn, 2 * (a - 1))
                        dve.tensor_tensor(pair_rows[:, a % 2, :, j * WH:(j + 1) * WH], mine,
                                          row_rec_all[:, h, :].unsqueeze(2).broadcast_to([P, TT, WH]),
                                          ALU.mult).then_inc(ro, 1)
                    dve.wait_ge(ot, pairs)
                    dve.tensor_tensor(x[:, :, :], x[:, :, :], tiles_of(4), ALU.add).then_inc(ch, 1)

                @block.scalar
                def _(act):
                    act.wait_ge(ch, 1)
                    act.activation(null_all[:, :, :], null_all[:, :, :], ACT.Exp, scale=WIDE_SCALE).then_inc(ex, 1)
                    for a in range(pairs):
                        if a >= 2:
                            act.wait_ge(ot, a - 1)
                        for k in range(2):
                            act.wait_ge(tn, 2 * a + k + 1)
                            act.activation(qT[:, a % 2, k * HALF:(k + 1) * HALF], ps[:, 2 + k, :], ACT.Copy).then_inc(kp, 1)
            end_stage(*names)

        EXPERT_SIGNALS = ("rt_logits", "rt_chain", "rt_exp", "ex_gate", "ex_up", "ex_silu", "ex_fused",
                          "ex_down", "ex_added")
        FB = 8
        ROUTER_BANK = 7

        def logits(pe, router, n_e):
            pe.wait_ge(sem("ln_evacuated"), 2)
            lg = tiles_of(ROUTER_BANK, w=n_e)
            for t in range(TT):
                last = pe.matmul(lg[:, t, :], xT[:, t * P:(t + 1) * P], router, start=True, stop=True)
            last.then_inc(sem("rt_logits"), 1)

        def ranks_of(vals, n_e):
            shape = [P, TT, n_e, n_e]
            cmp4 = r_cmp[:, 0:TT * n_e * n_e].rearrange("p (t e f) -> p t e f", t=TT, e=n_e)
            eq4 = r_eq[:, 0:TT * n_e * n_e].rearrange("p (t e f) -> p t e f", t=TT, e=n_e)
            return cmp4, eq4, vals.unsqueeze(2).broadcast_to(shape), vals.unsqueeze(3).broadcast_to(shape)

        def compare(dve, step, n0, vals, n_e):
            cmp4, eq4, other, own = ranks_of(vals, n_e)
            ch = sem("rt_chain")
            if step == 1:
                dve.tensor_tensor(eq4, other, own, ALU.is_equal).then_inc(ch, 1)
            elif step == 2:
                dve.tensor_tensor(cmp4, other, own, ALU.is_gt).then_inc(ch, 1)
            elif step == 3:
                dve.wait_ge(ch, n0 + 1)
                dve.tensor_tensor(eq4, eq4, tri[:, 0:n_e, 0:n_e].unsqueeze(1).broadcast_to([P, TT, n_e, n_e]),
                                  ALU.mult).then_inc(ch, 1)
            else:
                dve.wait_ge(ch, n0 + 3)
                dve.tensor_tensor(cmp4, cmp4, eq4, ALU.add).then_inc(ch, 1)

        def chosen(dve, n0, vals, n_e, top):
            cmp4 = ranks_of(vals, n_e)[0]
            ch = sem("rt_chain")
            dve.wait_ge(ch, n0)
            dve.tensor_reduce(r_c[:, :, 0:n_e], cmp4, AX.X, ALU.add).then_inc(ch, 1)
            dve.wait_ge(ch, n0 + 1)
            dve.tensor_scalar(r_c[:, :, 0:n_e], r_c[:, :, 0:n_e], float(top) - 0.5, None, ALU.is_lt).then_inc(ch, 1)
            dve.wait_ge(ch, n0 + 2)

        def experts_first():
            gt, up, si, fu, dn, ad = (sem(n) for n in ("ex_gate", "ex_up", "ex_silu", "ex_fused", "ex_down", "ex_added"))
            mm, ch, ex = sem("rt_logits"), sem("rt_chain"), sem("rt_exp")
            lg = tiles_of(ROUTER_BANK, w=E0)
            a, b = r_a[:, :, 0:E0], r_b[:, :, 0:E0]
            wide = lambda v: v[:, :].unsqueeze(2).broadcast_to([P, TT, E0])
            steps = 2 * E0 * (F0 // P)
            LAG = 6
            with nc.Block() as block:
                @block.tensor
                def _(pe):
                    def down(m):
                        pe.wait_ge(fu, 2 * m + 2)
                        if m >= 4:
                            pe.wait_ge(ad, 4 * (m - 3))
                        for s in range(4):
                            for f in range(2):
                                mm_ = pe.matmul(ps[:, 4 + m % 4, s * P:(s + 1) * P],
                                                fuse[:, (2 * m + f) % FB, s * P:(s + 1) * P],
                                                W["m_down"][:, 2 * (m % E0) + f, :], start=(f == 0), stop=(f == 1))
                        mm_.then_inc(dn, 1)

                    norm_transpose(pe, xn)
                    for n in range(steps):
                        blk, e, f = n // (2 * E0), (n // 2) % E0, n % 2
                        if n == 0:
                            pe.wait_ge(sem("ln_evacuated"), 1)
                        if n >= 2:
                            pe.wait_ge(si, n - 1)
                            pe.wait_ge(fu, n - 1)
                        for m, w in enumerate(("m_gate", "m_up")):
                            pe.matmul(ps[:, 2 * m + n % 2, :], W[w][:, e * F0 + f * P:e * F0 + (f + 1) * P],
                                      xT[:, blk * HALF:(blk + 1) * HALF], start=True, stop=True).then_inc((gt, up)[m], 1)
                        if n == 1:
                            logits(pe, W["m_router"][:, :], E0)
                        if n % 2 == 0 and n >= LAG:
                            down((n - LAG) // 2)
                    for m in range((steps - LAG) // 2, steps // 2):
                        down(m)

                @block.gpsimd
                def _(pool):
                    norm_power(pool, (0, 1, 0))

                @block.scalar
                def _(act):
                    norm_evacuate(act)
                    for n in range(steps):
                        act.wait_ge(gt, n + 1)
                        if n >= 2:
                            act.wait_ge(fu, n - 1)
                        act.activation(act_g[:, n % 2, :], ps[:, n % 2, :], ACT.Silu).then_inc(si, 1)
                        if n == 1:
                            act.wait_ge(ch, 2)
                            act.activation(b, a, ACT.Exp).then_inc(ex, 1)
                        if n == 3:
                            act.wait_ge(ch, 5)
                            act.activation(b, a, ACT.Exp).then_inc(ex, 1)

                @block.vector
                def _(dve):
                    def fuse_step(n):
                        dve.wait_ge(si, n + 1)
                        dve.wait_ge(up, n + 1)
                        if n >= FB:
                            dve.wait_ge(dn, (n - FB) // 2 + 1)
                        dve.tensor_tensor(fuse[:, n % FB, :], act_g[:, n % 2, :], ps[:, 2 + n % 2, :], ALU.mult).then_inc(fu, 1)

                    def add(m):
                        dve.wait_ge(dn, m + 1)
                        e = m % E0
                        for s in range(4):
                            t = 4 * (m // E0) + s
                            if m % E0:
                                dve.wait_ge(ad, 4 * (m - 1) + s + 1)
                            dve.scalar_tensor_tensor(out=x[:, t, :], in0=ps[:, 4 + m % 4, s * P:(s + 1) * P],
                                                     scalar=r_w[:, t, e:e + 1], in1=x[:, t, :],
                                                     op0=ALU.mult, op1=ALU.add).then_inc(ad, 1)

                    norm_rows(dve, x, xn)
                    fuse_step(0)
                    fuse_step(1)
                    dve.wait_ge(mm, 1)
                    dve.tensor_reduce(r_s[:, :], lg, AX.X, ALU.max).then_inc(ch, 1)
                    dve.wait_ge(ch, 1)
                    dve.tensor_tensor(a, lg, wide(r_s), ALU.subtract).then_inc(ch, 1)
                    fuse_step(2)
                    dve.wait_ge(ex, 1)
                    dve.tensor_reduce(r_s[:, :], b, AX.X, ALU.add).then_inc(ch, 1)
                    dve.wait_ge(ch, 3)
                    dve.reciprocal(r_r[:, :], r_s[:, :]).then_inc(ch, 1)
                    dve.wait_ge(ch, 4)
                    dve.tensor_tensor(a, b, wide(r_r), ALU.mult).then_inc(ch, 1)
                    fuse_step(3)
                    dve.wait_ge(ch, 5)
                    for step in range(1, 5):
                        compare(dve, step, 5, a, E0)
                    fuse_step(4)
                    fuse_step(5)
                    chosen(dve, 9, a, E0, K0)
                    dve.wait_ge(ex, 2)
                    dve.tensor_tensor(b, b, r_c[:, :, 0:E0], ALU.mult).then_inc(ch, 1)
                    dve.wait_ge(ch, 12)
                    dve.tensor_reduce(r_s[:, :], b, AX.X, ALU.add).then_inc(ch, 1)
                    dve.wait_ge(ch, 13)
                    dve.reciprocal(r_r[:, :], r_s[:, :]).then_inc(ch, 1)
                    dve.wait_ge(ch, 14)
                    dve.tensor_tensor(r_w[:, :, 0:E0], b, wide(r_r), ALU.mult).then_inc(ch, 1)
                    fuse_step(6)
                    dve.wait_ge(ch, 15)
                    for n in range(LAG + 1, steps):
                        fuse_step(n)
                        if n % 2 == 1:
                            add((n - LAG - 1) // 2)
                        if n == 2 * E0 + LAG:
                            dve.wait_ge(ad, 4 * E0)
                            norm_statistics(dve, x, 0, 2)
                        if n == 2 * E0 + LAG + 2:
                            norm_scale(dve, x, xn, 0, 2)
                    for m in range((steps - LAG) // 2, steps // 2):
                        add(m)
            end_stage(*LN_SIGNALS, *EXPERT_SIGNALS)

        def experts_second(store_to=None):
            gt, up, si, fu, dn = (sem(n) for n in ("ex_gate", "ex_up", "ex_silu", "ex_fused", "ex_down"))
            sp_, sd = sem("ex_spread"), sem("ex_scaled")
            mm, ch, ex = sem("rt_logits"), sem("rt_chain"), sem("rt_exp")
            lg = tiles_of(ROUTER_BANK, w=E1)
            pairs = E1 // 2 + 1
            steps = 2 * pairs
            LAG, BUFS = 10, 12
            acts = big[:, 12288:12288 + BUFS * HALF].rearrange("p (a n) -> p a n", a=BUFS)
            w_parts = big[:, 10752:10752 + TT * 3 * E1 // 2].bitcast(BF16).rearrange("p (t k e) -> p t k e", t=TT, k=3)
            w_turned = big[:, 11264:11264 + S // 2].bitcast(BF16)
            turned = ps[0:3 * E1, ROUTER_BANK, :].bitcast(BF16)
            shared = lambda n: n % pairs == pairs - 1
            scaled_before = lambda n: n - n // pairs
            with nc.Block() as block:
                if store_to is not None:
                    @block.sync
                    def _(sp):
                        for k in range(2):
                            sp.wait_ge(sem("ex_sum"), k + 1)
                            sp.dma_start(store_to[:, 4 * k:4 * k + 4, :], x[:, 4 * k:4 * k + 4, :]).then_inc(sem("x_out"), 16)
                        sp.wait_ge(sem("x_out"), 32)

                @block.tensor
                def _(pe):
                    def spread(n):
                        blk, k = divmod(n, pairs)
                        c = scaled_before(n)
                        if c >= 2:
                            pe.wait_ge(sd, c - 1)
                        if n == 0:
                            pe.wait_ge(sem("rt_kept"), 1)
                        pe.matmul(ps[:, 6 + c % 2, :], expert_of_row[:, k * P:(k + 1) * P],
                                  w_turned[:, blk * HALF:(blk + 1) * HALF], start=True, stop=True).then_inc(sp_, 1)

                    def down(n):
                        blk, k = divmod(n, pairs)
                        rows = F1 if shared(n) else P
                        if shared(n):
                            pe.wait_ge(fu, n + 1)
                        else:
                            pe.wait_ge(sd, scaled_before(n) + 1)
                        for s in range(4):
                            mm_ = pe.matmul(ps[:, 4 + blk, s * P:(s + 1) * P], acts[0:rows, n % BUFS, s * P:(s + 1) * P],
                                            W["n_sdown"][:, :] if shared(n) else W["n_down"][:, k, :],
                                            start=(k == 0 and s == 0), stop=(k == pairs - 1), skip_group_check=True)
                        mm_.then_inc(dn, 1)

                    norm_transpose(pe, xn)
                    for n in range(steps + LAG):
                        blk, k = divmod(n, pairs)
                        if n == 0:
                            pe.wait_ge(sem("ln_evacuated"), 1)
                        if n < steps:
                            if n >= 2:
                                pe.wait_ge(si, n - 1)
                                pe.wait_ge(fu, n - 1)
                            for m, (w, ws) in enumerate((("n_gate", "n_sgate"), ("n_up", "n_sup"))):
                                lhs = W[ws][:, :] if shared(n) else W[w][:, k * P:(k + 1) * P]
                                pe.matmul(ps[0:F1 if shared(n) else P, 2 * m + n % 2, :], lhs, xT[:, blk * HALF:(blk + 1) * HALF],
                                          start=True, stop=True).then_inc((gt, up)[m], 1)
                        if n == 0:
                            logits(pe, W["n_router"][:, :], E1)
                        if n == LAG - 1:
                            pe.wait_ge(ch, 17)
                            for t in range(TT):
                                mm_ = pe.transpose(turned[:, t * P:(t + 1) * P], w_parts[:, t, :, :].rearrange("p k e -> p (k e)"),
                                                   ident_bf[:, :])
                            mm_.then_inc(sem("rt_turned"), 1)
                        if LAG - 1 <= n and n - LAG + 1 < steps and not shared(n - LAG + 1):
                            spread(n - LAG + 1)
                        if n >= LAG:
                            down(n - LAG)

                @block.gpsimd
                def _(pool):
                    pool.memset(w_turned, 0.0).then_inc(sem("rt_zeroed"), 1)
                    norm_power(pool, (0, 1, 0) if store_to is None else (0, 1))

                @block.scalar
                def _(act):
                    norm_evacuate(act)
                    for n in range(steps):
                        rows = F1 if shared(n) else P
                        act.wait_ge(gt, n + 1)
                        if n >= 2:
                            act.wait_ge(fu, n - 1)
                        act.activation(act_g[0:rows, n % 2, :], ps[0:rows, n % 2, :], ACT.Silu).then_inc(si, 1)
                        if n == 0:
                            act.wait_ge(mm, 1)
                            act.activation(r_a[:, :, :], lg, ACT.Exp, scale=-1.0).then_inc(ex, 1)
                        if n == LAG - 1:
                            act.wait_ge(sem("rt_turned"), 1)
                            act.wait_ge(sem("rt_zeroed"), 1)
                            act.activation(w_turned[0:3 * E1, :], turned, ACT.Copy).then_inc(sem("rt_kept"), 1)

                @block.vector
                def _(dve):
                    def fuse_step(n):
                        rows = F1 if shared(n) else P
                        dve.wait_ge(si, n + 1)
                        dve.wait_ge(up, n + 1)
                        if n >= BUFS:
                            dve.wait_ge(dn, n - BUFS + 1)
                        dve.tensor_tensor(acts[0:rows, n % BUFS, :], act_g[0:rows, n % 2, :], ps[0:rows, 2 + n % 2, :],
                                          ALU.mult).then_inc(fu, 1)

                    def scale_step(n):
                        c = scaled_before(n)
                        dve.wait_ge(sp_, c + 1)
                        dve.wait_ge(fu, n + 1)
                        dve.tensor_tensor(acts[:, n % BUFS, :], acts[:, n % BUFS, :], ps[:, 6 + c % 2, :], ALU.mult).then_inc(sd, 1)

                    norm_rows(dve, x, xn)
                    fuse_step(0)
                    dve.wait_ge(ex, 1)
                    dve.tensor_scalar(r_b[:, :, :], r_a[:, :, :], 1.0, None, ALU.add).then_inc(ch, 1)
                    dve.wait_ge(ch, 1)
                    dve.reciprocal(r_a[:, :, :], r_b[:, :, :]).then_inc(ch, 1)
                    dve.wait_ge(ch, 2)
                    dve.tensor_tensor(r_b[:, :, :], r_a[:, :, :],
                                      W["n_bias"][:, :].unsqueeze(1).broadcast_to([P, TT, E1]), ALU.add).then_inc(ch, 1)
                    fuse_step(1)
                    dve.wait_ge(ch, 3)
                    for step in range(1, 5):
                        compare(dve, step, 3, r_b[:, :, :], E1)
                        fuse_step(step + 1)
                    chosen(dve, 7, r_b[:, :, :], E1, K1)
                    fuse_step(6)
                    dve.tensor_tensor(r_b[:, :, :], r_a[:, :, :], r_c[:, :, :], ALU.mult).then_inc(ch, 1)
                    dve.wait_ge(ch, 10)
                    dve.tensor_reduce(r_s[:, :], r_b[:, :, :], AX.X, ALU.add).then_inc(ch, 1)
                    dve.wait_ge(ch, 11)
                    dve.reciprocal(r_r[:, :], r_s[:, :]).then_inc(ch, 1)
                    dve.wait_ge(ch, 12)
                    dve.scalar_tensor_tensor(out=r_w[:, :, :], in0=r_b[:, :, :], scalar=ROUTE_SCALE,
                                             in1=r_r[:, :].unsqueeze(2).broadcast_to([P, TT, E1]),
                                             op0=ALU.mult, op1=ALU.mult).then_inc(ch, 1)
                    dve.wait_ge(ch, 13)
                    dve.tensor_copy(w_parts[:, :, 0, :], r_w[:, :, :]).then_inc(ch, 1)
                    dve.wait_ge(ch, 14)
                    dve.tensor_tensor(r_b[:, :, :], r_w[:, :, :], w_parts[:, :, 0, :], ALU.subtract).then_inc(ch, 1)
                    dve.wait_ge(ch, 15)
                    dve.tensor_copy(w_parts[:, :, 1, :], r_b[:, :, :]).then_inc(ch, 1)
                    dve.wait_ge(ch, 16)
                    dve.tensor_tensor(w_parts[:, :, 2, :], r_b[:, :, :], w_parts[:, :, 1, :], ALU.subtract).then_inc(ch, 1)
                    for n in range(7, LAG - 1):
                        fuse_step(n)
                    for n in range(LAG - 1, steps + LAG + 1):
                        if n < steps:
                            fuse_step(n)
                        if n - LAG + 1 < steps and not shared(n - LAG + 1):
                            scale_step(n - LAG + 1)
                        if store_to is None and n - LAG == pairs + 1:
                            dve.wait_ge(sem("ex_sum"), 1)
                            norm_statistics(dve, x, 0, 2)
                        if store_to is None and n - LAG == pairs + 3:
                            norm_scale(dve, x, xn, 0, 2)
                        if n - LAG in (pairs, steps):
                            blk = (n - LAG) // pairs - 1
                            dve.wait_ge(dn, pairs * (blk + 1))
                            dve.tensor_tensor(x[:, 4 * blk:4 * blk + 4, :], x[:, 4 * blk:4 * blk + 4, :],
                                              tiles_of(4 + blk, n=4), ALU.add).then_inc(sem("ex_sum"), 1)
            end_stage(*LN_SIGNALS, "rt_logits", "rt_chain", "rt_exp", "rt_turned", "rt_zeroed", "rt_kept", "ex_gate",
                      "ex_up", "ex_silu", "ex_fused", "ex_down", "ex_spread", "ex_scaled", "ex_sum", "x_out")

        lin_k = big[:, 0:LIN_K * S].rearrange("p (k t d) -> p k t d", k=LIN_K, d=D)
        lin_v = big[:, 2048:2048 + LIN_K * S].rearrange("p (k t d) -> p k t d", k=LIN_K, d=D)
        lin_w = big[:, 4096:4096 + 5 * P].rearrange("p (k d) -> p k d", k=5)
        state = big[:, 4736:4736 + 2 * P].rearrange("p (k d) -> p k d", k=2)

        def linear_attention():
            wi, mm, ev, st, sv, om = (sem(n) for n in ("la_weights", "la_products", "la_evacuated", "la_states", "la_state", "la_out"))
            with nc.Block() as block:
                @block.gpsimd
                def _(pool):
                    norm_power(pool, (1,))
                    ws = [W["l_qw"][:, :]] + [W[w][:, k * D:(k + 1) * D] for w in ("l_kw", "l_vw") for k in range(LIN_K)]
                    for n, w in enumerate(ws):
                        pool.tensor_tensor(lin_w[:, n, :], w, ident[:, :], ALU.add).then_inc(wi, 1)

                @block.tensor
                def _(pe):
                    norm_transpose(pe, xn, -H)
                    pe.wait_ge(wi, 5)
                    for k in range(2):
                        pe.wait_ge(sem("ln_evacuated"), k + 1)
                        pe.matmul(ps[:, k, :], lin_w[:, 0, :], xT[:, k * HALF:(k + 1) * HALF], start=True, stop=True).then_inc(mm, 1)
                    for n in range(2 * LIN_K):
                        if n >= 3:
                            pe.wait_ge(ev, 2)
                        for t in range(TT):
                            last = pe.matmul(tiles_of(2 + 2 * (n % 3))[:, t, :], xT[:, t * P:(t + 1) * P],
                                             lin_w[:, 1 + n, :], start=True, stop=True)
                        last.then_inc(mm, 1)
                    pe.wait_ge(ev, 1 + 2 * LIN_K)
                    for k in range(LIN_K):
                        for t in range(TT):
                            last = pe.matmul(ps[:, k, 0:P], lin_k[:, k, t, :], lin_v[:, k, t, :],
                                             start=(t == 0), stop=(t == TT - 1))
                        last.then_inc(st, 1)
                    pe.wait_ge(sv, 3)
                    for t in range(TT):
                        last = pe.matmul(tiles_of(2)[:, t, :], qT[:, 0, t * P:(t + 1) * P], state[:, 0, :], start=True, stop=True)
                    last.then_inc(mm, 1)

                @block.scalar
                def _(act):
                    norm_evacuate(act)

                @block.vector
                def _(dve):
                    norm_rows(dve, x, xn, (1,))
                    dve.wait_ge(mm, 2)
                    dve.tensor_scalar(qT[:, 0, :].rearrange("p (k c) -> p k c", k=2), ps[:, 0:2, :], W["l_qb"][:, 0:1], None,
                                      ALU.add).then_inc(ev, 1)
                    for n in range(2 * LIN_K):
                        dst, b = ((lin_k, "l_kb"), (lin_v, "l_vb"))[n // LIN_K]
                        k = n % LIN_K
                        dve.wait_ge(mm, 3 + n)
                        dve.tensor_tensor(dst[:, k, :, :], tiles_of(2 + 2 * (n % 3)),
                                          W[b][:, k * D:(k + 1) * D].unsqueeze(1).broadcast_to([P, TT, D]), ALU.add).then_inc(ev, 1)
                    dve.wait_ge(st, 1)
                    dve.scalar_tensor_tensor(out=state[:, 0, :], in0=ps[:, 0, 0:P], scalar=1.0 / (LIN_N * LIN_N),
                                             in1=block_mask[:, :], op0=ALU.mult, op1=ALU.mult).then_inc(sv, 1)
                    dve.wait_ge(st, 2)
                    dve.tensor_copy(state[:, 1, :], ps[:, 1, 0:P]).then_inc(sv, 1)
                    dve.wait_ge(sv, 2)
                    dve.tensor_tensor(state[:, 0, :], state[:, 0, :], state[:, 1, :], ALU.mult).then_inc(sv, 1)
                    dve.wait_ge(mm, 3 + 2 * LIN_K)
                    dve.tensor_copy(o_rows[:, :, 0:D], tiles_of(2)).then_inc(om, 1)
            end_stage(*LN_SIGNALS, "la_weights", "la_products", "la_evacuated", "la_states", "la_state", "la_out")

        N_CONST = 9
        with nc.Block() as block:
            @block.sync
            def _(sp):
                const = {"ident": ident, "head_mask": head_mask, "pair_mask": pair_mask, "block_mask": block_mask,
                         "tri": tri, "eye8": eye8, "expert_rows": expert_rows}
                for n, t in const.items():
                    dims = (slice(None),) * len(t.shape)
                    sp.dma_start(t[dims], A[n]).then_inc(sem("weights_in"), 16)
                sp.dma_start(cos_t, A["cos"]).then_inc(sem("weights_in"), 16)
                sp.dma_start(sin_t, A["sin"]).then_inc(sem("weights_in"), 16)
                for n in resident:
                    dims = (slice(None),) * len(W[n].shape)
                    sp.dma_start(W[n][dims], A[n]).then_inc(sem("weights_in"), 16)
                sp.wait_ge(sem("weights_in"), 16 * (N_CONST + len(resident)))

            @block.gpsimd
            def _(pool):
                pool.memset(half_neg[:, :], -0.5).then_inc(sem("half_set"), 1)

            @block.vector
            def _(dve):
                dve.wait_ge(sem("weights_in"), 16 * (N_CONST + len(resident)))
                dve.tensor_copy(ident_bf[:, :], ident[:, :]).then_inc(sem("half_set"), 1)
                dve.tensor_copy(expert_of_row[:, :].rearrange("p (e f) -> p e f", f=F1),
                                expert_rows[:, :].unsqueeze(2).broadcast_to([P, E1, F1])).then_inc(sem("half_set"), 1)
        end_stage("weights_in", "half_set")

        null_keys()

        first_turn = turn_of[0]
        with nc.Fori(0, B) as b:
            lif_projections(x_in[b])
            lif_heads()
            heads_out(W["a_ow"][:, :], W["a_ob"])
            experts_first()
            wide_heads()
            wide_out()
            experts_first()
            rope_projections()
            rotary_heads()
            heads_out(W["c_ow"][:, :], W["c_ob"])
            experts_second()
            linear_attention()
            normed_rows_out(o_rows[:, :, 0:D], W["l_g"][:, 0:1], W["l_b"][:, 0:1], W["l_ow"][:, :], W["l_ob"])
            experts_second(store_to=x_out[b])
            if turn_of[0] != first_turn:
                nc.all_engine_barrier()
                turn_of[0] = first_turn




def _constants(np):
    inv_freq = (np.float32(1.0) / np.float32(10000.0) ** (np.arange(0, DH, 2, dtype=np.float32) / np.float32(DH))).astype(np.float32)
    freqs = np.arange(S, dtype=np.float32)[:, None] * inv_freq[None, :]
    cos = np.repeat(np.cos(freqs), 2, axis=-1).T.astype(np.float32)
    sin = np.repeat(np.sin(freqs), 2, axis=-1).T.astype(np.float32)
    sign = np.where(np.arange(DH) < DH // 2, -1.0, 1.0).astype(np.float32)[:, None]
    rows = np.arange(P)
    return {
        "ident": np.eye(P, dtype=np.float32),
        "eye8": np.broadcast_to(np.eye(TT, dtype=np.float32), (P, TT, TT)).copy(),
        "head_mask": (rows[:, None] // DH == np.arange(NH)[None, :]).astype(np.float32),
        "pair_mask": (rows[:, None] // WH == np.arange(2)[None, :]).astype(np.float32),
        "expert_rows": ((rows[:, None] % E1 == np.arange(E1)[None, :]) & (rows[:, None] < 3 * E1)).astype(np.float32),
        "block_mask": (rows[:, None] // DH == rows[None, :] // DH).astype(np.float32),
        "cos": np.tile(cos, (NH, 1)),
        "sin": np.tile(sin * sign, (NH, 1)),
        "tri": np.broadcast_to(np.tril(np.ones((E1, E1), np.float32), -1), (P, E1, E1)).copy(),
    }


def _layout(np, i):
    col = lambda v: v.reshape(P, 1)
    rows = lambda v: np.broadcast_to(v.reshape(1, -1), (P, v.size))
    d = np.arange(D)
    rot = (d // DH) * DH + (d % DH + DH // 2) % DH
    a = {"x": i["L0_attn_a_x"]}
    for k in "qkvo":
        a[f"a_{k}w"] = i[f"L0_attn_a_{k}_w"]
    a["a_qb"], a["a_kb"] = col(i["L0_attn_a_q_b"]), col(i["L0_attn_a_k_b"])
    a["a_vb"], a["a_ob"] = rows(i["L0_attn_a_v_b"]), rows(i["L0_attn_a_o_b"])
    a["m_router"] = i["L0_ffn_router_kernel_DE"]
    a["m_gate"] = i["L0_ffn_kernel_gating_EDF"].transpose(1, 0, 2).reshape(D, E0 * F0)
    a["m_up"] = i["L0_ffn_kernel_up_EDF"].transpose(1, 0, 2).reshape(D, E0 * F0)
    a["m_down"] = i["L0_ffn_kernel_down_EFD"].reshape(E0 * F0 // P, P, D).transpose(1, 0, 2)
    a["b_gamma"] = col(i["L0_attn_b_gamma"])
    a["b_qwT"] = i["L0_attn_b_w_q"].T.reshape(NH // 2, P, D).transpose(1, 0, 2)
    wkv = i["L0_attn_b_w_kv"]
    a["b_pw"] = np.stack([w.reshape(D, NH // 2, P) for w in (i["L0_attn_b_w_q"], wkv[:, :NH * WH], wkv[:, NH * WH:])], 2)
    a["b_ow"] = i["L0_attn_b_w_out"].reshape(NH // 2, P, D).transpose(1, 0, 2)
    a["b_nk"] = i["L0_attn_b_null_kv"][0].reshape(NH // 2, P).T
    a["b_nv"] = rows(i["L0_attn_b_null_kv"][1].reshape(-1))
    for k in "qkvo":
        a[f"c_{k}w"] = i[f"L1_attn_a_w{k}"].T
    a["c_qrw"], a["c_krw"] = i["L1_attn_a_wq"].T[:, rot], i["L1_attn_a_wk"].T[:, rot]
    a["c_qb"], a["c_kb"] = col(i["L1_attn_a_bq"]), col(i["L1_attn_a_bk"])
    a["c_qrb"], a["c_krb"] = col(i["L1_attn_a_bq"][rot]), col(i["L1_attn_a_bk"][rot])
    a["c_vb"], a["c_ob"] = rows(i["L1_attn_a_bv"]), rows(i["L1_attn_a_bo"])
    a["l_qw"], a["l_ow"] = i["L1_attn_b_Wq"], i["L1_attn_b_Wo"]
    a["l_kw"] = i["L1_attn_b_Wk"].transpose(1, 0, 2).reshape(D, LIN_K * D)
    a["l_vw"] = i["L1_attn_b_Wv"].transpose(1, 0, 2).reshape(D, LIN_K * D)
    a["l_qb"] = col(i["L1_attn_b_bq"])
    a["l_kb"], a["l_vb"], a["l_ob"] = rows(i["L1_attn_b_bk"]), rows(i["L1_attn_b_bv"]), rows(i["L1_attn_b_bo"])
    a["l_g"], a["l_b"] = col(i["L1_attn_b_ln_g"]), col(i["L1_attn_b_ln_b"])
    a["n_router"], a["n_bias"] = i["L1_ffn_gate_w"].T, rows(i["L1_ffn_gate_b"])
    w13 = i["L1_ffn_w13"].transpose(2, 0, 1)
    a["n_gate"], a["n_up"] = w13[:, :, :F1].reshape(D, E1 * F1), w13[:, :, F1:].reshape(D, E1 * F1)
    a["n_down"] = i["L1_ffn_w2"].transpose(0, 2, 1).reshape(E1 // 2, P, D).transpose(1, 0, 2)
    a["n_sgate"], a["n_sup"] = i["L1_ffn_w13_s"].T[:, :F1], i["L1_ffn_w13_s"].T[:, F1:]
    a["n_sdown"] = i["L1_ffn_w2_s"].T
    return a


def kernel(**inputs):
    import numpy as np
    import concourse.bacc as bacc
    from concourse.bass_utils import run_bass_kernel_spmd

    nc = bacc.Bacc("TRN2", target_bir_lowering=False, num_devices=1)
    given = {n: np.asarray(v) for n, v in inputs.items()}
    laid = {**_layout(np, given), **_constants(np)}
    arrays = {f"in_{n}": np.ascontiguousarray(v) for n, v in laid.items()}
    aps = {n: nc.dram_tensor(f"in_{n}", arrays[f"in_{n}"].shape, mybir.dt.from_np(arrays[f"in_{n}"].dtype),
                             kind="ExternalInput").ap() for n in laid}
    out = nc.dram_tensor("out", (B, S, D), F32, kind="ExternalOutput").ap()
    hybrid_kernel(nc, aps, out)
    r = run_bass_kernel_spmd(nc, [arrays], core_ids=[0])
    return r.results[0]["out"]
```
